# Optimizing a Trainium2 kernel written in Bass

```python
import numpy as np
import jax
import jax.numpy as jnp

def _softmax(x, axis=-1):
    return jax.nn.softmax(x, axis=axis)

def _gelu(x):
    return jax.nn.gelu(x, approximate=True)

def _silu(x):
    return jax.nn.silu(x)

def _sigmoid(x):
    return jax.nn.sigmoid(x)

def _layernorm(x, axis=-1, eps=1e-05):
    m = jnp.mean(x, axis=axis, keepdims=True)
    v = jnp.var(x, axis=axis, keepdims=True)
    return (x - m) / jnp.sqrt(v + eps)

def _scatter_add(tgt, idx, src, axis=0):
    return tgt.at[idx].add(src)

def _segment_sum(src, seg, n):
    return jax.ops.segment_sum(src, seg, n)
kernel_name = 'mk_perceiver_d1_seqx_r4_3db8dd'

def setup_inputs(seed: int=0):
    np.random.seed(seed)
    _w = jnp.asarray

    def _rec_inputs():
        import jax
        import jax.numpy as jnp
        _rk = jax.random.key(seed)
        x = -0.0002928 + 1 * jax.random.normal(jax.random.fold_in(_rk, 1), (4, 256, 256), jnp.float32)
        _lenS = 256 - jax.random.randint(jax.random.fold_in(_rk, 7), (4,), 0, max(1, 256 // 4) + 1, jnp.int32)
        _lenS2 = 4096 - jax.random.randint(jax.random.fold_in(_rk, 8), (4,), 0, max(1, 4096 // 4) + 1, jnp.int32)
        _ctx_1024P = jax.random.normal(jax.random.fold_in(_rk, 11), (4, 16, 256), jnp.float32)
        _ctx_1024c = jax.random.dirichlet(jax.random.fold_in(_rk, 511), 0.3 * jnp.ones((16,), jnp.float32), (4, 4096))
        _ctx_1024t = jnp.einsum('bsk,bkd->bsd', _ctx_1024c, _ctx_1024P)
        _ctx_1024t = _ctx_1024t * jax.lax.rsqrt(jnp.mean(jnp.square(_ctx_1024t)) + 1e-12) * 0.953939
        ctx_1024 = -1.39393e-06 + 0.999914 * (_ctx_1024t + 0.3 * jax.random.normal(jax.random.fold_in(_rk, 611), (4, 4096, 256), jnp.float32))
        _validS = jnp.arange(256)[None, :] < _lenS[:, None]
        _validS2 = jnp.arange(4096)[None, :] < _lenS2[:, None]
        _causal = jnp.tril(jnp.ones((256, 256), dtype=bool))
        mask_1x1xSxS2_ik0 = jnp.where(jnp.broadcast_to(_validS2[0:1, None, None, :], (1, 1, 256, 4096)), 0, 1).astype(jnp.int32)
        return (x, ctx_1024, mask_1x1xSxS2_ik0)
    x, ctx_1024, mask_1x1xSxS2_ik0 = _rec_inputs()

    def _L0_xattn_setup():
        import jax, jax.numpy as jnp
        import numpy as np
        B, L, E, H = (2, 512, 256, 16)
        Dh = E // H
        key = jax.random.key(seed)
        ks = jax.random.split(key, 12)
        s = 0.02
        inp = {'x_q': jax.random.normal(ks[0], (B, L, E), jnp.float32), 'x_k': jax.random.normal(ks[1], (B, L, E), jnp.float32), 'x_v': jax.random.normal(ks[2], (B, L, E), jnp.float32), 'mask': jnp.tril(jnp.ones((L, L), jnp.int32))[None, None], 'Wq': jax.random.normal(ks[3], (E, E), jnp.float32) * s, 'bq': jnp.zeros((E,), jnp.float32), 'Wk': jax.random.normal(ks[4], (E, E), jnp.float32) * s, 'bk': jnp.zeros((E,), jnp.float32), 'Wv': jax.random.normal(ks[5], (E, E), jnp.float32) * s, 'bv': jnp.zeros((E,), jnp.float32), 'Wo': jax.random.normal(ks[6], (E, E), jnp.float32) * s, 'bo': jnp.zeros((E,), jnp.float32)}
        return inp
    _L0_xattn_all = _L0_xattn_setup()
    _L0_xattn_in = {k: v for k, v in _L0_xattn_all.items() if k in ('Wq', 'bq', 'Wk', 'bk', 'Wv', 'bv', 'Wo', 'bo')}
    del _L0_xattn_all

    def _L0_attn_setup():
        import jax, jax.numpy as jnp
        import numpy as np
        NUM_HEADS = 16
        ROPE_BASE = 10000.0

        def _rotate_half(x):
            xr = x.reshape(*x.shape[:-1], -1, 2)
            x1, x2 = (xr[..., 0], xr[..., 1])
            return jnp.stack((-x2, x1), axis=-1).reshape(x.shape)

        def _rope(x):
            hd = x.shape[-1]
            n = x.shape[-2]
            inv_freq = 1.0 / ROPE_BASE ** (jnp.arange(0, hd, 2, dtype=jnp.float32) / hd)
            freqs = jnp.outer(jnp.arange(n, dtype=jnp.float32), inv_freq)
            freqs = jnp.repeat(freqs, 2, axis=-1)
            return x * jnp.cos(freqs) + _rotate_half(x) * jnp.sin(freqs)
        key = jax.random.key(seed)
        k0, k1, k2 = jax.random.split(key, 3)
        B, N, D = (2, 512, 256)
        X = jax.random.normal(k0, (B, N, D), jnp.float32)
        Wqkv = jax.random.normal(k1, (D, 3 * D), jnp.float32) * D ** (-0.5)
        Wout = jax.random.normal(k2, (D, D), jnp.float32) * D ** (-0.5)
        bout = jnp.zeros((D,), jnp.float32)
        return {'X': X, 'Wqkv': Wqkv, 'Wout': Wout, 'bout': bout}
    _L0_attn_all = _L0_attn_setup()
    _L0_attn_in = {k: v for k, v in _L0_attn_all.items() if k in ('Wqkv', 'Wout', 'bout')}
    del _L0_attn_all

    def _L0_ffn_setup():
        import jax, jax.numpy as jnp
        import numpy as np
        D_MODEL = 256
        D_FF = 1024
        NUM_EXPERTS = 8
        key = jax.random.key(seed)
        ks = jax.random.split(key, 8)
        scale_in = 1.0 / np.sqrt(D_MODEL)
        scale_ff = 1.0 / np.sqrt(D_FF)
        x = jax.random.normal(ks[0], (4, 512, D_MODEL), dtype=jnp.float32)
        gate_w = jax.random.uniform(ks[1], (NUM_EXPERTS, D_MODEL), jnp.float32, -scale_in, scale_in)
        gate_b = jax.random.uniform(ks[2], (NUM_EXPERTS,), jnp.float32, -scale_in, scale_in)
        expert_bias = jnp.zeros((NUM_EXPERTS,), dtype=jnp.float32)
        w1 = jax.random.uniform(ks[3], (NUM_EXPERTS, D_MODEL, D_FF), jnp.float32, -scale_in, scale_in)
        b1 = jax.random.uniform(ks[4], (NUM_EXPERTS, D_FF), jnp.float32, -scale_in, scale_in)
        w2 = jax.random.uniform(ks[5], (NUM_EXPERTS, D_FF, D_MODEL), jnp.float32, -scale_ff, scale_ff)
        b2 = jax.random.uniform(ks[6], (NUM_EXPERTS, D_MODEL), jnp.float32, -scale_ff, scale_ff)
        return {'x': x, 'gate_w': gate_w, 'gate_b': gate_b, 'expert_bias': expert_bias, 'w1': w1, 'b1': b1, 'w2': w2, 'b2': b2}
    _L0_ffn_all = _L0_ffn_setup()
    _L0_ffn_in = {k: v for k, v in _L0_ffn_all.items() if k in ('gate_w', 'gate_b', 'expert_bias', 'w1', 'b1', 'w2', 'b2')}
    del _L0_ffn_all
    return {'x': x, 'ctx_1024': ctx_1024, 'mask_1x1xSxS2_ik0': mask_1x1xSxS2_ik0, 'L0_xattn_Wq': _L0_xattn_in['Wq'], 'L0_xattn_bq': _L0_xattn_in['bq'], 'L0_xattn_Wk': _L0_xattn_in['Wk'], 'L0_xattn_bk': _L0_xattn_in['bk'], 'L0_xattn_Wv': _L0_xattn_in['Wv'], 'L0_xattn_bv': _L0_xattn_in['bv'], 'L0_xattn_Wo': _L0_xattn_in['Wo'], 'L0_xattn_bo': _L0_xattn_in['bo'], 'L0_attn_Wqkv': _L0_attn_in['Wqkv'], 'L0_attn_Wout': _L0_attn_in['Wout'], 'L0_attn_bout': _L0_attn_in['bout'], 'L0_ffn_gate_w': _L0_ffn_in['gate_w'], 'L0_ffn_gate_b': _L0_ffn_in['gate_b'], 'L0_ffn_expert_bias': _L0_ffn_in['expert_bias'], 'L0_ffn_w1': _L0_ffn_in['w1'], 'L0_ffn_b1': _L0_ffn_in['b1'], 'L0_ffn_w2': _L0_ffn_in['w2'], 'L0_ffn_b2': _L0_ffn_in['b2']}

def reference(x, ctx_1024, mask_1x1xSxS2_ik0, L0_xattn_Wq, L0_xattn_bq, L0_xattn_Wk, L0_xattn_bk, L0_xattn_Wv, L0_xattn_bv, L0_xattn_Wo, L0_xattn_bo, L0_attn_Wqkv, L0_attn_Wout, L0_attn_bout, L0_ffn_gate_w, L0_ffn_gate_b, L0_ffn_expert_bias, L0_ffn_w1, L0_ffn_b1, L0_ffn_w2, L0_ffn_b2):
    import jax
    import jax.numpy as jnp

    def _L0_xattn_ref(x_q, x_k, x_v, mask, Wq, bq, Wk, bk, Wv, bv, Wo, bo):
        import jax, jax.numpy as jnp
        import numpy as np
        B, L, E, H = (2, 512, 256, 16)
        Dh = E // H
        N, Lq, _ = x_q.shape
        Lk = x_k.shape[1]
        q = (x_q @ Wq.T + bq).reshape(N, Lq, H, Dh).transpose(0, 2, 1, 3)
        k = (x_k @ Wk.T + bk).reshape(N, Lk, H, Dh).transpose(0, 2, 1, 3)
        v = (x_v @ Wv.T + bv).reshape(N, Lk, H, Dh).transpose(0, 2, 1, 3)
        scores = jnp.einsum('bhqd,bhkd->bhqk', q, k) / jnp.sqrt(jnp.float32(Dh))
        scores = jnp.where(mask == 0, jnp.float32(-1000000000.0), scores)
        attn = jax.nn.softmax(scores, axis=-1)
        out = jnp.einsum('bhqk,bhkd->bhqd', attn, v)
        out = out.transpose(0, 2, 1, 3).reshape(N, Lq, E)
        return out @ Wo.T + bo

    def _L0_attn_ref(X, Wqkv, Wout, bout):
        import jax, jax.numpy as jnp
        import numpy as np
        NUM_HEADS = 16
        ROPE_BASE = 10000.0

        def _rotate_half(x):
            xr = x.reshape(*x.shape[:-1], -1, 2)
            x1, x2 = (xr[..., 0], xr[..., 1])
            return jnp.stack((-x2, x1), axis=-1).reshape(x.shape)

        def _rope(x):
            hd = x.shape[-1]
            n = x.shape[-2]
            inv_freq = 1.0 / ROPE_BASE ** (jnp.arange(0, hd, 2, dtype=jnp.float32) / hd)
            freqs = jnp.outer(jnp.arange(n, dtype=jnp.float32), inv_freq)
            freqs = jnp.repeat(freqs, 2, axis=-1)
            return x * jnp.cos(freqs) + _rotate_half(x) * jnp.sin(freqs)
        B, N, D = X.shape
        H = NUM_HEADS
        hd = D // H
        scale = hd ** (-0.5)
        qkv = X @ Wqkv
        q, k, v = jnp.split(qkv, 3, axis=-1)

        def to_heads(t):
            return t.reshape(B, N, H, hd).transpose(0, 2, 1, 3)
        Q, K, V = (to_heads(q), to_heads(k), to_heads(v))
        Q = _rope(Q)
        K = _rope(K)
        scores = jnp.einsum('bhnd,bhmd->bhnm', Q, K) * scale
        causal = jnp.tril(jnp.ones((N, N), dtype=bool))
        scores = jnp.where(causal, scores, -jnp.inf)
        attn = jax.nn.softmax(scores, axis=-1)
        out = jnp.einsum('bhnm,bhmd->bhnd', attn, V)
        out = out.transpose(0, 2, 1, 3).reshape(B, N, D)
        return out @ Wout + bout

    def _L0_ffn_ref(x, gate_w, gate_b, expert_bias, w1, b1, w2, b2):
        import jax, jax.numpy as jnp
        import numpy as np
        D_MODEL = 256
        D_FF = 1024
        NUM_EXPERTS = 8
        gate_logits = jnp.einsum('bsd,ed->bse', x, gate_w) + gate_b + expert_bias
        top_idx = jnp.argmax(gate_logits, axis=-1)
        out = jnp.zeros_like(x)
        for e in range(NUM_EXPERTS):
            mask = (top_idx == e)[..., None].astype(x.dtype)
            h = jax.nn.relu(jnp.einsum('bsd,df->bsf', x, w1[e]) + b1[e])
            y = jnp.einsum('bsf,fd->bsd', h, w2[e]) + b2[e]
            out = out + mask * y
        return out
    x = x + _L0_xattn_ref(_layernorm(x, axis=-1), ctx_1024, ctx_1024, mask_1x1xSxS2_ik0, L0_xattn_Wq, L0_xattn_bq, L0_xattn_Wk, L0_xattn_bk, L0_xattn_Wv, L0_xattn_bv, L0_xattn_Wo, L0_xattn_bo)
    x = x + _L0_attn_ref(_layernorm(x, axis=-1), L0_attn_Wqkv, L0_attn_Wout, L0_attn_bout)
    x = x + _L0_ffn_ref(_layernorm(x, axis=-1), L0_ffn_gate_w, L0_ffn_gate_b, L0_ffn_expert_bias, L0_ffn_w1, L0_ffn_b1, L0_ffn_w2, L0_ffn_b2)
    return x

_drawn_inputs = setup_inputs


def setup_inputs(seed=0):
    import zlib

    import numpy as np

    out = dict(_drawn_inputs(seed))
    spreads = {'L0_xattn_bq': (0.0, 0.8),
     'L0_xattn_bk': (0.0, 0.8),
     'L0_xattn_bv': (0.0, 0.1),
     'L0_xattn_bo': (0.0, 0.1),
     'L0_attn_bout': (0.0, 0.1),
     'L0_ffn_expert_bias': (0.0, 0.1)}
    factors = {'L0_xattn_Wq': 5.897, 'L0_xattn_Wk': 5.806, 'L0_ffn_b1': 4.099, 'L0_ffn_b2': 3.293}
    for name, (base, spread) in spreads.items():
        noise = np.random.default_rng([zlib.crc32(name.encode()), seed]).standard_normal(out[name].shape)
        drawn = base * np.exp(spread * noise) if base else spread * noise
        out[name] = jnp.asarray(drawn.astype(out[name].dtype))
    for name, factor in factors.items():
        out[name] = (out[name] * factor).astype(out[name].dtype)
    return out
```

```python
from contextlib import ExitStack

import numpy as np

import concourse.bass as bass
from concourse import mybir

F32 = mybir.dt.float32
BF16 = mybir.dt.bfloat16
I32 = mybir.dt.int32
ALU = mybir.AluOpType
ACT = mybir.ActivationFunctionType
AX = mybir.AxisListType

P = 128
NB, SQ, E = 4, 256, 256
H, D = 16, 16
LK = 4096
TK = LK // P
CH = 8
NU, HU = 8, 8
NT = NB * SQ // P
KE = E // P
SLOT = 32
BIG = float(2 ** 30)
EPS = 1e-5
NE, F = 8, 1024
SLOTS = NT + NE - 1
PAIR = 2 * D * 3
ROWS = PAIR + 3
STEPS = 2 * CH
TICKETS = 6


class Chain:

    def __init__(self, eng, sem, start=0):
        self.eng, self.sem, self.n = eng, sem, start

    def add(self, ins):
        self.n = self.n + 1
        ins.then_inc(self.sem, 1)
        return self.n

    def wait(self, n=None):
        self.eng.wait_ge(self.sem, self.n if n is None else n)


def tickets_before(s):
    if isinstance(s, int):
        return [0, 2][s] if s < 2 else 7 + 6 * (s - 2) if s <= 8 else 47
    return s * 6 - 5


def build(nc, x, ctx_l, mask_l, w_l, w_qkv_l, wo_pad, biases, rows_in, consts, causal_in, rope_in, gate_l,
          w1, b1_l, w2, b2, out):
    ctx = ExitStack()
    with ctx:
        def sb(name, shape, dt):
            return ctx.enter_context(nc.sbuf_tensor(name, shape, dt))

        def sem(name):
            return ctx.enter_context(nc.semaphore(name))

        arena = sb("arena", [P, 170 * 256], F32)

        def cut(at, shape, dt, names=None, **sizes):
            n = int(np.prod(shape))
            size = n * (2 if dt == BF16 else 4) // 4
            v = arena[:, at * 256:at * 256 + size]
            if dt != F32:
                v = v.bitcast(dt)
            if len(shape) > 1:
                axes = "abcde"[:len(shape)]
                v = v.rearrange("p (%s) -> p %s" % (" ".join(axes), " ".join(axes)),
                                **dict(zip(axes[1:], shape[1:])))
            return v

        k_stack = cut(0, [2, HU, CH * P], BF16)
        q_stack = cut(32, [HU, NU, SQ], BF16)
        v_sb = cut(64, [2, CH, HU, SLOT], F32)
        work = cut(80, [4096], F32)
        o_acc = cut(96, [NU, 2 * SQ], F32)
        probs = cut(112, [2, 4 * SQ], F32)
        ctx_sb = cut(120, [CH, KE, P], F32)
        mask_in = cut(128, [CH, 2 * SQ], I32)
        bias_qk = cut(144, [2, CH * P], BF16)
        bias_kq = cut(148, [CH, SQ], BF16)
        junk = cut(152, [2, 512], BF16)
        masked = cut(152, [512], F32)
        w_sb = cut(154, [3, KE, E], F32)
        w_qkv = cut(160, [KE, 3 * E], F32)
        rope = cut(166, [4, SQ], F32)
        mask_all = cut(0, [TK, SQ], I32)
        mask_nz = cut(96, [TK, SQ], BF16)
        q_full = cut(112, [2048], F32)
        q_rest = cut(64, [2048], F32)
        q_slots = cut(80, [4, 2048], BF16)
        pick = cut(120, [TK, TK], F32)[0:1]
        xn = cut(128, [NT, E], F32)
        xn_t = cut(136, [KE, NT * P], F32)
        k_slots = cut(80, [4, 1024], BF16)
        k_full = cut(88, [1024], F32)
        k_rest = cut(92, [1024], F32)
        sums = cut(112, [2, 2 * SQ], F32)
        r_slots = [cut(80, [4, 1024], BF16), cut(88, [4, 1024], BF16)]
        r_full = [cut(96, [1024], F32), cut(100, [1024], F32)]
        r_rest = [cut(104, [1024], F32), cut(108, [1024], F32)]
        r_swap = [cut(120, [1024], F32), cut(124, [1024], F32)]
        t_sums = cut(120, [2, 2 * SQ], F32)
        w1_sb = [cut(16 * e, [KE, F], F32) for e in range(NE)]
        w2_sb = [cut(16 * e + 8, [F // P, E], F32) for e in range(NE)]
        xs_in = cut(128, [SLOTS, E], F32)
        y_all = xs_in
        xs_t = cut(144, [KE, SLOTS * P], F32)
        b2_bc = cut(160, [NE, E], F32)
        picked = cut(144, [NT, E], F32)

        x_sb = sb("x_sb", [P, NT, E], F32)
        wo_sb = sb("wo_sb", [P, 2, 4, E], F32)
        bias_sb = sb("bias_sb", [P, 8], F32)
        b1_sb = sb("b1_sb", [P, NE, F // P], F32)
        gate_sb = sb("gate_sb", [P, KE, NE], F32)
        rows_bc = sb("rows_bc", [P, 2 * E + 2 * NE], F32)
        cst = sb("cst", [P, 4 * P], F32)
        causal = sb("causal", [P, 2, 2, SQ], BF16)
        ident_b = sb("ident_b", [P, P], BF16)
        ones_b = sb("ones_b", [P, P], BF16)
        lower_b = sb("lower_b", [P, P], BF16)
        zeros = sb("zeros", [P, E], F32)
        ln_stat = sb("ln_stat", [P, NT, 6], F32)
        ln_mv = sb("ln_mv", [P, NT, 2], F32)
        ln_r = sb("ln_r", [P, NT], F32)
        eps_sb = sb("eps_sb", [P, 1], F32)
        tile_any = sb("tile_any", [P, TK], F32)
        tile_any_b = sb("tile_any_b", [P, TK], BF16)
        row_dead = sb("row_dead", [P, SQ], F32)
        q_scale = sb("q_scale", [P, SQ], F32)
        neg_big = sb("neg_big", [P, SQ], F32)
        neg_big_col = sb("neg_big_col", [P, 2], F32)
        cmp = sb("cmp", [1, 256], F32)
        tiles_i = sb("tiles_i", [1, 48], I32)
        m_run = sb("m_run", [P, NU, 16], F32)
        m_tile = sb("m_tile", [P, 1], F32)
        m_old = sb("m_old", [P, 16], F32)
        m_cur = sb("m_cur", [P, 16], F32)
        m_neg = sb("m_neg", [P, 2, 16], F32)
        m_parts = sb("m_parts", [P, 2, 3, HU], BF16)
        m_diff = sb("m_diff", [P, 16], F32)
        m_rows = sb("m_rows", [48, P], BF16)
        f_bc = sb("f_bc", [P, 2, 16, 32], F32)
        hidden = f_bc[:, :, :, :].rearrange("p a n r -> p (a n r)").rearrange("p (c n) -> p c n", c=F // P)
        route = sb("route", [P, 8, NT, NE], F32)
        route_b = sb("route_b", [P, NT, NE], BF16)
        slot_i = sb("slot_i", [P, NT], I32)
        runs_i = sb("runs_i", [1, 2 * NE], I32)

        ident_f = cst[:, 0:P]
        xs_dram = nc.dram_tensor("xs_dram", [SLOTS * P, E], F32).ap()
        ys_dram = nc.dram_tensor("ys_dram", [SLOTS * P, E], F32).ap()

        ps_s = ctx.enter_context(nc.psum_tensor("ps_s", [P, 2, 1024], F32))
        ps_a = ctx.enter_context(nc.psum_tensor("ps_a", [P, 2, 512], F32))
        ps_o = ctx.enter_context(nc.psum_tensor("ps_o", [P, 512], F32))
        ps_m = ctx.enter_context(nc.psum_tensor("ps_m", [P, 512], F32))
        ps_t = ps_s[:, :, :].rearrange("p a n -> p (a n)")

        in_x, in_w, in_c = sem("in_x"), sem("in_w"), sem("in_c")
        in_m = [sem(f"in_m{i}") for i in range(4)]
        dve_own, act_own, pool_own = sem("dve_own"), sem("act_own"), sem("pool_own")
        const_ready = sem("const_ready")
        diff_ready, max_steps = sem("diff_ready"), sem("max_steps")
        ln_var = sem("ln_var")
        ln_std = sem("ln_std")
        xn_ready = sem("xn_ready")
        xt_full, xt_taken = sem("xt_full"), sem("xt_taken")
        q_proj, q_taken = sem("q_proj"), sem("q_taken")
        nz_ready = sem("nz_ready")
        counts_ready = sem("counts_ready")
        any_ready = sem("any_ready")
        neg_ready = sem("neg_ready")
        neg_col_ready = sem("neg_col_ready")
        q_slots_ready = sem("q_slots_ready")
        q_stacked = sem("q_stacked")
        tiles_ready = sem("tiles_ready")
        state_ready = sem("state_ready")
        masks_in = sem("masks_in")
        masks_ready = sem("masks_ready")
        ctx_in = sem("ctx_in")
        misc_full, misc_taken = sem("misc_full"), sem("misc_taken")
        k_act, k_pool = sem("k_act"), sem("k_pool")
        k_low, k_high = sem("k_low"), sem("k_high")
        a_scores, a_max = sem("a_scores"), sem("a_max")
        scores, exps, pvs = sem("scores"), sem("exps"), sem("pvs")
        o_free = sem("o_free")
        max_own = sem("max_own")
        mrow_in = sem("mrow_in")
        f_ready = sem("f_ready")
        sums_out = sem("sums_out")
        normed, att_in, att_full, x1_ready = sem("normed"), sem("att_in"), sem("att_full"), sem("x1_ready")
        out_done = sem("out_done")
        in_late, zero_ready, xs_zeroed = sem("in_late"), sem("zero_ready"), sem("xs_zeroed")
        rot_full, swapped, cos_done = sem("rot_full"), sem("swapped"), sem("cos_done")
        sin_done, rotated, rest_done = sem("sin_done"), sem("rotated"), sem("rest_done")
        parts_act, parts_pool = sem("parts_act"), sem("parts_pool")
        stacked = [sem("stacked0"), sem("stacked1")]
        v_full, v_taken = sem("v_full"), sem("v_taken")
        self_scores, self_max = sem("self_scores"), sem("self_max")
        parts_ready, rows_full, rows_taken, rows_in_place = (
            sem("parts_ready"), sem("rows_full"), sem("rows_taken"), sem("rows_in_place"))
        t_scores, t_exps, t_pvs = sem("t_scores"), sem("t_exps"), sem("t_pvs")
        t_out = sem("t_out")
        self_normed, att2_full, x2_ready = sem("self_normed"), sem("att2_full"), sem("x2_ready")
        gate_full, hot_ready, ranks_full = sem("gate_full"), sem("hot_ready"), sem("ranks_full")
        runs_ready, slots_ready, scattered, xs_loaded = (
            sem("runs_ready"), sem("slots_ready"), sem("scattered"), sem("xs_loaded"))
        xs_full, xs_taken = sem("xs_full"), sem("xs_taken")
        w_in = [sem(f"w_in{e}") for e in range(NE)]
        b2_in = sem("b2_in")
        h_full, h_ready, y_full, y_taken = sem("h_full"), sem("h_ready"), sem("y_full"), sem("y_taken")
        ys_stored, x3_ready = sem("ys_stored"), sem("x3_ready")
        gathered = [sem(f"gathered{t}") for t in range(NT)]

        PV0 = 2 * STEPS

        def chunks_and_stages(eng, stage, start=None):
            if start:
                start(0)
            for s in range(NU + 2):
                stage(0, s, s)
            eng.wait_ge(tiles_ready, 1)
            n = eng.value_load(tiles_i[0:1, TK:TK + 1], min_val=1, max_val=TK // CH)
            with eng.If(n > 1):
                with eng.Fori(1, n) as c:
                    if start:
                        start(c)
                    for s in (0, 1):
                        stage(c, s, s)
                    with eng.Fori(1, NB) as b:
                        for k in (0, 1):
                            stage(c, b * 2 + k, k)
                    for s in (NU, NU + 1):
                        stage(c, s, s)
            return n

        def expert_tiles(eng, step):
            eng.wait_ge(runs_ready, 2)
            for e in range(NE):
                end = eng.value_load(runs_i[0:1, e:e + 1], min_val=1, max_val=SLOTS)
                first = eng.value_load(runs_i[0:1, NE + e:NE + e + 1], min_val=0, max_val=SLOTS - 1)
                with eng.Fori(first, end) as j:
                    step(e, j)

        def parts(s, k):
            if isinstance(s, int):
                return s >= 2, 1 <= s <= 8, s <= 7, s % 2, s // 2
            return True, True, True, k, None

        block = ctx.enter_context(nc.Block())

        @block.sync
        def _(sp):
            for i in range(4):
                if i == 1:
                    sp.dma_start(x_sb[:, :, :], x.rearrange("b (t p) d -> p (b t) d", p=P)).then_inc(in_x, 16)
                    sp.dma_start(cst[:, :], consts).then_inc(in_c, 16)
                if i == 2:
                    sp.dma_start(w_sb[:, :, :, :], w_l).then_inc(in_w, 16)
                    sp.dma_start(bias_sb[:, :], biases).then_inc(in_w, 16)
                    sp.dma_start(rows_bc[:, :], rows_in[0, :].partition_broadcast(P)).then_inc(in_w, 16)
                    sp.dma_start(wo_sb[:, :, :, :], wo_pad).then_inc(in_w, 16)
                sp.dma_start(mask_all[:, CH * i:CH * i + CH, :],
                             mask_l[CH * i:CH * i + CH, :, 0:SQ].rearrange("t p q -> p t q")).then_inc(in_m[i], 16)
            sp.dma_start(w_qkv[:, :, :], w_qkv_l).then_inc(in_late, 16)
            sp.dma_start(rope[:, :, :], rope_in).then_inc(in_late, 16)
            sp.dma_start(causal[:, :, :, :], causal_in).then_inc(in_late, 16)
            sp.dma_start(gate_sb[:, :, :], gate_l).then_inc(in_late, 16)
            sp.dma_start(b1_sb[:, :, :], b1_l).then_inc(in_late, 16)
            sp.wait_ge(zero_ready, 1)
            sp.dma_start(xs_dram.rearrange("(s p) n -> p s n", p=P),
                         zeros[:, :].unsqueeze(1).to_broadcast([P, SLOTS, E])).then_inc(xs_zeroed, 16)
            sp.dma_start(ys_dram.rearrange("(s p) n -> p s n", p=P),
                         zeros[:, :].unsqueeze(1).to_broadcast([P, SLOTS, E])).then_inc(xs_zeroed, 16)
            sp.wait_ge(q_slots_ready, 4)
            for hh in range(HU):
                rows = slice(16 * hh, 16 * hh + 16)
                sp.dma_start(q_stack[0:48, hh, :, :],
                             q_slots[rows, 0:1, :].to_broadcast([16, 3, 2048])).then_inc(q_stacked, 16)
                sp.dma_start(q_stack[48:96, hh, :, :], q_slots[rows, 1:4, :]).then_inc(q_stacked, 16)

            def start(c):
                sp.wait_ge(tiles_ready, 1)
                tiles = [sp.value_load(tiles_i[0:1, bass.ds(c * CH + j, 1)], min_val=0, max_val=TK)
                         for j in range(CH)]
                sp.wait_ge(masks_ready, c * 3)
                for j, t in enumerate(tiles):
                    sp.dma_start(mask_in[:, j, :], mask_l[bass.ds(t, 1), :, :].rearrange("a p q -> p (a q)")
                                 ).then_inc(masks_in, 16)

            def stage(c, s, k):
                b_on, a_on, k_on, par, _ = parts(s, k)
                cs = c * NU + s
                tk = c * (TICKETS * NU) + tickets_before(s)
                if k_on and par == 0:
                    tiles = [sp.value_load(tiles_i[0:1, bass.ds(c * CH + j, 1)], min_val=0, max_val=TK)
                             for j in range(CH)]
                    sp.wait_ge(misc_full, tk + (2 if a_on else 0))
                    for j, t in enumerate(tiles):
                        src = ctx_l[bass.ds(t, 1), :, bass.ds(s * (KE * P // 2), KE * P)]
                        sp.dma_start(ctx_sb[:, j, :, :], src.rearrange("a p n -> p (a n)").rearrange(
                            "p (k n) -> p k n", k=KE)).then_inc(ctx_in, 16)
                if k_on:
                    sp.wait_ge(k_act, cs * 3 + 3)
                    sp.wait_ge(k_pool, cs * 2 + 2)

                def stack(hh, done):
                    rows = slice(16 * hh, 16 * hh + 16)
                    sp.dma_start(k_stack[0:48, par, hh, :], k_slots[rows, 0:3, :]).then_inc(done, 16)
                    sp.dma_start(k_stack[48:96, par, hh, :], k_slots[rows, 1:4, :]).then_inc(done, 16)

                if k_on:
                    sp.wait_ge(pvs, cs * STEPS + CH)
                    for hh in range(4):
                        stack(hh, k_low)
                if a_on:
                    n = tk + (2 if a_on else 0) + (2 if k_on else 0) + 1
                    sp.wait_ge(misc_taken, n + 1)
                    u_at = (s - 1) % 2 * 4 + (s - 1) // 2 if isinstance(s, int) else None
                    if u_at is None:
                        u_at = s // 2 + (NB - 1) if k == 0 else (s - 1) // 2
                    for qt in range(2):
                        sp.dma_start(q_stack[PAIR:ROWS, :, bass.ds(u_at, 1), P * qt:P * qt + P].rearrange(
                            "p h u q -> p h (u q)"), m_rows[24 * qt:24 * qt + 24, :]).then_inc(mrow_in, 16)
                if k_on:
                    sp.wait_ge(pvs, cs * STEPS + STEPS)
                    for hh in range(4, HU):
                        stack(hh, k_high)

            sp.wait_ge(state_ready, 1)
            chunks_and_stages(sp, stage, start)
            for i in range(4):
                half, t = i // 2, i % 2
                sp.wait_ge(parts_act, 3 * i + 3)
                sp.wait_ge(parts_pool, i + 1)
                if i == 0:
                    sp.wait_ge(normed, NU)
                for hh in range(HU):
                    rows = slice(16 * hh, 16 * hh + 16)
                    if t == 0:
                        dst = q_stack[:, hh, NB * half:NB * half + NB, :].rearrange("p u q -> p (u q)")
                        sp.dma_start(dst[0:48], r_slots[0][rows, 0:1, :].to_broadcast([16, 3, 1024])
                                     ).then_inc(stacked[half], 16)
                        sp.dma_start(dst[48:96], r_slots[0][rows, 1:4, :]).then_inc(stacked[half], 16)
                    else:
                        dst = k_stack[:, half, hh, :]
                        sp.dma_start(dst[0:48], r_slots[1][rows, 0:3, :]).then_inc(stacked[half], 16)
                        sp.dma_start(dst[48:96], r_slots[1][rows, 1:4, :]).then_inc(stacked[half], 16)
            for u in range(NU):
                sp.wait_ge(rows_taken, u + 1)
                for qt in range(2):
                    sp.dma_start(q_stack[PAIR:ROWS, :, u, P * qt:P * qt + P], m_rows[24 * qt:24 * qt + 24, :]
                                 ).then_inc(rows_in_place, 16)
            sp.wait_ge(self_normed, NU)
            sp.wait_ge(xs_zeroed, 32)
            for e in (0, 1, 2, 3, 4, 5, 7, 6):
                if e == 6:
                    sp.wait_ge(x2_ready, NB)
                sp.dma_start(w1_sb[e], w1[e].rearrange("(k p) f -> p k f", p=P)).then_inc(w_in[e], 16)
                sp.dma_start(w2_sb[e], w2[e].rearrange("(c p) n -> p c n", p=P)).then_inc(w_in[e], 16)
            sp.dma_start(b2_bc.rearrange("p e n -> p (e n)"), b2.rearrange("e n -> (e n)").partition_broadcast(P)
                         ).then_inc(b2_in, 16)
            sp.wait_ge(scattered, 16 * NT)
            sp.dma_start(xs_in, xs_dram.rearrange("(s p) n -> p s n", p=P)).then_inc(xs_loaded, 16)

            def store(e, j):
                sp.wait_ge(y_taken, j + 2)
                sp.dma_start(ys_dram[bass.ds(j * P, P), :], y_all[:, bass.ds(j, 1), :].rearrange("p a n -> p (a n)")
                             ).then_inc(ys_stored, 16)

            expert_tiles(sp, store)
            for t in range(NT):
                sp.wait_ge(x3_ready, t + 1)
                sp.dma_start(out.rearrange("b (t p) d -> (b t) p d", p=P)[t], x_sb[:, t, :]).then_inc(out_done, 16)
            sp.wait_ge(out_done, 16 * NT)

        @block.vector
        def _(dve):
            own = Chain(dve, dve_own)
            own.add(dve.memset(eps_sb[:, :], EPS))
            own.add(dve.memset(ones_b[:, :], 1.0))
            dve.memset(zeros[:, :], 0.0).then_inc(zero_ready, 1)
            own.wait()
            dve.wait_ge(in_c, 16)
            own.add(dve.tensor_copy(lower_b[:, :], cst[:, 2 * P:3 * P]))
            own.wait()
            dve.tensor_copy(ident_b[:, :], ident_f).then_inc(const_ready, 1)

            def layernorm(src, dst):
                own.wait()
                for t in range(NT):
                    own.add(dve.bn_stats(ln_stat[:, t, :], src[:, t, :]))
                own.wait()
                for t in range(NT):
                    ins = dve.bn_aggr(ln_mv[:, t, :], ln_stat[:, t, :])
                    own.add(ins)
                own.wait()
                own.add(dve.tensor_copy(ln_r[:, :], ln_mv[:, :, 1]))
                own.wait()
                dve.tensor_scalar(ln_r[:, :], ln_r[:, :], 1.0, None, ALU.mult).then_inc(ln_var, 1)

            def layernorm_end(src, dst, n):
                dve.wait_ge(ln_std, n)
                own.add(dve.reciprocal(ln_r[:, :], ln_r[:, :]))
                own.wait()
                for t in range(NT):
                    dve.tensor_scalar(dst[:, t, :], src[:, t, :], ln_mv[:, t, 0:1], ln_r[:, t:t + 1],
                                      ALU.subtract, ALU.mult).then_inc(xn_ready, 1)

            dve.wait_ge(in_x, 16)
            layernorm(x_sb, xn)
            layernorm_end(x_sb, xn, 1)
            for t in range(TK):
                if t % CH == 0:
                    dve.wait_ge(in_m[t // CH], 16)
                dve.tensor_scalar(mask_nz[:, t, :], mask_all[:, t, :], 0.0, 0.0, ALU.not_equal, ALU.max,
                                  accum_out=tile_any[:, t:t + 1]).then_inc(nz_ready, 1)
            dve.wait_ge(nz_ready, TK)
            dve.tensor_copy(tile_any_b[:, :], tile_any[:, :]).then_inc(any_ready, 1)
            dve.wait_ge(counts_ready, 1)
            own.add(dve.tensor_scalar(row_dead[:, :], ps_m[:, 0:SQ], 0.0, None, ALU.is_equal))
            own.add(dve.tensor_scalar(q_scale[:, :], ps_m[:, 0:SQ], 0.0, D ** -0.5, ALU.is_gt, ALU.mult))
            dve.tensor_scalar(neg_big[:, :], ps_m[:, 0:SQ], 0.0, -BIG, ALU.is_gt, ALU.mult).then_inc(neg_ready, 1)
            own.wait()
            dve.wait_ge(q_taken, 4)
            n = own.add(dve.tensor_tensor(
                q_full.rearrange("p (u q) -> p u q", u=NU), q_full.rearrange("p (u q) -> p u q", u=NU),
                q_scale[:, :].unsqueeze(1).to_broadcast([P, NU, SQ]), ALU.mult))
            own.wait()
            dve.tensor_copy(q_slots[:, 0, :], q_full).then_inc(q_slots_ready, 1)
            dve.wait_ge(q_slots_ready, 1)
            own.add(dve.tensor_tensor(q_rest, q_full, q_slots[:, 0, :], ALU.subtract))
            own.wait()
            dve.tensor_copy(q_slots[:, 1, :], q_rest).then_inc(q_slots_ready, 1)
            dve.tensor_copy(q_slots[:, 2, :], q_rest).then_inc(q_slots_ready, 1)
            dve.wait_ge(q_slots_ready, 3)
            dve.tensor_tensor(q_slots[:, 3, :], q_rest, q_slots[:, 1, :], ALU.subtract).then_inc(q_slots_ready, 1)
            own.add(dve.tensor_reduce(cmp[:, 0:1], row_dead[0:1, :], AX.X, ALU.max))
            own.wait()
            own.add(dve.tensor_scalar(cmp[:, 32:64], ps_m[0:1, SQ:SQ + TK], 0.0, cmp[:, 0:1], ALU.is_gt, ALU.max))
            own.wait()
            own.add(dve.memset(cmp[:, 64:96], 1.0))
            own.wait()
            own.add(dve.tensor_tensor_scan(cmp[:, 96:128], cmp[:, 64:96], cmp[:, 32:64], 0.0, ALU.mult, ALU.add))
            own.wait()
            own.add(dve.tensor_tensor(cmp[:, 128:160], cmp[:, 96:128], cmp[:, 32:64], ALU.mult))
            own.wait()
            own.add(dve.tensor_scalar(cmp[:, 128:160], cmp[:, 128:160], -1.0, None, ALU.add))
            own.wait()
            row = lambda a: a.unsqueeze(1).to_broadcast([1, TK, TK])
            col = lambda a: a.unsqueeze(2).to_broadcast([1, TK, TK])
            own.add(dve.tensor_tensor(pick[:, :, :], row(cmp[:, 128:160]), col(cst[0:1, P:P + TK]), ALU.is_equal))
            own.wait()
            own.add(dve.tensor_tensor(pick[:, :, :], pick[:, :, :], row(cst[0:1, P:P + TK]), ALU.mult))
            own.wait()
            own.add(dve.tensor_reduce(cmp[:, 160:192], pick[:, :, :], AX.X, ALU.add))
            own.add(dve.tensor_scalar(cmp[:, 192:224], cst[0:1, P:P + TK], cmp[:, 127:128], float(TK),
                                      ALU.is_ge, ALU.mult))
            own.wait()
            own.add(dve.tensor_tensor(tiles_i[:, 0:TK], cmp[:, 160:192], cmp[:, 192:224], ALU.add))
            own.add(dve.tensor_scalar(cmp[:, 224:224 + TK // CH], cst[0:1, P:P + TK:CH], cmp[:, 127:128], None,
                                      ALU.is_lt))
            own.wait()
            own.add(dve.tensor_reduce(cmp[:, 1:2], cmp[:, 224:224 + TK // CH], AX.X, ALU.add))
            own.wait()
            dve.tensor_copy(tiles_i[:, TK:TK + 1], cmp[:, 1:2]).then_inc(tiles_ready, 1)
            dve.wait_ge(counts_ready, 1)
            own.add(dve.memset(m_run[:, :, :], -2 * BIG))
            own.add(dve.memset(k_stack[96:99], 1.0))
            own.add(dve.memset(v_sb[:, :, :, :, D:SLOT], 1.0))
            own.add(dve.memset(o_acc[:, :, :], 0.0))
            own.wait()
            dve.wait_ge(neg_col_ready, 1)
            dve.tensor_copy(neg_big_col[:, :], ps_m[:, 0:2]).then_inc(state_ready, 1)

            def start(c):
                dve.wait_ge(masks_in, c * (16 * CH) + 16 * CH)
                dve.wait_ge(pvs, c * (STEPS * NU) + PV0)
                dve.wait_ge(a_max, c * (32 * NU) + 2)
                dve.wait_ge(state_ready, 1)
                dve.scalar_tensor_tensor(bias_kq[:, :, :], mask_in[:, :, 0:SQ], 0.0,
                                         neg_big[:, :].unsqueeze(1).to_broadcast([P, CH, SQ]),
                                         ALU.is_equal, ALU.mult).then_inc(masks_ready, 1)
                for qt in range(2):
                    dve.tensor_scalar(bias_qk[:, qt, :].rearrange("p (j n) -> p j n", j=CH),
                                      mask_in[:, :, SQ + P * qt:SQ + P * qt + P], 0.0, neg_big_col[:, qt:qt + 1],
                                      ALU.is_equal, ALU.mult).then_inc(masks_ready, 1)

            def stage(c, s, k):
                b_on, a_on, k_on, par, _ = parts(s, k)
                cs = c * NU + s
                tk = c * (TICKETS * NU) + tickets_before(s)
                if a_on:
                    w = cs - 1
                    run = m_run[:, bass.ds(s - 1, 1), :].rearrange("p a n -> p (a n)")
                    mo = w * 7
                    if (isinstance(s, int) and s == 1):
                        dve.wait_ge(masks_ready, c * 3 + 3)
                    dve.wait_ge(f_ready, w)
                    dve.wait_ge(a_max, w * 32 + 2)
                    dve.tensor_copy(m_old[:, :], run).then_inc(max_own, 1)
                    for xx in range(32):
                        hh, c2, qt = xx // 4, xx // 2 % 2, xx % 2
                        col = slice(HU * qt + hh, HU * qt + hh + 1)
                        dve.wait_ge(a_scores, w * 32 + xx + 1)
                        dve.wait_ge(a_max, w * 32 + xx + 1)
                        if xx == 0:
                            dve.wait_ge(max_own, mo + 1)
                        bias = bias_qk[:, qt, 512 * c2:512 * c2 + 512]
                        older = (m_cur if c2 else m_old)[:, col]
                        if isinstance(c, int):
                            dve.tensor_tensor_reduce(junk[:, xx % 2, :], ps_a[:, xx % 2, :], bias, 1.0, older,
                                                     ALU.add, ALU.max, m_cur[:, col]).then_inc(a_max, 1)
                            continue
                        m3 = w * 64 + 2 * xx
                        dve.wait_ge(a_max, w * 32 + xx + 2)
                        dve.tensor_tensor(masked[:, :], ps_a[:, xx % 2, :], bias, ALU.add).then_inc(max_steps, 1)
                        dve.wait_ge(max_steps, m3 - 64 * NU + 1)
                        dve.tensor_reduce(m_tile[:, :], masked[:, :], AX.X, ALU.max).then_inc(max_steps, 1)
                        dve.wait_ge(max_steps, m3 - 64 * NU + 2)
                        dve.tensor_tensor(m_cur[:, col], m_tile[:, :], older, ALU.max).then_inc(a_max, 1)
                    dve.wait_ge(a_max, w * 32 + 34)
                    by_qt = lambda a: a.rearrange("p (t h) -> p t h", t=2)
                    dve.tensor_scalar(m_neg[:, 0, :], m_cur[:, :], -1.0, None, ALU.mult).then_inc(max_own, 1)
                    dve.tensor_scalar(m_parts[:, :, 0, :], by_qt(m_cur[:, :]), -1.0, None, ALU.mult
                                      ).then_inc(max_own, 1)
                    dve.tensor_copy(run, m_cur[:, :]).then_inc(max_own, 1)
                    dve.wait_ge(max_own, mo + 3)
                    dve.tensor_tensor(by_qt(m_neg[:, 1, :]), by_qt(m_neg[:, 0, :]), m_parts[:, :, 0, :],
                                      ALU.subtract).then_inc(max_own, 1)
                    dve.wait_ge(max_own, mo + 5)
                    dve.tensor_copy(m_parts[:, :, 1, :], by_qt(m_neg[:, 1, :])).then_inc(max_own, 1)
                    dve.wait_ge(max_own, mo + 6)
                    dve.tensor_tensor(m_parts[:, :, 2, :], by_qt(m_neg[:, 1, :]), m_parts[:, :, 1, :], ALU.subtract
                                      ).then_inc(max_own, 1)
                    dve.tensor_tensor(m_diff[:, :].rearrange("p (g t h) -> p g t h", g=2, t=2),
                                      m_old[:, :].rearrange("p (t g h) -> p g t h", g=2, t=2),
                                      m_cur[:, :].rearrange("p (t g h) -> p g t h", g=2, t=2),
                                      ALU.subtract).then_inc(diff_ready, 1)
                    n = tk + 2 + (2 if k_on else 0)
                    dve.wait_ge(misc_full, n + 1)
                    dve.wait_ge(mrow_in, w * 32)
                    dve.tensor_copy(m_rows[:, :], ps_m[0:48, 0:P]).then_inc(misc_taken, 1)
                if b_on:
                    w = cs - 2
                    acc = o_acc[:, bass.ds(s - 2, 1), :].rearrange("p a n -> p (a n)")
                    n = tk + (2 + 1 if a_on else 0) + (2 if k_on else 0)
                    dve.wait_ge(misc_full, n + 1)
                    dve.tensor_tensor(acc, acc, ps_m[:, :], ALU.mult).then_inc(misc_taken, 1)
                    dve.wait_ge(pvs, w * STEPS + PV0 + STEPS)
                    dve.wait_ge(misc_taken, n + 2)
                    dve.tensor_tensor(acc, acc, ps_o[:, :], ALU.add).then_inc(o_free, 1)

            n = chunks_and_stages(dve, stage, start)
            dve.wait_ge(o_free, n * NU + 1)
            own.add(dve.memset(junk[:, 0, 0:1], 0.0))
            own.wait()
            for u in range(NU):
                if u >= 2:
                    dve.wait_ge(normed, u - 1)
                own.add(dve.stream_shuffle(sums[:, u % 2, :], o_acc[:, u, :], [D] * 32))
                own.wait()
                dve.reciprocal(sums[:, u % 2, :], sums[:, u % 2, :]).then_inc(sums_out, 1)
            for b in range(NB):
                dve.wait_ge(att_full, b + 1)
                dve.wait_ge(pool_own, 1)
                dve.tensor_tensor(x_sb[:, 2 * b:2 * b + 2, :], x_sb[:, 2 * b:2 * b + 2, :],
                                  ps_s[:, b % 2, 0:512].rearrange("p (t n) -> p t n", t=2), ALU.add).then_inc(x1_ready, 1)

            dve.wait_ge(x1_ready, NB)
            layernorm(x_sb, xn)
            layernorm_end(x_sb, xn, 2)
            for i in range(4):
                t = i % 2
                ps = ps_s[:, i % 2, :]
                dve.wait_ge(rot_full, i + 1)
                if i >= 2:
                    dve.wait_ge(parts_act, 3 * (i - 2) + 3)
                    dve.wait_ge(parts_pool, i - 1)
                elif i == 0:
                    dve.wait_ge(in_late, 80)
                    dve.wait_ge(att_full, NB)
                dve.stream_shuffle(r_swap[t], ps, [c ^ 1 for c in range(32)]).then_inc(swapped, 1)
                dve.tensor_tensor(r_full[t].rearrange("p (b q) -> p b q", b=NB), ps.rearrange("p (b q) -> p b q", b=NB),
                                  rope[:, 2 * t, :].unsqueeze(1).to_broadcast([P, NB, SQ]), ALU.mult
                                  ).then_inc(cos_done, 1)
                dve.wait_ge(cos_done, i + 1)
                dve.wait_ge(sin_done, i + 1)
                dve.tensor_tensor(r_full[t], r_full[t], r_swap[t], ALU.add).then_inc(rotated, 1)
                dve.wait_ge(parts_act, 3 * i + (1 if t == 0 else 2))
                dve.wait_ge(rotated, i + 1)
                dve.tensor_tensor(r_rest[t], r_full[t], r_slots[t][:, t, :], ALU.subtract).then_inc(rest_done, 1)

            def self_out(u):
                dve.wait_ge(t_pvs, 4 * u + 4)
                dve.wait_ge(parts_pool, 4)
                if u >= 2:
                    dve.wait_ge(self_normed, u - 1)
                own.add(dve.stream_shuffle(t_sums[:, u % 2, :], ps_o[:, :], [D] * 32))
                dve.tensor_copy(o_acc[:, u, :], ps_o[:, :]).then_inc(t_out, 1)
                own.wait()
                dve.reciprocal(t_sums[:, u % 2, :], t_sums[:, u % 2, :]).then_inc(t_out, 1)

            by_qt = lambda a: a.rearrange("p (t h) -> p t h", t=2)
            for u in range(NU):
                for y in range(8):
                    hp, qt = y // 2, y % 2
                    dve.wait_ge(self_scores, 8 * u + y + 1)
                    if y == 0 and u:
                        own.wait()
                    dve.tensor_reduce(m_cur[:, HU * qt + 2 * hp:HU * qt + 2 * hp + 2],
                                      ps_a[:, y % 2, :].rearrange("p (h k) -> p h k", h=2), AX.X, ALU.max
                                      ).then_inc(self_max, 1)
                dve.wait_ge(self_max, 8 * u + 8)
                own.add(dve.tensor_scalar(m_neg[:, 0, :], m_cur[:, :], -1.0, None, ALU.mult))
                if u:
                    dve.wait_ge(rows_full, u)
                own.add(dve.tensor_scalar(m_parts[:, :, 0, :], by_qt(m_cur[:, :]), -1.0, None, ALU.mult))
                own.wait()
                own.add(dve.tensor_tensor(by_qt(m_neg[:, 1, :]), by_qt(m_neg[:, 0, :]), m_parts[:, :, 0, :],
                                          ALU.subtract))
                own.wait()
                own.add(dve.tensor_copy(m_parts[:, :, 1, :], by_qt(m_neg[:, 1, :])))
                own.wait()
                dve.tensor_tensor(m_parts[:, :, 2, :], by_qt(m_neg[:, 1, :]), m_parts[:, :, 1, :], ALU.subtract
                                  ).then_inc(parts_ready, 1)
                dve.wait_ge(rows_full, u + 1)
                if u:
                    dve.wait_ge(rows_in_place, 32 * u)
                dve.tensor_copy(m_rows[:, :], ps_m[0:48, 0:P]).then_inc(rows_taken, 1)
                if u:
                    self_out(u - 1)
            self_out(NU - 1)
            for b in range(NB):
                dve.wait_ge(att2_full, b + 1)
                dve.wait_ge(pool_own, 2)
                dve.tensor_tensor(x_sb[:, 2 * b:2 * b + 2, :], x_sb[:, 2 * b:2 * b + 2, :],
                                  ps_s[:, b % 2, 0:512].rearrange("p (t n) -> p t n", t=2), ALU.add).then_inc(x2_ready, 1)

            dve.wait_ge(x2_ready, NB)
            layernorm(x_sb, xn)
            layernorm_end(x_sb, xn, 3)
            te = lambda k: route[:, k, :, :]
            over_t = lambda a: a.unsqueeze(1).to_broadcast([P, NT, NE])
            over_e = lambda a: a.unsqueeze(2).to_broadcast([P, NT, NE])

            def then(ins):
                own.add(ins)
                own.wait()

            dve.wait_ge(gate_full, 1)
            then(dve.tensor_tensor(te(0), ps_m[:, 0:NT * NE].rearrange("p (t e) -> p t e", t=NT),
                                   over_t(rows_bc[:, 2 * E:2 * E + NE]), ALU.add))
            then(dve.tensor_tensor(te(0), te(0), over_t(rows_bc[:, 2 * E + NE:2 * E + 2 * NE]), ALU.add))
            then(dve.tensor_reduce(route[:, 1, 0, :], te(0), AX.X, ALU.max))
            then(dve.tensor_tensor(te(2), te(0), over_e(route[:, 1, 0, :]), ALU.is_ge))
            rev = cst[:, P + 64:P + 64 + NE]
            then(dve.tensor_tensor(te(2), te(2), over_t(rev), ALU.mult))
            then(dve.tensor_reduce(route[:, 1, 1, :], te(2), AX.X, ALU.max))
            then(dve.tensor_tensor(te(3), over_t(rev), over_e(route[:, 1, 1, :]), ALU.is_equal))
            dve.tensor_copy(route_b[:, :, :], te(3)).then_inc(hot_ready, 1)
            dve.wait_ge(ranks_full, 1)
            own.add(dve.memset(route[:, 5, 0, :], 0.0))
            then(dve.tensor_copy(te(4), ps_m[:, 64:128].rearrange("p (t e) -> p t e", t=NT)))
            for t in range(1, NT):
                then(dve.tensor_tensor(route[:, 5, t, :], route[:, 5, t - 1, :], route[:, 4, t - 1, :], ALU.add))
            total, tiles, upto, base, base_row = (route[:, 6, k, :] for k in range(5))
            then(dve.tensor_tensor(total, route[:, 5, NT - 1, :], route[:, 4, NT - 1, :], ALU.add))
            more = route[:, 7, :, 0:NT - 1]
            then(dve.tensor_tensor(more, total.unsqueeze(2).to_broadcast([P, NE, NT - 1]),
                                   cst[:, P + 80:P + 80 + NT - 1].unsqueeze(1).to_broadcast([P, NE, NT - 1]), ALU.is_gt))
            then(dve.tensor_reduce(tiles, more, AX.X, ALU.add))
            own.add(dve.memset(route[:, 6, 5, :], 1.0))
            then(dve.tensor_scalar(tiles, tiles, 1.0, None, ALU.add))
            then(dve.tensor_tensor_scan(upto, route[:, 6, 5, :], tiles, 0.0, ALU.mult, ALU.add))
            then(dve.tensor_tensor(base, upto, tiles, ALU.subtract))
            dve.tensor_copy(runs_i[:, 0:NE], upto[0:1]).then_inc(runs_ready, 1)
            dve.tensor_copy(runs_i[:, NE:2 * NE], base[0:1]).then_inc(runs_ready, 1)
            then(dve.tensor_scalar(base_row, base, float(P), None, ALU.mult))
            then(dve.tensor_tensor(te(2), te(5), ps_m[:, 128:192].rearrange("p (t e) -> p t e", t=NT), ALU.add))
            then(dve.tensor_tensor(te(2), te(2), over_t(base_row), ALU.add))
            then(dve.tensor_tensor(te(2), te(2), te(3), ALU.mult))
            then(dve.tensor_reduce(route[:, 1, 2, :], te(2), AX.X, ALU.add))
            dve.tensor_copy(slot_i[:, :], route[:, 1, 2, :]).then_inc(slots_ready, 1)

            dve.wait_ge(b2_in, 16)
            dve.wait_ge(xs_taken, 8)

            def y_out(e, j):
                dve.wait_ge(y_full, j + 1)
                dve.tensor_tensor(y_all[:, bass.ds(j, 1), :].rearrange("p a n -> p (a n)"), ps_o[:, 0:E],
                                  b2_bc[:, e, :], ALU.add).then_inc(y_taken, 1)

            expert_tiles(dve, y_out)
            for t in range(NT):
                dve.wait_ge(gathered[t], 16)
                dve.tensor_tensor(x_sb[:, t, :], x_sb[:, t, :], picked[:, t, :], ALU.add).then_inc(x3_ready, 1)

        @block.scalar
        def _(act):
            act.sem_inc(exps, 2)
            act.sem_inc(misc_taken, 1)
            act.sem_inc(a_max, 2)
            act.sem_inc(pvs, PV0)
            act.sem_inc(o_free, 1)
            act.sem_inc(h_ready, F // P)
            act.sem_inc(y_taken, 1)
            act.wait_ge(in_w, 64)

            def deviations_and_rows(n):
                act.wait_ge(ln_var, n)
                act.wait_ge(const_ready, 1)
                act.activation(ln_r[:, :], ln_r[:, :], ACT.Sqrt, bias=eps_sb[:, 0:1]).then_inc(ln_std, 1)
                for i in range(4):
                    act.wait_ge(xt_full, 4 * (n - 1) + i + 1)
                    k, half = i // 2, i % 2
                    act.copy(xn_t[:, k, 512 * half:512 * half + 512], ps_t[:, 512 * i:512 * i + 512]
                             ).then_inc(xt_taken, 1)

            deviations_and_rows(1)
            for i in range(4):
                act.wait_ge(q_proj, i + 1)
                src = [ps_a[:, 0, :], ps_a[:, 1, :], ps_o[:, :], ps_t[:, 0:512]][i]
                act.activation(q_full[:, 512 * i:512 * i + 512], src, ACT.Identity,
                               bias=bias_sb[:, i // 2:i // 2 + 1]).then_inc(q_taken, 1)

            def stage(c, s, k):
                b_on, a_on, k_on, par, _ = parts(s, k)
                cs = c * NU + s
                tk = c * (TICKETS * NU) + tickets_before(s)

                def v_out(i):
                    act.wait_ge(misc_full, tk + i + 1)
                    if i == 0:
                        act.wait_ge(pvs, cs * STEPS)
                    act.copy(v_sb[:, 1 - par, 4 * i:4 * i + 4, :, 0:D],
                             ps_m[:, :].rearrange("p (j h d) -> p j h d", j=4, h=HU)).then_inc(misc_taken, 1)

                def k_out(i):
                    act.wait_ge(misc_full, tk + (2 if a_on else 0) + i + 1)
                    act.wait_ge(k_pool, cs * 2)
                    act.activation(k_full[:, 512 * i:512 * i + 512], ps_m[:, :], ACT.Identity,
                                   bias=bias_sb[:, 2 + par:3 + par]).then_inc(misc_taken, 1)

                def k_first(slot):
                    if slot == 1:
                        act.wait_ge(misc_taken, tk + (2 if a_on else 0) + 3)
                        act.wait_ge(k_low, cs * 128)
                        act.wait_ge(k_high, cs * 128)
                    act.copy(k_slots[:, slot, :], k_full).then_inc(k_act, 1)

                def k_second():
                    act.wait_ge(k_pool, cs * 2 + 1)
                    act.copy(k_slots[:, 2, :], k_rest).then_inc(k_act, 1)

                def factor():
                    act.wait_ge(diff_ready, cs)
                    act.activation(f_bc[:, 1 - par, :, :], m_diff[:, :].unsqueeze(2).to_broadcast([P, 16, 32]),
                                   ACT.Exp).then_inc(f_ready, 1)

                for i in range(STEPS):
                    if b_on:
                        w = cs - 2
                        act.wait_ge(scores, w * STEPS + i + 1)
                        act.wait_ge(pvs, w * STEPS + PV0 + i - 1)
                        act.activation(probs[:, i % 2, :], ps_s[:, i % 2, :], ACT.Exp).then_inc(exps, 1)
                    if a_on and i < 2:
                        v_out(i)
                    if k_on and i in (6, 7):
                        k_out(i - 6)
                    if k_on and i in (8, 9):
                        k_first((1, 3)[i - 8])
                    if k_on and i == 11:
                        k_second()
                    if a_on and i == 14:
                        factor()

            act.wait_ge(state_ready, 1)
            chunks_and_stages(act, stage)
            for u in range(NU):
                b, half = u // 2, u % 2
                act.wait_ge(normed, u + 1)
                for g in range(2):
                    sl = o_acc[:, u, SQ * g:SQ * g + SQ]
                    act.activation(sl, sl, ACT.Identity, bias=bias_sb[:, 4 + 2 * half + g:5 + 2 * half + g]
                                   ).then_inc(att_in, 1)

            deviations_and_rows(2)
            for i in range(4):
                t = i % 2
                act.wait_ge(rotated, i + 1)
                if i >= 2:
                    act.wait_ge(stacked[0], 16 * 4 * HU)
                else:
                    act.wait_ge(normed, NU)
                for slot in ((0,), (1, 3))[t]:
                    act.copy(r_slots[t][:, slot, :], r_full[t]).then_inc(parts_act, 1)
                act.wait_ge(rest_done, i + 1)
                for slot in ((1, 2), (2,))[t]:
                    act.copy(r_slots[t][:, slot, :], r_rest[t]).then_inc(parts_act, 1)
            for t in range(NT):
                act.wait_ge(v_full, t + 1)
                act.copy(v_sb.rearrange("p a t h c -> p a t (h c)")[:, :, t, :].rearrange(
                    "p a (h c) -> p a h c", c=SLOT)[:, :, :, 0:D],
                         ps_a[:, t % 2, 0:E].rearrange("p (a h c) -> p a h c", a=2, h=HU)).then_inc(v_taken, 1)
            for u in range(NU):
                for i in range(4):
                    act.wait_ge(t_scores, 4 * u + i + 1)
                    if 4 * u + i >= 2:
                        act.wait_ge(t_pvs, 4 * u + i - 1)
                    act.activation(probs[:, i % 2, :], ps_s[:, i % 2, :], ACT.Exp).then_inc(t_exps, 1)
            deviations_and_rows(3)
            for r in range(8):
                n = min(4, KE * SLOTS - 4 * r)
                act.wait_ge(xs_full, r + 1)
                act.copy(xs_t.rearrange("p k n -> p (k n)")[:, 512 * r:512 * r + P * n],
                         ps_t[:, 512 * (r % 4):512 * (r % 4) + P * n]).then_inc(xs_taken, 1)

            def relu(e, j):
                for c in range(F // P):
                    if c % 2 == 0:
                        act.wait_ge(h_full, j * (F // P) + c + 2)
                    if c == 0:
                        act.wait_ge(y_full, j)
                    act.activation(hidden[:, c, :], ps_t[:, 256 * c:256 * c + P], ACT.Relu, bias=b1_sb[:, e, c:c + 1]
                                   ).then_inc(h_ready, 1)

            expert_tiles(act, relu)

        @block.gpsimd
        def _(pool):
            pool.wait_ge(xn_ready, NT)
            pool.wait_ge(in_w, 64)
            def add_row(k):
                pool.tensor_tensor(x_sb[:, :, :], x_sb[:, :, :],
                                   rows_bc[:, E * k:E * k + E].unsqueeze(1).to_broadcast([P, NT, E]),
                                   ALU.add).then_inc(pool_own, 1)

            add_row(0)

            def stage(c, s, k):
                b_on, a_on, k_on, par, _ = parts(s, k)
                cs = c * NU + s
                if k_on:
                    pool.wait_ge(k_act, cs * 3 + 1)
                    pool.wait_ge(k_pool, cs * 2)
                    pool.tensor_tensor(k_rest, k_full, k_slots[:, 1, :], ALU.subtract).then_inc(k_pool, 1)
                    pool.wait_ge(k_act, cs * 3 + 3)
                    pool.wait_ge(k_pool, cs * 2 + 1)
                    pool.tensor_tensor(k_slots[:, 0, :], k_rest, k_slots[:, 2, :], ALU.subtract).then_inc(k_pool, 1)

            pool.wait_ge(q_stacked, 16 * 2 * HU)
            chunks_and_stages(pool, stage)
            for u in range(NU):
                pool.wait_ge(sums_out, u + 1)
                pool.tensor_tensor(o_acc[:, u, :], o_acc[:, u, :], sums[:, u % 2, :], ALU.mult).then_inc(normed, 1)
            pool.wait_ge(xn_ready, 2 * NT)
            add_row(1)
            for i in range(4):
                t = i % 2
                pool.wait_ge(swapped, i + 1)
                pool.tensor_tensor(r_swap[t].rearrange("p (b q) -> p b q", b=NB),
                                   r_swap[t].rearrange("p (b q) -> p b q", b=NB),
                                   rope[:, 2 * t + 1, :].unsqueeze(1).to_broadcast([P, NB, SQ]), ALU.mult
                                   ).then_inc(sin_done, 1)
                pool.wait_ge(parts_act, 3 * i + 3)
                pool.wait_ge(rest_done, i + 1)
                second, third = ((1, 3), (2, 0))[t]
                pool.tensor_tensor(r_slots[t][:, third, :], r_rest[t], r_slots[t][:, second, :], ALU.subtract
                                   ).then_inc(parts_pool, 1)
            for u in range(NU):
                pool.wait_ge(t_out, 2 * u + 2)
                pool.tensor_tensor(o_acc[:, u, :], o_acc[:, u, :], t_sums[:, u % 2, :], ALU.mult
                                   ).then_inc(self_normed, 1)
            pool.wait_ge(slots_ready, 1)
            pool.wait_ge(xs_zeroed, 32)
            pool.wait_ge(xn_ready, 3 * NT)
            for t in range(NT):
                pool.indirect_dma_start(xs_dram, bass.IndirectOffsetOnAxis(ap=slot_i[:, t:t + 1], axis=0),
                                        xn[:, t, :], None).then_inc(scattered, 16)
            pool.wait_ge(runs_ready, 2)
            n = pool.value_load(runs_i[0:1, NE - 1:NE], min_val=NE, max_val=SLOTS)
            pool.wait_ge(ys_stored, n * 16)
            pool.tensor_tensor(m_neg[:, 0, :], m_neg[:, 1, :], m_neg[:, 1, :], ALU.add).then_inc(pool_own, 1)
            pool.wait_ge(pool_own, 3)
            for t in range(NT):
                pool.indirect_dma_start(picked[:, t, :], None, ys_dram,
                                        bass.IndirectOffsetOnAxis(ap=slot_i[:, t:t + 1], axis=0)).then_inc(gathered[t], 16)

        @block.tensor
        def _(pe):
            pe.wait_ge(const_ready, 1)

            def turn_rows(n):
                for i in range(4):
                    k, half = i // 2, i % 2
                    pe.wait_ge(xn_ready, NT * (n - 1) + 4 * half + 4)
                    for t in range(4 * half, 4 * half + 4):
                        mm = pe.transpose(ps_t[:, 1024 * k + P * t:1024 * k + P * t + P], xn[:, t, P * k:P * k + P],
                                          ident_f)
                    mm.then_inc(xt_full, 1)

            turn_rows(1)
            pe.wait_ge(in_w, 64)
            pe.wait_ge(xt_taken, 4)
            for i in range(4):
                half, bb = i // 2, i % 2
                dst = [ps_a[:, 0, :], ps_a[:, 1, :], ps_o[:, :], ps_t[:, 0:512]][i]
                for k in range(KE):
                    mm = pe.matmul(dst, w_sb[:, 0, k, P * half:P * half + P], xn_t[:, k, 512 * bb:512 * bb + 512],
                                   start=(k == 0), stop=(k == KE - 1))
                mm.then_inc(q_proj, 1)
            for t in range(TK):
                pe.wait_ge(nz_ready, t + 1)
                pe.matmul(ps_m[:, 0:SQ], ones_b[:, :], mask_nz[:, t, :], start=(t == 0), stop=(t == TK - 1))
            pe.wait_ge(any_ready, 1)
            pe.matmul(ps_m[:, SQ:SQ + TK], ones_b[:, :], tile_any_b[:, :], start=True, stop=True).then_inc(counts_ready, 1)
            pe.wait_ge(neg_ready, 1)
            pe.wait_ge(tiles_ready, 1)
            for qt in range(2):
                mm = pe.matmul(ps_m[:, qt:qt + 1], neg_big[0:1, P * qt:P * qt + P], cst[0:1, 2 * P - 1:2 * P],
                               start=True, stop=True)
            mm.then_inc(neg_col_ready, 1)

            def stage(c, s, k):
                b_on, a_on, k_on, par, _ = parts(s, k)
                cs = c * NU + s
                tk = c * (TICKETS * NU) + tickets_before(s)
                if isinstance(s, int):
                    at_a = (s - 1) % 2 * NB + (s - 1) // 2
                    at_b = (s - 2) % 2 * NB + (s - 2) // 2
                elif k == 0:
                    at_a, at_b = s // 2 + (NB - 1), s // 2 - 1
                else:
                    at_a, at_b = (s - 1) // 2, (s - 1) // 2 + (NB - 1)
                n = tk

                def fill(n, mm_of):
                    pe.wait_ge(misc_taken, n + 1)
                    mm_of().then_inc(misc_full, 1)

                def v_mm(i):
                    def go():
                        for j in range(4 * i, 4 * i + 4):
                            for kk in range(KE):
                                mm = pe.matmul(ps_m[:, P * (j % 4):P * (j % 4) + P], ctx_sb[:, j, kk, :],
                                               w_sb[:, 2, kk, P * (1 - par):P * (1 - par) + P],
                                               start=(kk == 0), stop=(kk == KE - 1))
                        return mm
                    return go

                def k_mm(i):
                    def go():
                        for kk in range(KE):
                            mm = pe.matmul(ps_m[:, :], w_sb[:, 1, kk, P * par:P * par + P],
                                           ctx_sb[:, 4 * i:4 * i + 4, kk, :], start=(kk == 0), stop=(kk == KE - 1))
                        return mm
                    return go

                def a_mm(xx):
                    hh, c2, qt = xx // 4, xx // 2 % 2, xx % 2
                    w = cs - 1
                    if xx == 0:
                        pe.wait_ge(k_low, w * 128 + 128)
                    if xx == 16:
                        pe.wait_ge(k_high, w * 128 + 128)
                    pe.wait_ge(a_max, w * 32 + xx + 1)
                    pe.matmul(ps_a[:, xx % 2, :],
                              q_stack[0:PAIR, hh, bass.ds(at_a, 1), P * qt:P * qt + P].rearrange("p a q -> p (a q)"),
                              k_stack[0:PAIR, 1 - par, hh, 512 * c2:512 * c2 + 512],
                              start=True, stop=True).then_inc(a_scores, 1)

                def s_mm(i):
                    g, j = i // CH, i % CH
                    w = cs - 2
                    if i == 0:
                        pe.wait_ge(mrow_in, w * 32 + 32)
                        pe.wait_ge(masks_ready, c * 3 + 1)
                    pe.wait_ge(exps, w * STEPS + i + 1)
                    for h4 in range(4):
                        if h4 % 2 == 0:
                            pe.matmul(ps_s[:, i % 2, SQ * h4:SQ * (h4 + 2)], ident_b[:, :],
                                      bias_kq[:, j:j + 1, :].to_broadcast([P, 2, SQ]),
                                      start=True, stop=False, skip_group_check=True)
                        mm = pe.matmul(ps_s[:, i % 2, SQ * h4:SQ * h4 + SQ],
                                       k_stack[0:ROWS, par, 4 * g + h4, P * j:P * j + P],
                                       q_stack[0:ROWS, 4 * g + h4, bass.ds(at_b, 1), :].rearrange("p a q -> p (a q)"),
                                       start=False, stop=h4 % 2 == 1, skip_group_check=True)
                    mm.then_inc(scores, 1)

                def pv_mm(i):
                    g, j = i // CH, i % CH
                    w = cs - 2
                    if i == 0:
                        pe.wait_ge(o_free, w + 1)
                    pe.wait_ge(exps, w * STEPS + i + 3)
                    for h4 in range(4):
                        mm = pe.matmul(ps_o[32 * h4:32 * h4 + 32, SQ * g:SQ * g + SQ],
                                       v_sb[:, par, j, 4 * g + h4, :], probs[:, i % 2, SQ * h4:SQ * h4 + SQ],
                                       start=(j == 0), stop=(j == CH - 1), tile_position=(0, 32 * h4),
                                       skip_group_check=True)
                    mm.then_inc(pvs, 1)

                def m_mm():
                    pe.wait_ge(max_own, (cs - 1) * 7 + 7)
                    return pe.matmul(ps_m[0:48, 0:P], m_parts[:, :, :, :].rearrange("p t a h -> p (t a h)"), ident_b[:, :],
                                     start=True, stop=True)

                def f_mm():
                    pe.wait_ge(f_ready, cs - 2 + 1)
                    for gt in range(4):
                        mm = pe.matmul(ps_m[:, P * gt:P * gt + P],
                                       f_bc[:, par, 4 * gt:4 * gt + 4, :].rearrange("p h r -> p (h r)"), ident_f,
                                       start=True, stop=True)
                    return mm

                for i in range(STEPS):
                    if b_on:
                        s_mm(i)
                    if a_on:
                        for xx in range(3 * i, min(3 * i + 3, 32)):
                            a_mm(xx)
                    if b_on and i:
                        pv_mm(i - 1)
                    if a_on and i < 2:
                        fill(n, v_mm(i))
                        n = n + 1
                    if k_on and i in (6, 7):
                        if i == 6 and par == 0:
                            bt = (cs // 2 if not isinstance(s, int) else c * NB + s // 2)
                            bt = c * NB + (s // 2)
                            pe.wait_ge(ctx_in, bt * 128 + 128)
                        fill(n, k_mm(i - 6))
                        n = n + 1
                    if a_on and i == 13:
                        fill(n, m_mm)
                        n = n + 1
                    if b_on and i == 14:
                        fill(n, f_mm)
                        n = n + 1
                if b_on:
                    pv_mm(STEPS - 1)

            pe.wait_ge(state_ready, 1)
            pe.wait_ge(q_stacked, 16 * 2 * HU)
            chunks_and_stages(pe, stage)
            for b in range(NB):
                pe.wait_ge(att_in, 4 * b + 4)
                if b >= 2:
                    pe.wait_ge(x1_ready, b - 1)
                for qt in range(2):
                    for hg in range(4):
                        mm = pe.matmul(ps_s[:, b % 2, E * qt:E * qt + E],
                                       o_acc[:, 2 * b + hg // 2, SQ * (hg % 2) + P * qt:SQ * (hg % 2) + P * qt + P],
                                       wo_sb[:, 0, hg, :], start=(hg == 0), stop=(hg == 3))
                mm.then_inc(att_full, 1)

            pe.wait_ge(x1_ready, NB)
            turn_rows(2)
            pe.wait_ge(xt_taken, 8)
            pe.wait_ge(in_late, 80)
            for i in range(4):
                half, t = i // 2, i % 2
                if i >= 2:
                    pe.wait_ge(swapped, i - 1)
                    pe.wait_ge(cos_done, i - 1)
                for bb in range(2):
                    for k in range(KE):
                        mm = pe.matmul(ps_s[:, i % 2, 512 * bb:512 * bb + 512],
                                       w_qkv[:, k, E * t + P * half:E * t + P * half + P],
                                       xn_t[:, k, 512 * bb:512 * bb + 512], start=(k == 0), stop=(k == KE - 1))
                mm.then_inc(rot_full, 1)
            for t in range(NT):
                if t >= 2:
                    pe.wait_ge(v_taken, t - 1)
                for k in range(KE):
                    mm = pe.matmul(ps_a[:, t % 2, 0:E], xn_t[:, k, P * t:P * t + P], w_qkv[:, k, 2 * E:3 * E],
                                   start=(k == 0), stop=(k == KE - 1))
                mm.then_inc(v_full, 1)
            pe.wait_ge(v_taken, NT)
            pe.wait_ge(cos_done, 4)
            pe.wait_ge(swapped, 4)

            def self_max_scores(u):
                half, b = u // NB, u % NB
                if b == 0:
                    pe.wait_ge(stacked[half], 16 * 4 * HU)
                for y in range(8):
                    hp, qt = y // 2, y % 2
                    if 8 * u + y >= 2:
                        pe.wait_ge(self_max, 8 * u + y - 1)
                    pe.matmul(ps_a[:, y % 2, :], ident_b[:, :], causal[:, 0, qt:qt + 1, :].to_broadcast([P, 2, SQ]),
                              start=True, stop=False, skip_group_check=True)
                    for hh in (2 * hp, 2 * hp + 1):
                        mm = pe.matmul(ps_a[:, y % 2, SQ * (hh % 2):SQ * (hh % 2) + SQ],
                                       q_stack[0:PAIR, hh, u, P * qt:P * qt + P],
                                       k_stack[0:PAIR, half, hh, SQ * b:SQ * b + SQ],
                                       start=False, stop=hh % 2 == 1, skip_group_check=True)
                    mm.then_inc(self_scores, 1)

            def self_sums(u, i):
                half, b, g, j = u // NB, u % NB, i // 2, i % 2
                if i == 0:
                    pe.wait_ge(rows_in_place, 32 * u + 32)
                if 4 * u + i >= 2:
                    pe.wait_ge(t_exps, 4 * u + i - 1)
                for h4 in range(4):
                    if h4 % 2 == 0:
                        pe.matmul(ps_s[:, i % 2, SQ * h4:SQ * (h4 + 2)], ident_b[:, :],
                                  causal[:, 1, j:j + 1, :].to_broadcast([P, 2, SQ]),
                                  start=True, stop=False, skip_group_check=True)
                    mm = pe.matmul(ps_s[:, i % 2, SQ * h4:SQ * h4 + SQ],
                                   k_stack[0:ROWS, half, 4 * g + h4, SQ * b + P * j:SQ * b + P * j + P],
                                   q_stack[0:ROWS, 4 * g + h4, u, :],
                                   start=False, stop=h4 % 2 == 1, skip_group_check=True)
                mm.then_inc(t_scores, 1)

            def self_pv(u, i):
                half, b, g, j = u // NB, u % NB, i // 2, i % 2
                if i == 0 and u:
                    pe.wait_ge(t_out, 2 * u)
                pe.wait_ge(t_exps, 4 * u + i + 1)
                for h4 in range(4):
                    mm = pe.matmul(ps_o[32 * h4:32 * h4 + 32, SQ * g:SQ * g + SQ],
                                   v_sb[:, half, 2 * b + j, 4 * g + h4, :], probs[:, i % 2, SQ * h4:SQ * h4 + SQ],
                                   start=(j == 0), stop=(j == 1), tile_position=(0, 32 * h4), skip_group_check=True)
                mm.then_inc(t_pvs, 1)

            for u in range(NU + 1):
                if u < NU:
                    self_max_scores(u)
                if u:
                    for i in range(4):
                        self_sums(u - 1, i)
                        if i:
                            self_pv(u - 1, i - 1)
                    self_pv(u - 1, 3)
                if u < NU:
                    pe.wait_ge(parts_ready, u + 1)
                    if u:
                        pe.wait_ge(rows_taken, u)
                    pe.matmul(ps_m[0:48, 0:P], m_parts[:, :, :, :].rearrange("p t a h -> p (t a h)"), ident_b[:, :],
                              start=True, stop=True).then_inc(rows_full, 1)
            for b in range(NB):
                pe.wait_ge(self_normed, NU)
                if b >= 2:
                    pe.wait_ge(x2_ready, b - 1)
                for qt in range(2):
                    for hg in range(4):
                        mm = pe.matmul(ps_s[:, b % 2, E * qt:E * qt + E],
                                       o_acc[:, hg // 2 * NB + b, SQ * (hg % 2) + P * qt:SQ * (hg % 2) + P * qt + P],
                                       wo_sb[:, 1, hg, :], start=(hg == 0), stop=(hg == 3))
                mm.then_inc(att2_full, 1)

            pe.wait_ge(x2_ready, NB)
            turn_rows(3)
            pe.wait_ge(xt_taken, 12)
            for t in range(NT):
                for k in range(KE):
                    mm = pe.matmul(ps_m[:, NE * t:NE * t + NE], xn_t[:, k, P * t:P * t + P], gate_sb[:, k, :],
                                   start=(k == 0), stop=(k == KE - 1))
            mm.then_inc(gate_full, 1)
            pe.wait_ge(hot_ready, 1)
            hot = route_b[:, :, :].rearrange("p t e -> p (t e)")
            pe.matmul(ps_m[:, 64:128], ones_b[:, :], hot, start=True, stop=True)
            pe.matmul(ps_m[:, 128:192], lower_b[:, :], hot, start=True, stop=True).then_inc(ranks_full, 1)
            pe.wait_ge(xs_loaded, 16)
            for r in range(8):
                if r >= 4:
                    pe.wait_ge(xs_taken, r - 3)
                for i in range(4 * r, min(4 * r + 4, KE * SLOTS)):
                    mm = pe.transpose(ps_t[:, P * (i % 16):P * (i % 16) + P],
                                      xs_in[:, i % SLOTS, P * (i // SLOTS):P * (i // SLOTS) + P], ident_f)
                mm.then_inc(xs_full, 1)
            pe.wait_ge(xs_taken, 8)

            def expert(e, j):
                for c in range(F // P):
                    if c == 0:
                        pe.wait_ge(w_in[e], 32)
                    if c % 2 == 0:
                        pe.wait_ge(h_ready, j * (F // P) + c + 2)
                    for k in range(KE):
                        mm = pe.matmul(ps_t[:, 256 * c:256 * c + P], w1_sb[e][:, k, P * c:P * c + P],
                                       xs_t[:, k, bass.ds(j * P, P)], start=(k == 0), stop=(k == KE - 1))
                    mm.then_inc(h_full, 1)
                for c in range(F // P):
                    if c == 0:
                        pe.wait_ge(y_taken, j + 1)
                    pe.wait_ge(h_ready, j * (F // P) + (F // P) + c + 1)
                    mm = pe.matmul(ps_o[:, 0:E], hidden[:, c, :], w2_sb[e][:, c, :],
                                   start=(c == 0), stop=(c == F // P - 1))
                mm.then_inc(y_full, 1)

            expert_tiles(pe, expert)


def lay_out(i):
    c = np.zeros((TK + 1, P, NB, KE, P), np.float32)
    c[:TK] = i["ctx_1024"].reshape(NB, TK, P, KE, P).transpose(1, 4, 0, 3, 2)
    m = i["mask_1x1xSxS2_ik0"].reshape(SQ, TK, P)
    mk = np.zeros((TK + 1, P, 2 * SQ), m.dtype)
    mk[:TK, :, :SQ] = m.transpose(1, 2, 0)
    mk[:TK, :, SQ:] = m.reshape(2, P, TK, P).transpose(2, 1, 0, 3).reshape(TK, P, 2 * P)
    t = lambda w: w.T.reshape(KE, P, E).transpose(1, 0, 2)
    w = np.stack([t(i["L0_xattn_Wq"]), t(i["L0_xattn_Wk"]), t(i["L0_xattn_Wv"])], 1)

    def pad(wt):
        r = np.zeros((4, 32, 4, E), np.float32)
        r[:, :D] = wt.reshape(4, 4, D, E).transpose(1, 2, 0, 3)
        return r.reshape(P, 4, E)

    b = np.zeros((P, 8), np.float32)
    b[:, 0:2] = i["L0_xattn_bq"].reshape(2, P).T
    b[:, 2:4] = i["L0_xattn_bk"].reshape(2, P).T
    bv = np.zeros((4, 32, 4), np.float32)
    bv[:, :D] = i["L0_xattn_bv"].reshape(4, 4, D).transpose(1, 2, 0)
    b[:, 4:8] = bv.reshape(P, 4)
    cst = np.zeros((P, 4 * P), np.float32)
    cst[:, :P] = np.eye(P)
    cst[:, P:P + TK] = np.arange(TK)
    cst[:, P + 64:P + 64 + NE] = NE - np.arange(NE)
    cst[:, P + 80:P + 80 + NT - 1] = P * np.arange(1, NT)
    cst[:, 2 * P - 1] = 1
    cst[:, 2 * P:3 * P] = np.triu(np.ones((P, P)), 1)
    inv = (1.0 / np.float32(10000.0) ** (np.arange(0, D, 2, dtype=np.float32) / np.float32(D))).astype(np.float32)
    freq = np.repeat(np.outer(np.arange(SQ, dtype=np.float32), inv), 2, axis=1)
    sign = np.tile(np.array([-1, 1], np.float32), D // 2)
    cos, sin = np.cos(freq).T, (np.sin(freq) * sign).T
    rope = np.stack([cos * np.float32(D ** -0.5), sin * np.float32(D ** -0.5), cos, sin]).astype(np.float32)
    rope = np.tile(rope, (1, HU, 1)).transpose(1, 0, 2)
    at = np.arange(SQ)
    hidden = np.where(at[None, :] > at[:, None], -BIG, 0).astype(np.float32)
    causal = np.stack([hidden.reshape(2, P, SQ), hidden.T.reshape(2, P, SQ)]).transpose(2, 0, 1, 3)
    return {
        "x": i["x"], "ctx_l": c.reshape(TK + 1, P, NB * KE * P), "mask_l": mk, "w_l": w,
        "w_qkv_l": i["L0_attn_Wqkv"].reshape(KE, P, 3 * E).transpose(1, 0, 2),
        "wo_pad": np.stack([pad(i["L0_xattn_Wo"].T), pad(i["L0_attn_Wout"])], 1), "biases": b,
        "rows_in": np.concatenate([i["L0_xattn_bo"], i["L0_attn_bout"], i["L0_ffn_gate_b"],
                                   i["L0_ffn_expert_bias"]])[None],
        "consts": cst, "causal_in": causal.astype(mybir.dt.np(BF16)), "rope_in": rope,
        "gate_l": i["L0_ffn_gate_w"].T.reshape(KE, P, NE).transpose(1, 0, 2),
        "w1": i["L0_ffn_w1"], "b1_l": i["L0_ffn_b1"].reshape(NE, F // P, P).transpose(2, 0, 1),
        "w2": i["L0_ffn_w2"], "b2": i["L0_ffn_b2"],
    }


def kernel(**inputs):
    import concourse.bacc as bacc
    from concourse.bass_utils import run_bass_kernel_spmd

    nc = bacc.Bacc("TRN2", target_bir_lowering=False, num_devices=1)
    arrays = {k: np.ascontiguousarray(v) for k, v in lay_out({k: np.asarray(v) for k, v in inputs.items()}).items()}
    args = [nc.dram_tensor(k, v.shape, mybir.dt.from_np(v.dtype), kind="ExternalInput").ap()
            for k, v in arrays.items()]
    out = nc.dram_tensor("out", [NB, SQ, E], F32, kind="ExternalOutput").ap()
    build(nc, *args, out)
    return run_bass_kernel_spmd(nc, [arrays], core_ids=[0]).results[0]["out"]
```

```python
from contextlib import ExitStack

import numpy as np

import concourse.bass as bass
from concourse import mybir

F32 = mybir.dt.float32
BF16 = mybir.dt.bfloat16
I32 = mybir.dt.int32
ALU = mybir.AluOpType
ACT = mybir.ActivationFunctionType
AX = mybir.AxisListType

P = 128
NB, SQ, E = 4, 256, 256
H, D = 16, 16
LK = 4096
TK = LK // P
CH = 8
NU, HU = 8, 8
NT = NB * SQ // P
KE = E // P
SLOT = 32
BIG = float(2 ** 30)
EPS = 1e-5
NE, F = 8, 1024
SLOTS = NT + NE - 1
PAIR = 2 * D * 3
ROWS = PAIR + 4
STEPS = 2 * CH
TICKETS = 6


class Chain:

    def __init__(self, eng, sem, start=0):
        self.eng, self.sem, self.n = eng, sem, start

    def add(self, ins):
        self.n = self.n + 1
        ins.then_inc(self.sem, 1)
        return self.n

    def wait(self, n=None):
        self.eng.wait_ge(self.sem, self.n if n is None else n)


def tickets_before(s):
    if isinstance(s, int):
        return [0, 2][s] if s < 2 else 7 + 6 * (s - 2) if s <= 8 else 47
    return s * 6 - 5


def build(nc, x, ctx_l, mask_l, w_l, w_qkv_l, wo_pad, biases, rows_in, consts, causal_in, rope_in, gate_l,
          edges_in, w1, b1_l, w2, b2, out):
    ctx = ExitStack()
    with ctx:
        def sb(name, shape, dt):
            return ctx.enter_context(nc.sbuf_tensor(name, shape, dt))

        def sem(name):
            return ctx.enter_context(nc.semaphore(name))

        arena = sb("arena", [P, 170 * 256], F32)

        def cut(at, shape, dt, names=None, **sizes):
            n = int(np.prod(shape))
            size = n * (2 if dt == BF16 else 4) // 4
            v = arena[:, at * 256:at * 256 + size]
            if dt != F32:
                v = v.bitcast(dt)
            if len(shape) > 1:
                axes = "abcde"[:len(shape)]
                v = v.rearrange("p (%s) -> p %s" % (" ".join(axes), " ".join(axes)),
                                **dict(zip(axes[1:], shape[1:])))
            return v

        k_stack = cut(0, [2, HU, CH * P], BF16)
        q_stack = cut(32, [HU, NU, SQ], BF16)
        v_sb = cut(64, [2, CH, HU, SLOT], F32)
        work = cut(80, [4096], F32)
        o_acc = cut(96, [NU, 2 * SQ], F32)
        probs = cut(112, [2, 4 * SQ], F32)
        ctx_sb = cut(120, [CH, KE, P], F32)
        mask_in = cut(128, [CH, 2 * SQ], I32)
        bias_qk = cut(144, [2, CH * P], BF16)
        bias_kq = cut(148, [CH, SQ], BF16)
        junk = cut(152, [2, 512], BF16)
        masked = cut(152, [512], F32)
        w_sb = cut(154, [3, KE, E], F32)
        w_qkv = cut(160, [KE, 3 * E], F32)
        rope = cut(166, [4, SQ], F32)
        mask_all = cut(0, [TK, SQ], I32)
        mask_nz = cut(96, [TK, SQ], BF16)
        q_full = cut(112, [2048], F32)
        q_rest = cut(144, [2048], F32)
        q_slots = cut(96, [4, 2048], BF16)
        pick = cut(0, [TK, TK], F32)[0:1]
        xn = cut(128, [NT, E], F32)
        xn_t = cut(136, [KE, NT * P], F32)
        ctx_of = [ctx_sb, cut(128, [CH, KE, P], F32)]
        mask_line = cut(136, [CH * P], I32)[0:1]
        mask_row = cut(140, [CH * P], BF16)[0:1]
        sums = cut(144, [2, 2 * SQ], F32)
        k_slots = cut(80, [4, 1024], BF16)
        k_full = cut(88, [1024], F32)
        k_rest = cut(92, [1024], F32)
        r_slots = [cut(80, [4, 1024], BF16), cut(88, [4, 1024], BF16)]
        r_full = [cut(96, [1024], F32), cut(100, [1024], F32)]
        r_rest = [cut(104, [1024], F32), cut(108, [1024], F32)]
        r_swap = [cut(120, [1024], F32), cut(124, [1024], F32)]
        t_sums = cut(120, [2, 2 * SQ], F32)
        w1_sb = [cut(16 * e, [KE, F], F32) for e in range(NE)]
        w2_sb = [cut(16 * e + 8, [F // P, E], F32) for e in range(NE)]
        xs_in = cut(128, [SLOTS, E], F32)
        y_all = xs_in
        xs_t = cut(144, [KE, SLOTS * P], F32)
        b2_bc = cut(160, [NE, E], F32)
        picked = cut(144, [NT, E], F32)

        x_sb = sb("x_sb", [P, NT, E], F32)
        wo_sb = sb("wo_sb", [P, 2, 4, E], F32)
        bias_sb = sb("bias_sb", [P, 8], F32)
        b1_sb = sb("b1_sb", [P, NE, F // P], F32)
        gate_sb = sb("gate_sb", [P, KE, NE], F32)
        rows_bc = sb("rows_bc", [P, 2 * E + 2 * NE], F32)
        cst = sb("cst", [P, 4 * P], F32)
        causal = sb("causal", [P, 2, 2, SQ], BF16)
        ident_b = sb("ident_b", [P, P], BF16)
        ones_b = sb("ones_b", [P, P], BF16)
        lower_b = sb("lower_b", [P, P], BF16)
        zeros = sb("zeros", [P, E], F32)
        ln_stat = sb("ln_stat", [P, NT, 6], F32)
        ln_mv = sb("ln_mv", [P, NT, 2], F32)
        ln_r = sb("ln_r", [P, NT], F32)
        eps_sb = sb("eps_sb", [P, 1], F32)
        tile_any = sb("tile_any", [P, TK], F32)
        tile_any_b = sb("tile_any_b", [P, 2 * TK], BF16)
        tile_mixed = sb("tile_mixed", [P, TK], F32)
        row_dead = sb("row_dead", [P, SQ], F32)
        q_scale = sb("q_scale", [P, SQ], F32)
        neg_big = sb("neg_big", [P, SQ], F32)
        neg_big_col = sb("neg_big_col", [P, 2], F32)
        cmp = sb("cmp", [1, 256], F32)
        tiles_i = sb("tiles_i", [1, 48], I32)
        m_run = sb("m_run", [P, NU, 16], F32)
        m_tile = sb("m_tile", [P, 1], F32)
        m_half = sb("m_half", [P, 32], F32)
        m_quick = sb("m_quick", [P, 3, 2, HU], F32)
        q_parts = sb("q_parts", [P, 2, 2, 3, 4], BF16)
        quick_rows = sb("quick_rows", [24, 2, P], BF16)
        m_old = sb("m_old", [P, 16], F32)
        m_cur = sb("m_cur", [P, 16], F32)
        m_neg = sb("m_neg", [P, 2, 16], F32)
        m_parts = sb("m_parts", [P, 2, 3, HU], BF16)
        m_diff = sb("m_diff", [P, 16], F32)
        m_rows = sb("m_rows", [48, P], BF16)
        f_bc = sb("f_bc", [P, 2, 16, 32], F32)
        hidden = f_bc[:, :, :, :].rearrange("p a n r -> p (a n r)").rearrange("p (c n) -> p c n", c=F // P)
        route = sb("route", [P, 8, NT, NE], F32)
        route_b = sb("route_b", [P, NT, NE], BF16)
        slot_i = sb("slot_i", [P, NT], I32)
        runs_i = sb("runs_i", [1, 2 * NE], I32)

        ident_f = cst[:, 0:P]
        xs_dram = nc.dram_tensor("xs_dram", [SLOTS * P, E], F32).ap()
        ys_dram = nc.dram_tensor("ys_dram", [SLOTS * P, E], F32).ap()

        ps_s = ctx.enter_context(nc.psum_tensor("ps_s", [P, 2, 1024], F32))
        ps_a = ctx.enter_context(nc.psum_tensor("ps_a", [P, 2, 512], F32))
        ps_o = ctx.enter_context(nc.psum_tensor("ps_o", [P, 512], F32))
        ps_m = ctx.enter_context(nc.psum_tensor("ps_m", [P, 512], F32))
        ps_t = ps_s[:, :, :].rearrange("p a n -> p (a n)")

        in_x, in_w, in_c = sem("in_x"), sem("in_w"), sem("in_c")
        in_m = [sem(f"in_m{i}") for i in range(4)]
        dve_own, act_own, pool_own = sem("dve_own"), sem("act_own"), sem("pool_own")
        const_ready = sem("const_ready")
        diff_ready, max_steps = sem("diff_ready"), sem("max_steps")
        ln_var = sem("ln_var")
        ln_std = sem("ln_std")
        xn_ready = sem("xn_ready")
        xt_full, xt_taken = sem("xt_full"), sem("xt_taken")
        q_proj, q_taken = sem("q_proj"), sem("q_taken")
        nz_ready = sem("nz_ready")
        counts_ready = sem("counts_ready")
        any_ready = sem("any_ready")
        neg_ready = sem("neg_ready")
        neg_col_ready = sem("neg_col_ready")
        q_slots_ready = sem("q_slots_ready")
        q_stacked = sem("q_stacked")
        tiles_ready = sem("tiles_ready")
        edges_set, v_ones, mask_set = sem("edges_set"), sem("v_ones"), sem("mask_set")
        line_in, row_ready = sem("line_in"), sem("row_ready")
        cross_own = sem("cross_own")
        kept, minus_ready, state_ready = sem("kept"), sem("minus_ready"), sem("state_ready")
        ctx_in_of, rows_set = [sem("ctx_in0"), sem("ctx_in1")], [sem("rows_set0"), sem("rows_set1")]
        masks_in = sem("masks_in")
        masks_ready = sem("masks_ready")
        ctx_in = sem("ctx_in")
        misc_full, misc_taken = sem("misc_full"), sem("misc_taken")
        k_act, k_pool = sem("k_act"), sem("k_pool")
        k_low, k_high = sem("k_low"), sem("k_high")
        a_scores, a_max = sem("a_scores"), sem("a_max")
        scores, exps, pvs = sem("scores"), sem("exps"), sem("pvs")
        o_free = sem("o_free")
        max_own = sem("max_own")
        mrow_in = sem("mrow_in")
        f_ready = sem("f_ready")
        sums_out = sem("sums_out")
        normed, att_in, att_full, x1_ready = sem("normed"), sem("att_in"), sem("att_full"), sem("x1_ready")
        out_done = sem("out_done")
        in_late, zero_ready, xs_zeroed = sem("in_late"), sem("zero_ready"), sem("xs_zeroed")
        rot_full, swapped, cos_done = sem("rot_full"), sem("swapped"), sem("cos_done")
        sin_done, rotated, rest_done = sem("sin_done"), sem("rotated"), sem("rest_done")
        parts_act, parts_pool = sem("parts_act"), sem("parts_pool")
        stacked = [sem("stacked0"), sem("stacked1")]
        v_full, v_taken = sem("v_full"), sem("v_taken")
        self_scores, self_max = sem("self_scores"), sem("self_max")
        parts_ready, rows_full, rows_taken, rows_in_place = (
            sem("parts_ready"), sem("rows_full"), sem("rows_taken"), sem("rows_in_place"))
        t_scores, t_exps, t_pvs = sem("t_scores"), sem("t_exps"), sem("t_pvs")
        t_out = sem("t_out")
        self_normed, att2_full, x2_ready = sem("self_normed"), sem("att2_full"), sem("x2_ready")
        gate_full, hot_ready, ranks_full = sem("gate_full"), sem("hot_ready"), sem("ranks_full")
        runs_ready, slots_ready, scattered, xs_loaded = (
            sem("runs_ready"), sem("slots_ready"), sem("scattered"), sem("xs_loaded"))
        xs_full, xs_taken = sem("xs_full"), sem("xs_taken")
        w_in = [sem(f"w_in{e}") for e in range(NE)]
        b2_in = sem("b2_in")
        h_full, h_ready, y_full, y_taken = sem("h_full"), sem("h_ready"), sem("y_full"), sem("y_taken")
        ys_stored, x3_ready = sem("ys_stored"), sem("x3_ready")
        gathered = [sem(f"gathered{t}") for t in range(NT)]

        PV0 = 2 * STEPS

        def cross_attention(eng, quick, stage, before=None, start=None, end=None):
            eng.wait_ge(tiles_ready, 1)
            n = eng.value_load(tiles_i[0:1, TK:TK + 1], min_val=0, max_val=TK // CH)
            with eng.If(n < 1):
                for s in range(NU + 2):
                    quick(s)
            with eng.If(n > 0):
                if before:
                    before()
                with eng.Fori(0, n) as c:
                    if start:
                        start(c)
                    for s in (0, 1):
                        stage(c, s, s)
                    with eng.Fori(1, NB) as b:
                        for k in (0, 1):
                            stage(c, b * 2 + k, k)
                    for s in (NU, NU + 1):
                        stage(c, s, s)
                if end:
                    end(n)

        def quick_tickets(s):
            b_on, a_on, k_on, par, _ = parts(s, s)
            v = tickets_before(s)
            last = v + (2 if a_on else 0)
            k = last + (1 if b_on else 0)
            return v, last, k, k + (2 if k_on else 0)

        def expert_tiles(eng, step):
            eng.wait_ge(runs_ready, 2)
            for e in range(NE):
                end = eng.value_load(runs_i[0:1, e:e + 1], min_val=1, max_val=SLOTS)
                first = eng.value_load(runs_i[0:1, NE + e:NE + e + 1], min_val=0, max_val=SLOTS - 1)
                with eng.Fori(first, end) as j:
                    step(e, j)

        def parts(s, k):
            if isinstance(s, int):
                return s >= 2, 1 <= s <= 8, s <= 7, s % 2, s // 2
            return True, True, True, k, None

        block = ctx.enter_context(nc.Block())

        @block.sync
        def _(sp):
            sp.dma_start(x_sb[:, :, :], x.rearrange("b (t p) d -> p (b t) d", p=P)).then_inc(in_x, 16)
            sp.dma_start(cst[:, :], consts).then_inc(in_c, 16)
            sp.dma_start(bias_sb[:, :], biases).then_inc(in_w, 16)
            sp.dma_start(rows_bc[:, :], rows_in[0, :].partition_broadcast(P)).then_inc(in_w, 16)
            sp.dma_start(w_sb[:, :, :, :], w_l).then_inc(in_w, 16)
            for i in range(4):
                sp.dma_start(mask_all[:, CH * i:CH * i + CH, :],
                             mask_l[CH * i:CH * i + CH, :, 0:SQ].rearrange("t p q -> p t q")).then_inc(in_m[i], 16)
            sp.dma_start(wo_sb[:, :, :, :], wo_pad).then_inc(in_late, 16)
            sp.dma_start(w_qkv[:, :, :], w_qkv_l).then_inc(in_late, 16)
            sp.dma_start(rope[:, :, :], rope_in).then_inc(in_late, 16)
            sp.dma_start(causal[:, :, :, :], causal_in).then_inc(in_late, 16)
            sp.dma_start(gate_sb[:, :, :], gate_l).then_inc(in_late, 16)
            sp.dma_start(b1_sb[:, :, :], b1_l).then_inc(in_late, 16)
            q_edge = q_stack.rearrange("p h u q -> p (h u q)")[PAIR:ROWS]
            k_edge = k_stack.rearrange("p a h n -> p (a h n)")[PAIR:ROWS]
            sp.dma_start(q_edge, edges_in[1]).then_inc(edges_set, 16)
            sp.wait_ge(nz_ready, TK)
            sp.dma_start(k_edge, edges_in[0]).then_inc(edges_set, 16)

            def stack_q():
                sp.wait_ge(q_slots_ready, 4)
                for hh in range(HU):
                    rows = slice(16 * hh, 16 * hh + 16)
                    sp.dma_start(q_stack[0:48, hh, :, :],
                                 q_slots[rows, 0:1, :].to_broadcast([16, 3, 2048])).then_inc(q_stacked, 16)
                    sp.dma_start(q_stack[48:96, hh, :, :], q_slots[rows, 1:4, :]).then_inc(q_stacked, 16)

            def clear(i):
                dst = (xs_dram, ys_dram)[i % 2][3 * (i // 2) * P:3 * (i // 2) * P + 3 * P]
                sp.wait_ge(zero_ready, 1)
                sp.dma_start(dst.rearrange("(s p) n -> p s n", p=P),
                             zeros[:, :].unsqueeze(1).to_broadcast([P, 3, E])).then_inc(xs_zeroed, 16)

            def load_ctx(b):
                tiles = [sp.value_load(tiles_i[0:1, j:j + 1], min_val=0, max_val=TK) for j in range(CH)]
                for j, t in enumerate(tiles):
                    src = ctx_l[bass.ds(t, 1), :, KE * P * b:KE * P * b + KE * P]
                    sp.dma_start(ctx_of[b % 2][:, j, :, :], src.rearrange("a p n -> p (a n)").rearrange(
                        "p (k n) -> p k n", k=KE)).then_inc(ctx_in_of[b % 2], 16)

            def quick(s):
                b_on, a_on, k_on, par, _ = parts(s, s)
                v_at, last_at, k_at, first_at = quick_tickets(s)
                if s == 0:
                    load_ctx(0)
                    sp.wait_ge(q_proj, 4)
                    for j in range(CH):
                        t = sp.value_load(tiles_i[0:1, j:j + 1], min_val=0, max_val=TK)
                        sp.dma_start(mask_line[:, P * j:P * j + P], mask_l[bass.ds(t, 1), 0:1, SQ:SQ + P].rearrange(
                            "a p n -> p (a n)")).then_inc(line_in, 16)
                    load_ctx(1)
                    sp.wait_ge(row_ready, 1)
                    sp.wait_ge(edges_set, 32)
                    sp.dma_start(k_stack.rearrange("p a h n -> p (a h) n")[PAIR:PAIR + 1],
                                 mask_row.unsqueeze(1).to_broadcast([1, 2 * HU, CH * P])).then_inc(mask_set, 16)
                    stack_q()
                elif s % 2 == 0 and s + 2 < NU:
                    sp.wait_ge(misc_full, v_at + 2)
                    load_ctx(s // 2 + 1)
                if b_on:
                    sp.wait_ge(misc_taken, last_at + 2)
                    rows_of_maxima(s - 2, 1)
                if k_on:
                    sp.wait_ge(k_act, 3 * s + 3)
                    sp.wait_ge(k_pool, 2 * s + 2)
                    sp.wait_ge(pvs, s * STEPS + CH)
                    for hh in range(4):
                        stack_k(par, hh, k_low)
                if a_on:
                    sp.wait_ge(misc_taken, first_at + 2)
                    rows_of_maxima(s - 1, 0)
                if k_on:
                    sp.wait_ge(pvs, s * STEPS + STEPS)
                    for hh in range(4, HU):
                        stack_k(par, hh, k_high)
                if 2 <= s < 7:
                    clear(2 * s - 4)
                    clear(2 * s - 3)

            def rows_of_maxima(u, g):
                at = u % 2 * NB + u // 2
                for qt in range(2):
                    sp.dma_start(q_stack[PAIR + 1:ROWS, 4 * g:4 * g + 4, at, P * qt:P * qt + P],
                                 quick_rows[12 * qt:12 * qt + 12, g, :]).then_inc(rows_set[g], 16)

            def stack_k(par, hh, done):
                rows = slice(16 * hh, 16 * hh + 16)
                sp.dma_start(k_stack[0:48, par, hh, :], k_slots[rows, 0:3, :]).then_inc(done, 16)
                sp.dma_start(k_stack[48:96, par, hh, :], k_slots[rows, 1:4, :]).then_inc(done, 16)

            def start(c):
                tiles = [sp.value_load(tiles_i[0:1, bass.ds(c * CH + j, 1)], min_val=0, max_val=TK)
                         for j in range(CH)]
                sp.wait_ge(masks_ready, c * 3 + 1)
                for j, t in enumerate(tiles):
                    sp.dma_start(mask_in[:, j, :], mask_l[bass.ds(t, 1), :, :].rearrange("a p q -> p (a q)")
                                 ).then_inc(masks_in, 16)

            def stage(c, s, k):
                b_on, a_on, k_on, par, _ = parts(s, k)
                cs = c * NU + s
                tk = c * (TICKETS * NU) + tickets_before(s)
                if k_on and par == 0:
                    tiles = [sp.value_load(tiles_i[0:1, bass.ds(c * CH + j, 1)], min_val=0, max_val=TK)
                             for j in range(CH)]
                    sp.wait_ge(misc_full, tk + (3 if a_on else 1))
                    for j, t in enumerate(tiles):
                        src = ctx_l[bass.ds(t, 1), :, bass.ds(s * (KE * P // 2), KE * P)]
                        sp.dma_start(ctx_sb[:, j, :, :], src.rearrange("a p n -> p (a n)").rearrange(
                            "p (k n) -> p k n", k=KE)).then_inc(ctx_in, 16)
                if k_on:
                    sp.wait_ge(k_act, cs * 3 + 3)
                    sp.wait_ge(k_pool, cs * 2 + 3)

                if k_on:
                    sp.wait_ge(pvs, cs * STEPS + CH)
                    for hh in range(4):
                        stack_k(par, hh, k_low)
                if a_on:
                    n = tk + (2 if a_on else 0) + (2 if k_on else 0) + 1
                    sp.wait_ge(misc_taken, n + 1)
                    u_at = (s - 1) % 2 * 4 + (s - 1) // 2 if isinstance(s, int) else None
                    if u_at is None:
                        u_at = s // 2 + (NB - 1) if k == 0 else (s - 1) // 2
                    for qt in range(2):
                        sp.dma_start(q_stack[PAIR + 1:ROWS, :, bass.ds(u_at, 1), P * qt:P * qt + P].rearrange(
                            "p h u q -> p h (u q)"), m_rows[24 * qt:24 * qt + 24, :]).then_inc(mrow_in, 16)
                if k_on:
                    sp.wait_ge(pvs, cs * STEPS + STEPS)
                    for hh in range(4, HU):
                        stack_k(par, hh, k_high)

            def before():
                sp.wait_ge(q_proj, 4)
                stack_q()
                for i in range(2 * SLOTS // 3):
                    clear(i)

            cross_attention(sp, quick, stage, before, start)
            for i in range(4):
                half, t = i // 2, i % 2
                sp.wait_ge(parts_act, 3 * i + 3)
                sp.wait_ge(parts_pool, i + 1)
                if i == 0:
                    sp.wait_ge(normed, NU)
                    sp.dma_start(k_edge, edges_in[0]).then_inc(stacked[0], 16)
                for hh in range(HU):
                    rows = slice(16 * hh, 16 * hh + 16)
                    if t == 0:
                        dst = q_stack[:, hh, NB * half:NB * half + NB, :].rearrange("p u q -> p (u q)")
                        sp.dma_start(dst[0:48], r_slots[0][rows, 0:1, :].to_broadcast([16, 3, 1024])
                                     ).then_inc(stacked[half], 16)
                        sp.dma_start(dst[48:96], r_slots[0][rows, 1:4, :]).then_inc(stacked[half], 16)
                    else:
                        dst = k_stack[:, half, hh, :]
                        sp.dma_start(dst[0:48], r_slots[1][rows, 0:3, :]).then_inc(stacked[half], 16)
                        sp.dma_start(dst[48:96], r_slots[1][rows, 1:4, :]).then_inc(stacked[half], 16)
            for u in range(NU):
                sp.wait_ge(rows_taken, u + 1)
                for qt in range(2):
                    sp.dma_start(q_stack[PAIR + 1:ROWS, :, u, P * qt:P * qt + P], m_rows[24 * qt:24 * qt + 24, :]
                                 ).then_inc(rows_in_place, 16)
            sp.wait_ge(self_normed, NU)
            sp.wait_ge(xs_zeroed, 32 * SLOTS // 3)
            for e in (0, 1, 2, 3, 4, 5, 7, 6):
                if e == 6:
                    sp.wait_ge(x2_ready, NB)
                sp.dma_start(w1_sb[e], w1[e].rearrange("(k p) f -> p k f", p=P)).then_inc(w_in[e], 16)
                sp.dma_start(w2_sb[e], w2[e].rearrange("(c p) n -> p c n", p=P)).then_inc(w_in[e], 16)
            sp.dma_start(b2_bc.rearrange("p e n -> p (e n)"), b2.rearrange("e n -> (e n)").partition_broadcast(P)
                         ).then_inc(b2_in, 16)
            sp.wait_ge(scattered, 16 * NT)
            sp.dma_start(xs_in, xs_dram.rearrange("(s p) n -> p s n", p=P)).then_inc(xs_loaded, 16)

            def store(e, j):
                sp.wait_ge(y_taken, j + 2)
                sp.dma_start(ys_dram[bass.ds(j * P, P), :], y_all[:, bass.ds(j, 1), :].rearrange("p a n -> p (a n)")
                             ).then_inc(ys_stored, 16)

            expert_tiles(sp, store)
            for t in range(NT):
                sp.wait_ge(x3_ready, t + 1)
                sp.dma_start(out.rearrange("b (t p) d -> (b t) p d", p=P)[t], x_sb[:, t, :]).then_inc(out_done, 16)
            sp.wait_ge(out_done, 16 * NT)

        @block.vector
        def _(dve):
            own = Chain(dve, dve_own)
            own.add(dve.memset(eps_sb[:, :], EPS))
            own.add(dve.memset(ones_b[:, :], 1.0))
            own.wait()
            dve.wait_ge(in_c, 16)
            own.add(dve.tensor_copy(lower_b[:, :], cst[:, 2 * P:3 * P]))
            own.wait()
            dve.tensor_copy(ident_b[:, :], ident_f).then_inc(const_ready, 1)

            def layernorm(src, dst):
                own.wait()
                for t in range(NT):
                    own.add(dve.bn_stats(ln_stat[:, t, :], src[:, t, :]))
                own.wait()
                for t in range(NT):
                    ins = dve.bn_aggr(ln_mv[:, t, :], ln_stat[:, t, :])
                    own.add(ins)
                own.wait()
                own.add(dve.tensor_copy(ln_r[:, :], ln_mv[:, :, 1]))
                own.wait()
                dve.tensor_scalar(ln_r[:, :], ln_r[:, :], 1.0, None, ALU.mult).then_inc(ln_var, 1)

            def layernorm_end(src, dst, n):
                dve.wait_ge(ln_std, n)
                own.add(dve.reciprocal(ln_r[:, :], ln_r[:, :]))
                own.wait()
                for t in range(NT):
                    dve.tensor_scalar(dst[:, t, :], src[:, t, :], ln_mv[:, t, 0:1], ln_r[:, t:t + 1],
                                      ALU.subtract, ALU.mult).then_inc(xn_ready, 1)

            dve.wait_ge(in_x, 16)
            layernorm(x_sb, xn)
            layernorm_end(x_sb, xn, 1)
            for t in range(TK):
                if t % CH == 0:
                    dve.wait_ge(in_m[t // CH], 16)
                dve.tensor_scalar(mask_nz[:, t, :], mask_all[:, t, :], 0.0, 0.0, ALU.not_equal, ALU.add,
                                  accum_out=tile_any[:, t:t + 1]).then_inc(nz_ready, 1)
            dve.wait_ge(nz_ready, TK)
            own.add(dve.tensor_scalar(tile_mixed[:, :], tile_any[:, :], float(SQ), None, ALU.is_lt))
            own.wait()
            dve.scalar_tensor_tensor(tile_any_b[:, TK:2 * TK], tile_any[:, :], 0.0, tile_mixed[:, :],
                                     ALU.is_gt, ALU.mult).then_inc(any_ready, 1)
            dve.tensor_scalar(tile_any_b[:, 0:TK], tile_any[:, :], 0.0, None, ALU.is_gt).then_inc(any_ready, 1)
            dve.wait_ge(counts_ready, 1)
            own.add(dve.tensor_scalar(row_dead[:, :], ps_m[:, 0:SQ], 0.0, None, ALU.is_equal))
            own.add(dve.tensor_scalar(q_scale[:, :], ps_m[:, 0:SQ], 0.0, D ** -0.5, ALU.is_gt, ALU.mult))
            dve.tensor_scalar(neg_big[:, :], ps_m[:, 0:SQ], 0.0, -BIG, ALU.is_gt, ALU.mult).then_inc(neg_ready, 1)
            own.wait()
            own.add(dve.tensor_reduce(cmp[:, 0:1], row_dead[0:1, :], AX.X, ALU.max))
            own.wait()
            own.add(dve.tensor_scalar(cmp[:, 32:64], ps_m[0:1, SQ:SQ + TK], 0.0, cmp[:, 0:1], ALU.is_gt, ALU.max))
            own.wait()
            own.add(dve.memset(cmp[:, 64:96], 1.0))
            own.wait()
            own.add(dve.tensor_tensor_scan(cmp[:, 96:128], cmp[:, 64:96], cmp[:, 32:64], 0.0, ALU.mult, ALU.add))
            own.wait()
            own.add(dve.tensor_tensor(cmp[:, 128:160], cmp[:, 96:128], cmp[:, 32:64], ALU.mult))
            own.wait()
            own.add(dve.tensor_scalar(cmp[:, 128:160], cmp[:, 128:160], -1.0, None, ALU.add))
            own.wait()
            row = lambda a: a.unsqueeze(1).to_broadcast([1, TK, TK])
            col = lambda a: a.unsqueeze(2).to_broadcast([1, TK, TK])
            own.add(dve.tensor_tensor(pick[:, :, :], row(cmp[:, 128:160]), col(cst[0:1, P:P + TK]), ALU.is_equal))
            own.wait()
            own.add(dve.tensor_tensor(pick[:, :, :], pick[:, :, :], row(cst[0:1, P:P + TK]), ALU.mult))
            own.wait()
            own.add(dve.tensor_reduce(cmp[:, 160:192], pick[:, :, :], AX.X, ALU.add))
            own.add(dve.tensor_scalar(cmp[:, 192:224], cst[0:1, P:P + TK], cmp[:, 127:128], float(TK),
                                      ALU.is_ge, ALU.mult))
            own.wait()
            own.add(dve.tensor_tensor(tiles_i[:, 0:TK], cmp[:, 160:192], cmp[:, 192:224], ALU.add))
            own.add(dve.tensor_scalar(cmp[:, 224:224 + TK // CH], cst[0:1, P:P + TK:CH], cmp[:, 127:128], None,
                                      ALU.is_lt))
            own.wait()
            own.add(dve.tensor_reduce(cmp[:, 1:2], cmp[:, 224:224 + TK // CH], AX.X, ALU.add))
            own.add(dve.tensor_reduce(cmp[:, 2:3], ps_m[0:1, SQ + TK:SQ + 2 * TK], AX.X, ALU.max))
            own.wait()
            own.add(dve.tensor_scalar(cmp[:, 3:4], cmp[:, 1:2], 1.0, None, ALU.is_equal))
            own.wait()
            own.add(dve.scalar_tensor_tensor(cmp[:, 4:5], cmp[:, 2:3], 0.0, cmp[:, 3:4], ALU.is_equal, ALU.mult))
            own.wait()
            dve.tensor_tensor(tiles_i[:, TK:TK + 1], cmp[:, 1:2], cmp[:, 4:5], ALU.subtract).then_inc(tiles_ready, 1)

            def split_q(own):
                dve.wait_ge(q_taken, 4)
                own.add(dve.tensor_tensor(
                    q_full.rearrange("p (u q) -> p u q", u=NU), q_full.rearrange("p (u q) -> p u q", u=NU),
                    q_scale[:, :].unsqueeze(1).to_broadcast([P, NU, SQ]), ALU.mult))
                own.wait()
                dve.tensor_copy(q_slots[:, 0, :], q_full).then_inc(q_slots_ready, 1)
                dve.wait_ge(q_slots_ready, 1)
                own.add(dve.tensor_tensor(q_rest, q_full, q_slots[:, 0, :], ALU.subtract))
                own.wait()
                dve.tensor_copy(q_slots[:, 1, :], q_rest).then_inc(q_slots_ready, 1)
                dve.tensor_copy(q_slots[:, 2, :], q_rest).then_inc(q_slots_ready, 1)
                dve.wait_ge(q_slots_ready, 3)
                dve.tensor_tensor(q_slots[:, 3, :], q_rest, q_slots[:, 1, :], ALU.subtract).then_inc(q_slots_ready, 1)

            step = Chain(dve, cross_own)

            def invert(u, part):
                at = sums[:, u % 2, P * part:P * part + P]
                dve.reciprocal(at, at).then_inc(sums_out, 1)

            def quick(s):
                b_on, a_on, k_on, par, _ = parts(s, s)
                v_at, last_at, k_at, first_at = quick_tickets(s)
                w = s - 1
                if s == 0:
                    dve.wait_ge(line_in, 16 * CH)
                    dve.tensor_scalar(mask_row, mask_line, 0.0, -BIG, ALU.is_equal, ALU.mult).then_inc(row_ready, 1)
                    split_q(step)

                def minus(g):
                    dve.wait_ge(a_max, 32 * w + 16 * g + 18)
                    step.wait()
                    top, neg, rest = (m_quick[:, i, g, :] for i in range(3))
                    step.add(dve.tensor_reduce(top, m_half[:, 16 * g:16 * g + 16].rearrange("p (n c) -> p n c", c=2),
                                               AX.X, ALU.max))
                    step.wait()
                    split = lambda a: a.rearrange("p (t h) -> p t h", t=2)
                    step.add(dve.tensor_scalar(neg, top, -1.0, None, ALU.mult))
                    step.add(dve.tensor_scalar(q_parts[:, g, :, 0, :], split(top), -1.0, None, ALU.mult))
                    step.wait()
                    step.add(dve.tensor_tensor(split(rest), split(neg), q_parts[:, g, :, 0, :], ALU.subtract))
                    step.wait()
                    step.add(dve.tensor_copy(q_parts[:, g, :, 1, :], split(rest)))
                    step.wait()
                    dve.tensor_tensor(q_parts[:, g, :, 2, :], split(rest), q_parts[:, g, :, 1, :], ALU.subtract
                                      ).then_inc(minus_ready, 1)

                def take_rows(u, g, ticket):
                    dve.wait_ge(misc_full, ticket + 1)
                    if u:
                        dve.wait_ge(rows_set[g], 32 * u)
                    dve.tensor_copy(quick_rows[:, g, :], ps_m[0:24, 0:P]).then_inc(misc_taken, 1)

                for i in range(STEPS):
                    if a_on:
                        hh, qt = i // 2, i % 2
                        for c2 in range(2):
                            xx = 2 * i + c2
                            dve.wait_ge(a_scores, 32 * w + xx + 1)
                            if xx == 0:
                                step.wait()
                            at = 16 * (hh // 4) + 8 * qt + 2 * (hh % 4) + c2
                            dve.tensor_reduce(m_half[:, at:at + 1], ps_a[:, c2, :], AX.X, ALU.max).then_inc(a_max, 1)
                    if b_on and i == 2:
                        take_rows(s - 2, 1, last_at)
                    if s >= 3 and 3 <= i < 7:
                        invert(s - 3, i - 3)
                    if a_on and i == 7:
                        minus(0)
                    if a_on and i == 10:
                        take_rows(w, 0, first_at)
                    if a_on and i == 15:
                        minus(1)
                if b_on:
                    dve.wait_ge(pvs, (s - 2) * STEPS + PV0 + STEPS)
                    if s >= 4:
                        dve.wait_ge(normed, s - 3)
                    dve.stream_shuffle(sums[:, s % 2, :], ps_o[:, :], [D] * 32).then_inc(kept, 1)
                    dve.tensor_copy(o_acc[:, s - 2, :], ps_o[:, :]).then_inc(o_free, 1)
                    dve.wait_ge(kept, s - 1)
                if s == NU + 1:
                    for i in range(4):
                        invert(NU - 1, i)
            def before():
                own = Chain(dve, cross_own)
                split_q(own)
                own.add(dve.memset(m_run[:, :, :], -2 * BIG))
                dve.wait_ge(q_stacked, 16 * 2 * HU)
                own.add(dve.memset(o_acc[:, :, :], 0.0))
                own.wait()
                dve.wait_ge(neg_col_ready, 1)
                dve.tensor_copy(neg_big_col[:, :], ps_m[:, 0:2]).then_inc(state_ready, 1)

            def start(c):
                dve.wait_ge(masks_in, c * (16 * CH) + 16 * CH)
                dve.wait_ge(pvs, c * (STEPS * NU) + PV0)
                dve.wait_ge(a_max, c * (32 * NU) + 2)
                dve.wait_ge(state_ready, 1)
                dve.scalar_tensor_tensor(bias_kq[:, :, :], mask_in[:, :, 0:SQ], 0.0,
                                         neg_big[:, :].unsqueeze(1).to_broadcast([P, CH, SQ]),
                                         ALU.is_equal, ALU.mult).then_inc(masks_ready, 1)
                for qt in range(2):
                    dve.tensor_scalar(bias_qk[:, qt, :].rearrange("p (j n) -> p j n", j=CH),
                                      mask_in[:, :, SQ + P * qt:SQ + P * qt + P], 0.0, neg_big_col[:, qt:qt + 1],
                                      ALU.is_equal, ALU.mult).then_inc(masks_ready, 1)

            def stage(c, s, k):
                b_on, a_on, k_on, par, _ = parts(s, k)
                cs = c * NU + s
                tk = c * (TICKETS * NU) + tickets_before(s)
                if a_on:
                    w = cs - 1
                    run = m_run[:, bass.ds(s - 1, 1), :].rearrange("p a n -> p (a n)")
                    mo = w * 7
                    if (isinstance(s, int) and s == 1):
                        dve.wait_ge(masks_ready, c * 3 + 4)
                    dve.wait_ge(f_ready, w + 1)
                    dve.wait_ge(a_max, w * 32 + 2)
                    dve.tensor_copy(m_old[:, :], run).then_inc(max_own, 1)
                    for xx in range(32):
                        hh, c2, qt = xx // 4, xx // 2 % 2, xx % 2
                        col = slice(HU * qt + hh, HU * qt + hh + 1)
                        dve.wait_ge(a_scores, w * 32 + xx + 1)
                        dve.wait_ge(a_max, w * 32 + xx + 1)
                        if xx == 0:
                            dve.wait_ge(max_own, mo + 1)
                        bias = bias_qk[:, qt, 512 * c2:512 * c2 + 512]
                        older = (m_cur if c2 else m_old)[:, col]
                        m3 = w * 64 + 2 * xx
                        dve.wait_ge(a_max, w * 32 + xx + 2)
                        dve.tensor_tensor(masked[:, :], ps_a[:, xx % 2, :], bias, ALU.add).then_inc(max_steps, 1)
                        dve.wait_ge(max_steps, m3 + 1)
                        dve.tensor_reduce(m_tile[:, :], masked[:, :], AX.X, ALU.max).then_inc(max_steps, 1)
                        dve.wait_ge(max_steps, m3 + 2)
                        dve.tensor_tensor(m_cur[:, col], m_tile[:, :], older, ALU.max).then_inc(a_max, 1)
                    dve.wait_ge(a_max, w * 32 + 34)
                    by_qt = lambda a: a.rearrange("p (t h) -> p t h", t=2)
                    dve.tensor_scalar(m_neg[:, 0, :], m_cur[:, :], -1.0, None, ALU.mult).then_inc(max_own, 1)
                    dve.tensor_scalar(m_parts[:, :, 0, :], by_qt(m_cur[:, :]), -1.0, None, ALU.mult
                                      ).then_inc(max_own, 1)
                    dve.tensor_copy(run, m_cur[:, :]).then_inc(max_own, 1)
                    dve.wait_ge(max_own, mo + 3)
                    dve.tensor_tensor(by_qt(m_neg[:, 1, :]), by_qt(m_neg[:, 0, :]), m_parts[:, :, 0, :],
                                      ALU.subtract).then_inc(max_own, 1)
                    dve.wait_ge(max_own, mo + 5)
                    dve.tensor_copy(m_parts[:, :, 1, :], by_qt(m_neg[:, 1, :])).then_inc(max_own, 1)
                    dve.wait_ge(max_own, mo + 6)
                    dve.tensor_tensor(m_parts[:, :, 2, :], by_qt(m_neg[:, 1, :]), m_parts[:, :, 1, :], ALU.subtract
                                      ).then_inc(max_own, 1)
                    dve.tensor_tensor(m_diff[:, :].rearrange("p (g t h) -> p g t h", g=2, t=2),
                                      m_old[:, :].rearrange("p (t g h) -> p g t h", g=2, t=2),
                                      m_cur[:, :].rearrange("p (t g h) -> p g t h", g=2, t=2),
                                      ALU.subtract).then_inc(diff_ready, 1)
                    n = tk + 2 + (2 if k_on else 0)
                    dve.wait_ge(misc_full, n + 2)
                    dve.wait_ge(mrow_in, w * 32 + 1)
                    dve.tensor_copy(m_rows[:, :], ps_m[0:48, 0:P]).then_inc(misc_taken, 1)
                if b_on:
                    w = cs - 2
                    acc = o_acc[:, bass.ds(s - 2, 1), :].rearrange("p a n -> p (a n)")
                    n = tk + (2 + 1 if a_on else 0) + (2 if k_on else 0)
                    dve.wait_ge(misc_full, n + 2)
                    dve.tensor_tensor(acc, acc, ps_m[:, :], ALU.mult).then_inc(misc_taken, 1)
                    dve.wait_ge(pvs, w * STEPS + PV0 + STEPS)
                    dve.wait_ge(misc_taken, n + 2)
                    dve.tensor_tensor(acc, acc, ps_o[:, :], ALU.add).then_inc(o_free, 1)

            def end(n):
                dve.wait_ge(o_free, n * NU + 1)
                dve.memset(junk[:, 0, 0:1], 0.0).then_inc(kept, 1)
                dve.wait_ge(kept, 1)
                for u in range(NU):
                    if u >= 2:
                        dve.wait_ge(normed, u - 1)
                    dve.stream_shuffle(sums[:, u % 2, :], o_acc[:, u, :], [D] * 32).then_inc(kept, 1)
                    dve.wait_ge(kept, u + 2)
                    for i in range(4):
                        invert(u, i)

            cross_attention(dve, quick, stage, before, start, end)
            for b in range(NB):
                dve.wait_ge(att_full, b + 1)
                dve.wait_ge(pool_own, 1)
                dve.tensor_tensor(x_sb[:, 2 * b:2 * b + 2, :], x_sb[:, 2 * b:2 * b + 2, :],
                                  ps_s[:, b % 2, 0:512].rearrange("p (t n) -> p t n", t=2), ALU.add).then_inc(x1_ready, 1)

            dve.wait_ge(x1_ready, NB)
            layernorm(x_sb, xn)
            layernorm_end(x_sb, xn, 2)
            for i in range(4):
                t = i % 2
                ps = ps_s[:, i % 2, :]
                dve.wait_ge(rot_full, i + 1)
                if i >= 2:
                    dve.wait_ge(parts_act, 3 * (i - 2) + 3)
                    dve.wait_ge(parts_pool, i - 1)
                elif i == 0:
                    dve.wait_ge(in_late, 96)
                    dve.wait_ge(att_full, NB)
                dve.stream_shuffle(r_swap[t], ps, [c ^ 1 for c in range(32)]).then_inc(swapped, 1)
                dve.tensor_tensor(r_full[t].rearrange("p (b q) -> p b q", b=NB), ps.rearrange("p (b q) -> p b q", b=NB),
                                  rope[:, 2 * t, :].unsqueeze(1).to_broadcast([P, NB, SQ]), ALU.mult
                                  ).then_inc(cos_done, 1)
                dve.wait_ge(cos_done, i + 1)
                dve.wait_ge(sin_done, i + 1)
                dve.tensor_tensor(r_full[t], r_full[t], r_swap[t], ALU.add).then_inc(rotated, 1)
                dve.wait_ge(parts_act, 3 * i + (1 if t == 0 else 2))
                dve.wait_ge(rotated, i + 1)
                dve.tensor_tensor(r_rest[t], r_full[t], r_slots[t][:, t, :], ALU.subtract).then_inc(rest_done, 1)

            def self_out(u):
                dve.wait_ge(t_pvs, 4 * u + 4)
                dve.wait_ge(parts_pool, 4)
                if u >= 2:
                    dve.wait_ge(self_normed, u - 1)
                own.add(dve.stream_shuffle(t_sums[:, u % 2, :], ps_o[:, :], [D] * 32))
                dve.tensor_copy(o_acc[:, u, :], ps_o[:, :]).then_inc(t_out, 1)
                own.wait()
                dve.reciprocal(t_sums[:, u % 2, :], t_sums[:, u % 2, :]).then_inc(t_out, 1)

            by_qt = lambda a: a.rearrange("p (t h) -> p t h", t=2)
            for u in range(NU):
                for y in range(8):
                    hp, qt = y // 2, y % 2
                    dve.wait_ge(self_scores, 8 * u + y + 1)
                    if y == 0 and u:
                        own.wait()
                    dve.tensor_reduce(m_cur[:, HU * qt + 2 * hp:HU * qt + 2 * hp + 2],
                                      ps_a[:, y % 2, :].rearrange("p (h k) -> p h k", h=2), AX.X, ALU.max
                                      ).then_inc(self_max, 1)
                dve.wait_ge(self_max, 8 * u + 8)
                own.add(dve.tensor_scalar(m_neg[:, 0, :], m_cur[:, :], -1.0, None, ALU.mult))
                if u:
                    dve.wait_ge(rows_full, u)
                own.add(dve.tensor_scalar(m_parts[:, :, 0, :], by_qt(m_cur[:, :]), -1.0, None, ALU.mult))
                own.wait()
                own.add(dve.tensor_tensor(by_qt(m_neg[:, 1, :]), by_qt(m_neg[:, 0, :]), m_parts[:, :, 0, :],
                                          ALU.subtract))
                own.wait()
                own.add(dve.tensor_copy(m_parts[:, :, 1, :], by_qt(m_neg[:, 1, :])))
                own.wait()
                dve.tensor_tensor(m_parts[:, :, 2, :], by_qt(m_neg[:, 1, :]), m_parts[:, :, 1, :], ALU.subtract
                                  ).then_inc(parts_ready, 1)
                dve.wait_ge(rows_full, u + 1)
                if u:
                    dve.wait_ge(rows_in_place, 32 * u)
                dve.tensor_copy(m_rows[:, :], ps_m[0:48, 0:P]).then_inc(rows_taken, 1)
                if u:
                    self_out(u - 1)
            self_out(NU - 1)
            for b in range(NB):
                dve.wait_ge(att2_full, b + 1)
                dve.wait_ge(pool_own, 2)
                dve.tensor_tensor(x_sb[:, 2 * b:2 * b + 2, :], x_sb[:, 2 * b:2 * b + 2, :],
                                  ps_s[:, b % 2, 0:512].rearrange("p (t n) -> p t n", t=2), ALU.add).then_inc(x2_ready, 1)

            dve.wait_ge(x2_ready, NB)
            layernorm(x_sb, xn)
            layernorm_end(x_sb, xn, 3)
            te = lambda k: route[:, k, :, :]
            over_t = lambda a: a.unsqueeze(1).to_broadcast([P, NT, NE])
            over_e = lambda a: a.unsqueeze(2).to_broadcast([P, NT, NE])

            def then(ins):
                own.add(ins)
                own.wait()

            dve.wait_ge(gate_full, 1)
            then(dve.tensor_tensor(te(0), ps_m[:, 0:NT * NE].rearrange("p (t e) -> p t e", t=NT),
                                   over_t(rows_bc[:, 2 * E:2 * E + NE]), ALU.add))
            then(dve.tensor_tensor(te(0), te(0), over_t(rows_bc[:, 2 * E + NE:2 * E + 2 * NE]), ALU.add))
            then(dve.tensor_reduce(route[:, 1, 0, :], te(0), AX.X, ALU.max))
            then(dve.tensor_tensor(te(2), te(0), over_e(route[:, 1, 0, :]), ALU.is_ge))
            rev = cst[:, P + 64:P + 64 + NE]
            then(dve.tensor_tensor(te(2), te(2), over_t(rev), ALU.mult))
            then(dve.tensor_reduce(route[:, 1, 1, :], te(2), AX.X, ALU.max))
            then(dve.tensor_tensor(te(3), over_t(rev), over_e(route[:, 1, 1, :]), ALU.is_equal))
            dve.tensor_copy(route_b[:, :, :], te(3)).then_inc(hot_ready, 1)
            dve.wait_ge(ranks_full, 1)
            own.add(dve.memset(route[:, 5, 0, :], 0.0))
            then(dve.tensor_copy(te(4), ps_m[:, 64:128].rearrange("p (t e) -> p t e", t=NT)))
            for t in range(1, NT):
                then(dve.tensor_tensor(route[:, 5, t, :], route[:, 5, t - 1, :], route[:, 4, t - 1, :], ALU.add))
            total, tiles, upto, base, base_row = (route[:, 6, k, :] for k in range(5))
            then(dve.tensor_tensor(total, route[:, 5, NT - 1, :], route[:, 4, NT - 1, :], ALU.add))
            more = route[:, 7, :, 0:NT - 1]
            then(dve.tensor_tensor(more, total.unsqueeze(2).to_broadcast([P, NE, NT - 1]),
                                   cst[:, P + 80:P + 80 + NT - 1].unsqueeze(1).to_broadcast([P, NE, NT - 1]), ALU.is_gt))
            then(dve.tensor_reduce(tiles, more, AX.X, ALU.add))
            own.add(dve.memset(route[:, 6, 5, :], 1.0))
            then(dve.tensor_scalar(tiles, tiles, 1.0, None, ALU.add))
            then(dve.tensor_tensor_scan(upto, route[:, 6, 5, :], tiles, 0.0, ALU.mult, ALU.add))
            then(dve.tensor_tensor(base, upto, tiles, ALU.subtract))
            dve.tensor_copy(runs_i[:, 0:NE], upto[0:1]).then_inc(runs_ready, 1)
            dve.tensor_copy(runs_i[:, NE:2 * NE], base[0:1]).then_inc(runs_ready, 1)
            then(dve.tensor_scalar(base_row, base, float(P), None, ALU.mult))
            then(dve.tensor_tensor(te(2), te(5), ps_m[:, 128:192].rearrange("p (t e) -> p t e", t=NT), ALU.add))
            then(dve.tensor_tensor(te(2), te(2), over_t(base_row), ALU.add))
            then(dve.tensor_tensor(te(2), te(2), te(3), ALU.mult))
            then(dve.tensor_reduce(route[:, 1, 2, :], te(2), AX.X, ALU.add))
            dve.tensor_copy(slot_i[:, :], route[:, 1, 2, :]).then_inc(slots_ready, 1)

            dve.wait_ge(b2_in, 16)
            dve.wait_ge(xs_taken, 8)

            def y_out(e, j):
                dve.wait_ge(y_full, j + 2)
                dve.tensor_tensor(y_all[:, bass.ds(j, 1), :].rearrange("p a n -> p (a n)"), ps_o[:, 0:E],
                                  b2_bc[:, e, :], ALU.add).then_inc(y_taken, 1)

            expert_tiles(dve, y_out)
            for t in range(NT):
                dve.wait_ge(gathered[t], 16)
                dve.tensor_tensor(x_sb[:, t, :], x_sb[:, t, :], picked[:, t, :], ALU.add).then_inc(x3_ready, 1)

        @block.scalar
        def _(act):
            act.sem_inc(exps, 2)
            act.sem_inc(misc_taken, 1)
            act.sem_inc(a_max, 2)
            act.sem_inc(pvs, PV0)
            act.sem_inc(o_free, 1)
            act.sem_inc(h_ready, F // P)
            act.sem_inc(y_taken, 1)
            act.sem_inc(y_full, 1)
            act.wait_ge(in_w, 48)

            def deviations_and_rows(n):
                act.wait_ge(ln_var, n)
                act.wait_ge(const_ready, 1)
                act.activation(ln_r[:, :], ln_r[:, :], ACT.Sqrt, bias=eps_sb[:, 0:1]).then_inc(ln_std, 1)
                for i in range(4):
                    act.wait_ge(xt_full, 4 * (n - 1) + i + 1)
                    k, half = i // 2, i % 2
                    act.copy(xn_t[:, k, 512 * half:512 * half + 512], ps_t[:, 512 * i:512 * i + 512]
                             ).then_inc(xt_taken, 1)

            deviations_and_rows(1)
            for i in range(4):
                act.wait_ge(q_proj, i + 1)
                src = [ps_a[:, 0, :], ps_a[:, 1, :], ps_o[:, :], ps_t[:, 0:512]][i]
                act.activation(q_full[:, 512 * i:512 * i + 512], src, ACT.Identity,
                               bias=bias_sb[:, i // 2:i // 2 + 1]).then_inc(q_taken, 1)

            def stage(c, s, k):
                b_on, a_on, k_on, par, _ = parts(s, k)
                cs = c * NU + s
                tk = c * (TICKETS * NU) + tickets_before(s)

                def v_out(i):
                    act.wait_ge(misc_full, tk + i + 2)
                    if i == 0:
                        act.wait_ge(pvs, cs * STEPS)
                    act.copy(v_sb[:, 1 - par, 4 * i:4 * i + 4, :, 0:D],
                             ps_m[:, :].rearrange("p (j h d) -> p j h d", j=4, h=HU)).then_inc(misc_taken, 1)

                def k_out(i):
                    act.wait_ge(misc_full, tk + (2 if a_on else 0) + i + 2)
                    act.wait_ge(k_pool, cs * 2 + 1)
                    act.activation(k_full[:, 512 * i:512 * i + 512], ps_m[:, :], ACT.Identity,
                                   bias=bias_sb[:, 2 + par:3 + par]).then_inc(misc_taken, 1)

                def k_first(slot):
                    if slot == 1:
                        act.wait_ge(misc_taken, tk + (2 if a_on else 0) + 3)
                        act.wait_ge(k_low, cs * 128 + 1)
                        act.wait_ge(k_high, cs * 128 + 1)
                    act.copy(k_slots[:, slot, :], k_full).then_inc(k_act, 1)

                def k_second():
                    act.wait_ge(k_pool, cs * 2 + 2)
                    act.copy(k_slots[:, 2, :], k_rest).then_inc(k_act, 1)

                def factor():
                    act.wait_ge(diff_ready, cs)
                    act.activation(f_bc[:, 1 - par, :, :], m_diff[:, :].unsqueeze(2).to_broadcast([P, 16, 32]),
                                   ACT.Exp).then_inc(f_ready, 1)

                for i in range(STEPS):
                    if b_on:
                        w = cs - 2
                        act.wait_ge(scores, w * STEPS + i + 1)
                        act.wait_ge(pvs, w * STEPS + PV0 + i - 1)
                        act.activation(probs[:, i % 2, :], ps_s[:, i % 2, :], ACT.Exp).then_inc(exps, 1)
                    if a_on and i < 2:
                        v_out(i)
                    if k_on and i in (6, 7):
                        k_out(i - 6)
                    if k_on and i in (8, 9):
                        k_first((1, 3)[i - 8])
                    if k_on and i == 11:
                        k_second()
                    if a_on and i == 14:
                        factor()

            def add_bv(u):
                act.wait_ge(normed, u + 1)
                for g in range(2):
                    at = o_acc[:, u, SQ * g:SQ * g + SQ]
                    act.activation(at, at, ACT.Identity, bias=bias_sb[:, 4 + u % 2 * 2 + g:5 + u % 2 * 2 + g]
                                   ).then_inc(att_in, 1)

            def quick(s):
                b_on, a_on, k_on, par, _ = parts(s, s)
                v_at, last_at, k_at, first_at = quick_tickets(s)
                for i in range(STEPS):
                    if b_on:
                        act.wait_ge(scores, (s - 2) * STEPS + i + 1)
                        act.wait_ge(pvs, (s - 2) * STEPS + PV0 + i - 1)
                        act.activation(probs[:, i % 2, :], ps_s[:, i % 2, :], ACT.Exp).then_inc(exps, 1)
                    if a_on and i < 2:
                        act.wait_ge(misc_full, v_at + i + 1)
                        if i == 0:
                            act.wait_ge(pvs, s * STEPS)
                        act.copy(v_sb[:, 1 - par, 4 * i:4 * i + 4, :, 0:D],
                                 ps_m[:, :].rearrange("p (j h d) -> p j h d", j=4, h=HU)).then_inc(misc_taken, 1)
                    if k_on and i in (3, 4):
                        act.wait_ge(misc_full, k_at + i - 2)
                        act.wait_ge(k_pool, 2 * s)
                        act.activation(k_full[:, 512 * (i - 3):512 * (i - 3) + 512], ps_m[:, :], ACT.Identity,
                                       bias=bias_sb[:, 2 + par:3 + par]).then_inc(misc_taken, 1)
                    if k_on and i in (5, 6):
                        if i == 5:
                            act.wait_ge(misc_taken, k_at + 3)
                            act.wait_ge(k_low, 128 * s)
                            act.wait_ge(k_high, 128 * s)
                        act.copy(k_slots[:, (1, 3)[i - 5], :], k_full).then_inc(k_act, 1)
                    if k_on and i == 8:
                        act.wait_ge(k_pool, 2 * s + 1)
                        act.copy(k_slots[:, 2, :], k_rest).then_inc(k_act, 1)
                    if s >= 4 and i == 2:
                        add_bv(s - 4)
                if s == NU + 1:
                    add_bv(NU - 2)
                    add_bv(NU - 1)

            def before():
                act.wait_ge(state_ready, 1)
                for done in (masks_ready, misc_full, k_low, k_high, k_pool, mrow_in, f_ready):
                    act.sem_inc(done, 1)

            def end(n):
                for u in range(NU):
                    add_bv(u)

            cross_attention(act, quick, stage, before, None, end)

            deviations_and_rows(2)
            for i in range(4):
                t = i % 2
                act.wait_ge(rotated, i + 1)
                if i >= 2:
                    act.wait_ge(stacked[0], 16 * 4 * HU + 16)
                else:
                    act.wait_ge(normed, NU)
                for slot in ((0,), (1, 3))[t]:
                    act.copy(r_slots[t][:, slot, :], r_full[t]).then_inc(parts_act, 1)
                act.wait_ge(rest_done, i + 1)
                for slot in ((1, 2), (2,))[t]:
                    act.copy(r_slots[t][:, slot, :], r_rest[t]).then_inc(parts_act, 1)
            for t in range(NT):
                act.wait_ge(v_full, t + 1)
                act.copy(v_sb.rearrange("p a t h c -> p a t (h c)")[:, :, t, :].rearrange(
                    "p a (h c) -> p a h c", c=SLOT)[:, :, :, 0:D],
                         ps_a[:, t % 2, 0:E].rearrange("p (a h c) -> p a h c", a=2, h=HU)).then_inc(v_taken, 1)
            for u in range(NU):
                for i in range(4):
                    act.wait_ge(t_scores, 4 * u + i + 1)
                    if 4 * u + i >= 2:
                        act.wait_ge(t_pvs, 4 * u + i - 1)
                    act.activation(probs[:, i % 2, :], ps_s[:, i % 2, :], ACT.Exp).then_inc(t_exps, 1)
            deviations_and_rows(3)
            for r in range(8):
                n = min(4, KE * SLOTS - 4 * r)
                act.wait_ge(xs_full, r + 1)
                act.copy(xs_t.rearrange("p k n -> p (k n)")[:, 512 * r:512 * r + P * n],
                         ps_t[:, 512 * (r % 4):512 * (r % 4) + P * n]).then_inc(xs_taken, 1)

            def relu(e, j):
                for c in range(F // P):
                    if c % 2 == 0:
                        act.wait_ge(h_full, j * (F // P) + c + 2)
                    if c == 0:
                        act.wait_ge(y_full, j + 1)
                    act.activation(hidden[:, c, :], ps_t[:, 256 * c:256 * c + P], ACT.Relu, bias=b1_sb[:, e, c:c + 1]
                                   ).then_inc(h_ready, 1)

            expert_tiles(act, relu)

        @block.gpsimd
        def _(pool):
            pool.memset(zeros[:, :], 0.0).then_inc(zero_ready, 1)
            pool.memset(v_sb[:, :, :, :, D:SLOT], 1.0).then_inc(v_ones, 1)
            pool.wait_ge(xn_ready, NT)
            pool.wait_ge(in_w, 48)
            def add_row(k):
                pool.tensor_tensor(x_sb[:, :, :], x_sb[:, :, :],
                                   rows_bc[:, E * k:E * k + E].unsqueeze(1).to_broadcast([P, NT, E]),
                                   ALU.add).then_inc(pool_own, 1)

            add_row(0)

            def stage(c, s, k):
                b_on, a_on, k_on, par, _ = parts(s, k)
                cs = c * NU + s
                if k_on:
                    credit = 0 if isinstance(c, int) else 1
                    pool.wait_ge(k_act, cs * 3 + 1)
                    pool.wait_ge(k_pool, cs * 2 + credit)
                    pool.tensor_tensor(k_rest, k_full, k_slots[:, 1, :], ALU.subtract).then_inc(k_pool, 1)
                    pool.wait_ge(k_act, cs * 3 + 3)
                    pool.wait_ge(k_pool, cs * 2 + 1 + credit)
                    pool.tensor_tensor(k_slots[:, 0, :], k_rest, k_slots[:, 2, :], ALU.subtract).then_inc(k_pool, 1)

            def divide(u):
                pool.wait_ge(sums_out, 4 * u + 4)
                pool.wait_ge(o_free, u + 2)
                pool.tensor_tensor(o_acc[:, u, :], o_acc[:, u, :], sums[:, u % 2, :], ALU.mult).then_inc(normed, 1)

            def quick(s):
                stage(0, s, s)
                if s >= 3:
                    divide(s - 3)
                if s == NU + 1:
                    divide(NU - 1)

            def end(n):
                for u in range(NU):
                    divide(u)

            cross_attention(pool, quick, stage, None, None, end)
            pool.wait_ge(xn_ready, 2 * NT)
            add_row(1)
            for i in range(4):
                t = i % 2
                pool.wait_ge(swapped, i + 1)
                pool.tensor_tensor(r_swap[t].rearrange("p (b q) -> p b q", b=NB),
                                   r_swap[t].rearrange("p (b q) -> p b q", b=NB),
                                   rope[:, 2 * t + 1, :].unsqueeze(1).to_broadcast([P, NB, SQ]), ALU.mult
                                   ).then_inc(sin_done, 1)
                pool.wait_ge(parts_act, 3 * i + 3)
                pool.wait_ge(rest_done, i + 1)
                second, third = ((1, 3), (2, 0))[t]
                pool.tensor_tensor(r_slots[t][:, third, :], r_rest[t], r_slots[t][:, second, :], ALU.subtract
                                   ).then_inc(parts_pool, 1)
            for u in range(NU):
                pool.wait_ge(t_out, 2 * u + 2)
                pool.tensor_tensor(o_acc[:, u, :], o_acc[:, u, :], t_sums[:, u % 2, :], ALU.mult
                                   ).then_inc(self_normed, 1)
            pool.wait_ge(slots_ready, 1)
            pool.wait_ge(xs_zeroed, 32 * SLOTS // 3)
            pool.wait_ge(xn_ready, 3 * NT)
            for t in range(NT):
                pool.indirect_dma_start(xs_dram, bass.IndirectOffsetOnAxis(ap=slot_i[:, t:t + 1], axis=0),
                                        xn[:, t, :], None).then_inc(scattered, 16)
            pool.wait_ge(runs_ready, 2)
            n = pool.value_load(runs_i[0:1, NE - 1:NE], min_val=NE, max_val=SLOTS)
            pool.wait_ge(ys_stored, n * 16)
            pool.tensor_tensor(m_neg[:, 0, :], m_neg[:, 1, :], m_neg[:, 1, :], ALU.add).then_inc(pool_own, 1)
            pool.wait_ge(pool_own, 3)
            for t in range(NT):
                pool.indirect_dma_start(picked[:, t, :], None, ys_dram,
                                        bass.IndirectOffsetOnAxis(ap=slot_i[:, t:t + 1], axis=0)).then_inc(gathered[t], 16)

        @block.tensor
        def _(pe):
            pe.wait_ge(const_ready, 1)

            def turn_rows(n):
                for i in range(4):
                    k, half = i // 2, i % 2
                    pe.wait_ge(xn_ready, NT * (n - 1) + 4 * half + 4)
                    for t in range(4 * half, 4 * half + 4):
                        mm = pe.transpose(ps_t[:, 1024 * k + P * t:1024 * k + P * t + P], xn[:, t, P * k:P * k + P],
                                          ident_f)
                    mm.then_inc(xt_full, 1)

            turn_rows(1)
            pe.wait_ge(in_w, 48)
            pe.wait_ge(xt_taken, 4)
            for i in range(4):
                half, bb = i // 2, i % 2
                dst = [ps_a[:, 0, :], ps_a[:, 1, :], ps_o[:, :], ps_t[:, 0:512]][i]
                for k in range(KE):
                    mm = pe.matmul(dst, w_sb[:, 0, k, P * half:P * half + P], xn_t[:, k, 512 * bb:512 * bb + 512],
                                   start=(k == 0), stop=(k == KE - 1))
                mm.then_inc(q_proj, 1)
            for t in range(TK):
                pe.wait_ge(nz_ready, t + 1)
                pe.matmul(ps_m[:, 0:SQ], ones_b[:, :], mask_nz[:, t, :], start=(t == 0), stop=(t == TK - 1))
            pe.wait_ge(any_ready, 2)
            pe.matmul(ps_m[:, SQ:SQ + 2 * TK], ones_b[:, :], tile_any_b[:, :], start=True, stop=True).then_inc(counts_ready, 1)
            pe.wait_ge(neg_ready, 1)

            def quick(s):
                b_on, a_on, k_on, par, _ = parts(s, s)
                v_at, last_at, k_at, first_at = quick_tickets(s)
                wa, wb = s - 1, s - 2
                at_a, at_b = wa % 2 * NB + wa // 2, wb % 2 * NB + wb // 2

                def take(ticket):
                    pe.wait_ge(misc_taken, ticket + 1)

                def turn_maxima(u, g, ticket):
                    pe.wait_ge(minus_ready, 2 * u + g + 1)
                    take(ticket)
                    pe.matmul(ps_m[0:24, 0:P], q_parts[:, g, :, :, :].rearrange("p t a h -> p (t a h)"), ident_b[:, :],
                              start=True, stop=True).then_inc(misc_full, 1)

                def sums_of(i):
                    g, j = i // CH, i % CH
                    if i == 0:
                        pe.wait_ge(o_free, wb + 1)
                        if wb:
                            pe.wait_ge(kept, wb)
                        else:
                            pe.wait_ge(v_ones, 1)
                    pe.wait_ge(exps, wb * STEPS + i + 3)
                    for h4 in range(4):
                        mm = pe.matmul(ps_o[32 * h4:32 * h4 + 32, SQ * g:SQ * g + SQ],
                                       v_sb[:, par, j, 4 * g + h4, :], probs[:, i % 2, SQ * h4:SQ * h4 + SQ],
                                       start=(j == 0), stop=(j == CH - 1), tile_position=(0, 32 * h4),
                                       skip_group_check=True)
                    mm.then_inc(pvs, 1)

                for i in range(STEPS):
                    if b_on:
                        g, j = i // CH, i % CH
                        if j == 0:
                            pe.wait_ge(rows_set[g], 32 * wb + 32)
                        pe.wait_ge(exps, wb * STEPS + i + 1)
                        for h4 in range(4):
                            mm = pe.matmul(ps_s[:, i % 2, SQ * h4:SQ * h4 + SQ],
                                           k_stack[0:ROWS, par, 4 * g + h4, P * j:P * j + P],
                                           q_stack[0:ROWS, 4 * g + h4, at_b, :], start=True, stop=True)
                        mm.then_inc(scores, 1)
                    if a_on:
                        hh, qt = i // 2, i % 2
                        if i == 0:
                            pe.wait_ge(k_low, 128 * wa + 128)
                            if s == 1:
                                pe.wait_ge(q_stacked, 16 * 2 * HU)
                                pe.wait_ge(mask_set, 16)
                        if i == CH:
                            pe.wait_ge(k_high, 128 * wa + 128)
                        for c2 in range(2):
                            pe.wait_ge(a_max, 32 * wa + 2 * i + c2 + 1)
                            pe.matmul(ps_a[:, c2, :], q_stack[0:PAIR + 1, hh, at_a, P * qt:P * qt + P],
                                      k_stack[0:PAIR + 1, 1 - par, hh, 512 * c2:512 * c2 + 512],
                                      start=True, stop=True).then_inc(a_scores, 1)
                    if b_on and i:
                        sums_of(i - 1)
                    if a_on and i < 2:
                        take(v_at + i)
                        for j in range(4 * i, 4 * i + 4):
                            for kk in range(KE):
                                mm = pe.matmul(ps_m[:, P * (j % 4):P * (j % 4) + P], ctx_of[wa // 2 % 2][:, j, kk, :],
                                               w_sb[:, 2, kk, P * (1 - par):P * (1 - par) + P],
                                               start=(kk == 0), stop=(kk == KE - 1))
                        mm.then_inc(misc_full, 1)
                    if b_on and i == 2:
                        turn_maxima(wb, 1, last_at)
                    if k_on and i in (3, 4):
                        if i == 3 and par == 0:
                            pe.wait_ge(ctx_in_of[s // 2 % 2], s // 4 * 128 + 128)
                        take(k_at + i - 3)
                        for kk in range(KE):
                            mm = pe.matmul(ps_m[:, :], w_sb[:, 1, kk, P * par:P * par + P],
                                           ctx_of[s // 2 % 2][:, 4 * (i - 3):4 * (i - 3) + 4, kk, :],
                                           start=(kk == 0), stop=(kk == KE - 1))
                        mm.then_inc(misc_full, 1)
                    if a_on and i == 10:
                        turn_maxima(wa, 0, first_at)
                if b_on:
                    sums_of(STEPS - 1)

            def stage(c, s, k):
                b_on, a_on, k_on, par, _ = parts(s, k)
                cs = c * NU + s
                tk = c * (TICKETS * NU) + tickets_before(s)
                if isinstance(s, int):
                    at_a = (s - 1) % 2 * NB + (s - 1) // 2
                    at_b = (s - 2) % 2 * NB + (s - 2) // 2
                elif k == 0:
                    at_a, at_b = s // 2 + (NB - 1), s // 2 - 1
                else:
                    at_a, at_b = (s - 1) // 2, (s - 1) // 2 + (NB - 1)
                n = tk

                def fill(n, mm_of):
                    pe.wait_ge(misc_taken, n + 1)
                    mm_of().then_inc(misc_full, 1)

                def v_mm(i):
                    def go():
                        for j in range(4 * i, 4 * i + 4):
                            for kk in range(KE):
                                mm = pe.matmul(ps_m[:, P * (j % 4):P * (j % 4) + P], ctx_sb[:, j, kk, :],
                                               w_sb[:, 2, kk, P * (1 - par):P * (1 - par) + P],
                                               start=(kk == 0), stop=(kk == KE - 1))
                        return mm
                    return go

                def k_mm(i):
                    def go():
                        for kk in range(KE):
                            mm = pe.matmul(ps_m[:, :], w_sb[:, 1, kk, P * par:P * par + P],
                                           ctx_sb[:, 4 * i:4 * i + 4, kk, :], start=(kk == 0), stop=(kk == KE - 1))
                        return mm
                    return go

                def a_mm(xx):
                    hh, c2, qt = xx // 4, xx // 2 % 2, xx % 2
                    w = cs - 1
                    if xx == 0:
                        pe.wait_ge(k_low, w * 128 + 129)
                    if xx == 16:
                        pe.wait_ge(k_high, w * 128 + 129)
                    pe.wait_ge(a_max, w * 32 + xx + 1)
                    pe.matmul(ps_a[:, xx % 2, :],
                              q_stack[0:PAIR, hh, bass.ds(at_a, 1), P * qt:P * qt + P].rearrange("p a q -> p (a q)"),
                              k_stack[0:PAIR, 1 - par, hh, 512 * c2:512 * c2 + 512],
                              start=True, stop=True).then_inc(a_scores, 1)

                def s_mm(i):
                    g, j = i // CH, i % CH
                    w = cs - 2
                    if i == 0:
                        pe.wait_ge(mrow_in, w * 32 + 33)
                        pe.wait_ge(masks_ready, c * 3 + 2)
                    pe.wait_ge(exps, w * STEPS + i + 1)
                    for h4 in range(4):
                        if h4 % 2 == 0:
                            pe.matmul(ps_s[:, i % 2, SQ * h4:SQ * (h4 + 2)], ident_b[:, :],
                                      bias_kq[:, j:j + 1, :].to_broadcast([P, 2, SQ]),
                                      start=True, stop=False, skip_group_check=True)
                        mm = pe.matmul(ps_s[:, i % 2, SQ * h4:SQ * h4 + SQ],
                                       k_stack[0:ROWS, par, 4 * g + h4, P * j:P * j + P],
                                       q_stack[0:ROWS, 4 * g + h4, bass.ds(at_b, 1), :].rearrange("p a q -> p (a q)"),
                                       start=False, stop=h4 % 2 == 1, skip_group_check=True)
                    mm.then_inc(scores, 1)

                def pv_mm(i):
                    g, j = i // CH, i % CH
                    w = cs - 2
                    if i == 0:
                        pe.wait_ge(o_free, w + 1)
                    pe.wait_ge(exps, w * STEPS + i + 3)
                    for h4 in range(4):
                        mm = pe.matmul(ps_o[32 * h4:32 * h4 + 32, SQ * g:SQ * g + SQ],
                                       v_sb[:, par, j, 4 * g + h4, :], probs[:, i % 2, SQ * h4:SQ * h4 + SQ],
                                       start=(j == 0), stop=(j == CH - 1), tile_position=(0, 32 * h4),
                                       skip_group_check=True)
                    mm.then_inc(pvs, 1)

                def m_mm():
                    pe.wait_ge(max_own, (cs - 1) * 7 + 7)
                    return pe.matmul(ps_m[0:48, 0:P], m_parts[:, :, :, :].rearrange("p t a h -> p (t a h)"), ident_b[:, :],
                                     start=True, stop=True)

                def f_mm():
                    pe.wait_ge(f_ready, cs)
                    for gt in range(4):
                        mm = pe.matmul(ps_m[:, P * gt:P * gt + P],
                                       f_bc[:, par, 4 * gt:4 * gt + 4, :].rearrange("p h r -> p (h r)"), ident_f,
                                       start=True, stop=True)
                    return mm

                for i in range(STEPS):
                    if b_on:
                        s_mm(i)
                    if a_on:
                        for xx in range(3 * i, min(3 * i + 3, 32)):
                            a_mm(xx)
                    if b_on and i:
                        pv_mm(i - 1)
                    if a_on and i < 2:
                        fill(n, v_mm(i))
                        n = n + 1
                    if k_on and i in (6, 7):
                        if i == 6 and par == 0:
                            bt = c * NB + (s // 2)
                            pe.wait_ge(ctx_in, bt * 128 + 128)
                        fill(n, k_mm(i - 6))
                        n = n + 1
                    if a_on and i == 13:
                        fill(n, m_mm)
                        n = n + 1
                    if b_on and i == 14:
                        fill(n, f_mm)
                        n = n + 1
                if b_on:
                    pv_mm(STEPS - 1)

            def before():
                for qt in range(2):
                    mm = pe.matmul(ps_m[:, qt:qt + 1], neg_big[0:1, P * qt:P * qt + P], cst[0:1, 2 * P - 1:2 * P],
                                   start=True, stop=True)
                mm.then_inc(neg_col_ready, 1)
                pe.wait_ge(state_ready, 1)
                pe.wait_ge(q_stacked, 16 * 2 * HU)
                pe.wait_ge(edges_set, 32)
                pe.wait_ge(v_ones, 1)

            cross_attention(pe, quick, stage, before)
            for b in range(NB):
                pe.wait_ge(att_in, 4 * b + 4)
                if b >= 2:
                    pe.wait_ge(x1_ready, b - 1)
                for qt in range(2):
                    for hg in range(4):
                        mm = pe.matmul(ps_s[:, b % 2, E * qt:E * qt + E],
                                       o_acc[:, 2 * b + hg // 2, SQ * (hg % 2) + P * qt:SQ * (hg % 2) + P * qt + P],
                                       wo_sb[:, 0, hg, :], start=(hg == 0), stop=(hg == 3))
                mm.then_inc(att_full, 1)

            pe.wait_ge(x1_ready, NB)
            turn_rows(2)
            pe.wait_ge(xt_taken, 8)
            pe.wait_ge(in_late, 96)
            for i in range(4):
                half, t = i // 2, i % 2
                if i >= 2:
                    pe.wait_ge(swapped, i - 1)
                    pe.wait_ge(cos_done, i - 1)
                for bb in range(2):
                    for k in range(KE):
                        mm = pe.matmul(ps_s[:, i % 2, 512 * bb:512 * bb + 512],
                                       w_qkv[:, k, E * t + P * half:E * t + P * half + P],
                                       xn_t[:, k, 512 * bb:512 * bb + 512], start=(k == 0), stop=(k == KE - 1))
                mm.then_inc(rot_full, 1)
            for t in range(NT):
                if t >= 2:
                    pe.wait_ge(v_taken, t - 1)
                for k in range(KE):
                    mm = pe.matmul(ps_a[:, t % 2, 0:E], xn_t[:, k, P * t:P * t + P], w_qkv[:, k, 2 * E:3 * E],
                                   start=(k == 0), stop=(k == KE - 1))
                mm.then_inc(v_full, 1)
            pe.wait_ge(v_taken, NT)
            pe.wait_ge(cos_done, 4)
            pe.wait_ge(swapped, 4)

            def self_max_scores(u):
                half, b = u // NB, u % NB
                if b == 0:
                    pe.wait_ge(stacked[half], 16 * 4 * HU + (16 if half == 0 else 0))
                for y in range(8):
                    hp, qt = y // 2, y % 2
                    if 8 * u + y >= 2:
                        pe.wait_ge(self_max, 8 * u + y - 1)
                    pe.matmul(ps_a[:, y % 2, :], ident_b[:, :], causal[:, 0, qt:qt + 1, :].to_broadcast([P, 2, SQ]),
                              start=True, stop=False, skip_group_check=True)
                    for hh in (2 * hp, 2 * hp + 1):
                        mm = pe.matmul(ps_a[:, y % 2, SQ * (hh % 2):SQ * (hh % 2) + SQ],
                                       q_stack[0:PAIR, hh, u, P * qt:P * qt + P],
                                       k_stack[0:PAIR, half, hh, SQ * b:SQ * b + SQ],
                                       start=False, stop=hh % 2 == 1, skip_group_check=True)
                    mm.then_inc(self_scores, 1)

            def self_sums(u, i):
                half, b, g, j = u // NB, u % NB, i // 2, i % 2
                if i == 0:
                    pe.wait_ge(rows_in_place, 32 * u + 32)
                if 4 * u + i >= 2:
                    pe.wait_ge(t_exps, 4 * u + i - 1)
                for h4 in range(4):
                    if h4 % 2 == 0:
                        pe.matmul(ps_s[:, i % 2, SQ * h4:SQ * (h4 + 2)], ident_b[:, :],
                                  causal[:, 1, j:j + 1, :].to_broadcast([P, 2, SQ]),
                                  start=True, stop=False, skip_group_check=True)
                    mm = pe.matmul(ps_s[:, i % 2, SQ * h4:SQ * h4 + SQ],
                                   k_stack[0:ROWS, half, 4 * g + h4, SQ * b + P * j:SQ * b + P * j + P],
                                   q_stack[0:ROWS, 4 * g + h4, u, :],
                                   start=False, stop=h4 % 2 == 1, skip_group_check=True)
                mm.then_inc(t_scores, 1)

            def self_pv(u, i):
                half, b, g, j = u // NB, u % NB, i // 2, i % 2
                if i == 0 and u:
                    pe.wait_ge(t_out, 2 * u)
                pe.wait_ge(t_exps, 4 * u + i + 1)
                for h4 in range(4):
                    mm = pe.matmul(ps_o[32 * h4:32 * h4 + 32, SQ * g:SQ * g + SQ],
                                   v_sb[:, half, 2 * b + j, 4 * g + h4, :], probs[:, i % 2, SQ * h4:SQ * h4 + SQ],
                                   start=(j == 0), stop=(j == 1), tile_position=(0, 32 * h4), skip_group_check=True)
                mm.then_inc(t_pvs, 1)

            for u in range(NU + 1):
                if u < NU:
                    self_max_scores(u)
                if u:
                    for i in range(4):
                        self_sums(u - 1, i)
                        if i:
                            self_pv(u - 1, i - 1)
                    self_pv(u - 1, 3)
                if u < NU:
                    pe.wait_ge(parts_ready, u + 1)
                    if u:
                        pe.wait_ge(rows_taken, u)
                    pe.matmul(ps_m[0:48, 0:P], m_parts[:, :, :, :].rearrange("p t a h -> p (t a h)"), ident_b[:, :],
                              start=True, stop=True).then_inc(rows_full, 1)
            for b in range(NB):
                pe.wait_ge(self_normed, NU)
                if b >= 2:
                    pe.wait_ge(x2_ready, b - 1)
                for qt in range(2):
                    for hg in range(4):
                        mm = pe.matmul(ps_s[:, b % 2, E * qt:E * qt + E],
                                       o_acc[:, hg // 2 * NB + b, SQ * (hg % 2) + P * qt:SQ * (hg % 2) + P * qt + P],
                                       wo_sb[:, 1, hg, :], start=(hg == 0), stop=(hg == 3))
                mm.then_inc(att2_full, 1)

            pe.wait_ge(x2_ready, NB)
            turn_rows(3)
            pe.wait_ge(xt_taken, 12)
            for t in range(NT):
                for k in range(KE):
                    mm = pe.matmul(ps_m[:, NE * t:NE * t + NE], xn_t[:, k, P * t:P * t + P], gate_sb[:, k, :],
                                   start=(k == 0), stop=(k == KE - 1))
            mm.then_inc(gate_full, 1)
            pe.wait_ge(hot_ready, 1)
            hot = route_b[:, :, :].rearrange("p t e -> p (t e)")
            pe.matmul(ps_m[:, 64:128], ones_b[:, :], hot, start=True, stop=True)
            pe.matmul(ps_m[:, 128:192], lower_b[:, :], hot, start=True, stop=True).then_inc(ranks_full, 1)
            pe.wait_ge(xs_loaded, 16)
            for r in range(8):
                if r >= 4:
                    pe.wait_ge(xs_taken, r - 3)
                for i in range(4 * r, min(4 * r + 4, KE * SLOTS)):
                    mm = pe.transpose(ps_t[:, P * (i % 16):P * (i % 16) + P],
                                      xs_in[:, i % SLOTS, P * (i // SLOTS):P * (i // SLOTS) + P], ident_f)
                mm.then_inc(xs_full, 1)
            pe.wait_ge(xs_taken, 8)

            def expert(e, j):
                for c in range(F // P):
                    if c == 0:
                        pe.wait_ge(w_in[e], 32)
                    if c % 2 == 0:
                        pe.wait_ge(h_ready, j * (F // P) + c + 2)
                    for k in range(KE):
                        mm = pe.matmul(ps_t[:, 256 * c:256 * c + P], w1_sb[e][:, k, P * c:P * c + P],
                                       xs_t[:, k, bass.ds(j * P, P)], start=(k == 0), stop=(k == KE - 1))
                    mm.then_inc(h_full, 1)
                for c in range(F // P):
                    if c == 0:
                        pe.wait_ge(y_taken, j + 1)
                    pe.wait_ge(h_ready, j * (F // P) + (F // P) + c + 1)
                    mm = pe.matmul(ps_o[:, 0:E], hidden[:, c, :], w2_sb[e][:, c, :],
                                   start=(c == 0), stop=(c == F // P - 1))
                mm.then_inc(y_full, 1)

            expert_tiles(pe, expert)


def lay_out(i):
    c = np.zeros((TK + 1, P, NB, KE, P), np.float32)
    c[:TK] = i["ctx_1024"].reshape(NB, TK, P, KE, P).transpose(1, 4, 0, 3, 2)
    m = i["mask_1x1xSxS2_ik0"].reshape(SQ, TK, P)
    mk = np.zeros((TK + 1, P, 2 * SQ), m.dtype)
    mk[:TK, :, :SQ] = m.transpose(1, 2, 0)
    mk[:TK, :, SQ:] = m.reshape(2, P, TK, P).transpose(2, 1, 0, 3).reshape(TK, P, 2 * P)
    t = lambda w: w.T.reshape(KE, P, E).transpose(1, 0, 2)
    w = np.stack([t(i["L0_xattn_Wq"]), t(i["L0_xattn_Wk"]), t(i["L0_xattn_Wv"])], 1)

    def pad(wt):
        r = np.zeros((4, 32, 4, E), np.float32)
        r[:, :D] = wt.reshape(4, 4, D, E).transpose(1, 2, 0, 3)
        return r.reshape(P, 4, E)

    b = np.zeros((P, 8), np.float32)
    b[:, 0:2] = i["L0_xattn_bq"].reshape(2, P).T
    b[:, 2:4] = i["L0_xattn_bk"].reshape(2, P).T
    bv = np.zeros((4, 32, 4), np.float32)
    bv[:, :D] = i["L0_xattn_bv"].reshape(4, 4, D).transpose(1, 2, 0)
    b[:, 4:8] = bv.reshape(P, 4)
    cst = np.zeros((P, 4 * P), np.float32)
    cst[:, :P] = np.eye(P)
    cst[:, P:P + TK] = np.arange(TK)
    cst[:, P + 64:P + 64 + NE] = NE - np.arange(NE)
    cst[:, P + 80:P + 80 + NT - 1] = P * np.arange(1, NT)
    cst[:, 2 * P - 1] = 1
    cst[:, 2 * P:3 * P] = np.triu(np.ones((P, P)), 1)
    inv = (1.0 / np.float32(10000.0) ** (np.arange(0, D, 2, dtype=np.float32) / np.float32(D))).astype(np.float32)
    freq = np.repeat(np.outer(np.arange(SQ, dtype=np.float32), inv), 2, axis=1)
    sign = np.tile(np.array([-1, 1], np.float32), D // 2)
    cos, sin = np.cos(freq).T, (np.sin(freq) * sign).T
    rope = np.stack([cos * np.float32(D ** -0.5), sin * np.float32(D ** -0.5), cos, sin]).astype(np.float32)
    rope = np.tile(rope, (1, HU, 1)).transpose(1, 0, 2)
    at = np.arange(SQ)
    hidden = np.where(at[None, :] > at[:, None], -BIG, 0).astype(np.float32)
    causal = np.stack([hidden.reshape(2, P, SQ), hidden.T.reshape(2, P, SQ)]).transpose(2, 0, 1, 3)
    edges = np.ones((2, 4, 2 * HU * CH * P), np.float32)
    edges[0, 0] = 0
    return {
        "x": i["x"], "ctx_l": c.reshape(TK + 1, P, NB * KE * P), "mask_l": mk, "w_l": w,
        "w_qkv_l": i["L0_attn_Wqkv"].reshape(KE, P, 3 * E).transpose(1, 0, 2),
        "wo_pad": np.stack([pad(i["L0_xattn_Wo"].T), pad(i["L0_attn_Wout"])], 1), "biases": b,
        "rows_in": np.concatenate([i["L0_xattn_bo"], i["L0_attn_bout"], i["L0_ffn_gate_b"],
                                   i["L0_ffn_expert_bias"]])[None],
        "consts": cst, "causal_in": causal.astype(mybir.dt.np(BF16)), "rope_in": rope,
        "gate_l": i["L0_ffn_gate_w"].T.reshape(KE, P, NE).transpose(1, 0, 2),
        "edges_in": edges.astype(mybir.dt.np(BF16)),
        "w1": i["L0_ffn_w1"], "b1_l": i["L0_ffn_b1"].reshape(NE, F // P, P).transpose(2, 0, 1),
        "w2": i["L0_ffn_w2"], "b2": i["L0_ffn_b2"],
    }


def kernel(**inputs):
    import concourse.bacc as bacc
    from concourse.bass_utils import run_bass_kernel_spmd

    nc = bacc.Bacc("TRN2", target_bir_lowering=False, num_devices=1)
    arrays = {k: np.ascontiguousarray(v) for k, v in lay_out({k: np.asarray(v) for k, v in inputs.items()}).items()}
    args = [nc.dram_tensor(k, v.shape, mybir.dt.from_np(v.dtype), kind="ExternalInput").ap()
            for k, v in arrays.items()]
    out = nc.dram_tensor("out", [NB, SQ, E], F32, kind="ExternalOutput").ap()
    build(nc, *args, out)
    return run_bass_kernel_spmd(nc, [arrays], core_ids=[0]).results[0]["out"]
```

```python
from contextlib import ExitStack

import numpy as np

import concourse.bass as bass
from concourse import mybir

F32 = mybir.dt.float32
BF16 = mybir.dt.bfloat16
I32 = mybir.dt.int32
ALU = mybir.AluOpType
ACT = mybir.ActivationFunctionType
AX = mybir.AxisListType

P = 128
NB, SQ, E = 4, 256, 256
H, D = 16, 16
LK = 4096
TK = LK // P
CH = 8
NU, HU = 8, 8
NT = NB * SQ // P
KE = E // P
SLOT = 32
BIG = float(2 ** 30)
EPS = 1e-5
NE, F = 8, 1024
SLOTS = NT + NE - 1
PAIR = 2 * D * 3
OF_Q, OF_K = (0, 0, 0, 1, 1, 2), (2, 0, 1, 0, 1, 0)
ROWS = PAIR + 4
STEPS = 2 * CH
TICKETS = 6


class Chain:

    def __init__(self, eng, sem):
        self.eng, self.sem, self.n = eng, sem, 0

    def add(self, ins):
        self.n = self.n + 1
        ins.then_inc(self.sem, 1)

    def wait(self):
        if self.n:
            self.eng.wait_ge(self.sem, self.n)


def tickets_before(s):
    if isinstance(s, int):
        return [0, 2][s] if s < 2 else 7 + 6 * (s - 2) if s <= 8 else 47
    return s * 6 - 5


def build(nc, x_l, ctx_l, mask_l, mask_first, w_l, w_qkv_l, wo_pad, biases, rows_in, consts, causal_in, rope_in, gate_l,
          edges_in, w1, b1_l, w2, b2, out):
    ctx = ExitStack()
    with ctx:
        def sb(name, shape, dt):
            return ctx.enter_context(nc.sbuf_tensor(name, shape, dt))

        def sem(name):
            return ctx.enter_context(nc.semaphore(name))

        arena = sb("arena", [P, 170 * 256], F32)

        def cut(at, shape, dt):
            n = int(np.prod(shape))
            size = n * (2 if dt == BF16 else 4) // 4
            v = arena[:, at * 256:at * 256 + size]
            if dt != F32:
                v = v.bitcast(dt)
            if len(shape) > 1:
                axes = "abcde"[:len(shape)]
                v = v.rearrange("p (%s) -> p %s" % (" ".join(axes), " ".join(axes)),
                                **dict(zip(axes[1:], shape[1:])))
            return v

        k_stack = cut(0, [2, HU, CH * P], BF16)
        q_stack = cut(32, [HU, NU, SQ], BF16)
        v_sb = cut(64, [2, CH, HU, SLOT], F32)
        o_acc = cut(96, [NU, 2 * SQ], F32)
        probs = cut(112, [2, 4 * SQ], F32)
        ctx_sb = cut(120, [CH, KE, P], F32)
        mask_in = cut(128, [CH, 2 * SQ], I32)
        bias_qk = cut(144, [2, CH * P], BF16)
        bias_kq = cut(148, [CH, SQ], BF16)
        masked = cut(152, [512], F32)
        w_sb = cut(154, [3, KE, E], F32)
        w_qkv = cut(160, [KE, 3 * E], F32)
        rope = cut(166, [4, SQ], F32)
        mask_all = cut(0, [TK, SQ], I32)
        mask_nz = cut(96, [TK, SQ], BF16)
        q_full = cut(112, [2048], F32)
        q_rest = cut(144, [2048], F32)
        q_slots = cut(96, [3, 2048], BF16)
        xn = cut(128, [NT, E], F32)
        xn_t = cut(136, [KE, NT * P], F32)
        ctx_of = [ctx_sb, cut(128, [CH, KE, P], F32)]
        mask_line = cut(136, [CH * P], I32)[0:1]
        mask_row = cut(140, [CH * P], BF16)[0:1]
        sums = cut(144, [2, 2 * SQ], F32)
        spread = cut(148, [2 * SQ], F32)
        k_slots = cut(80, [3, 1024], BF16)
        k_full = cut(88, [1024], F32)
        k_rest = cut(92, [1024], F32)
        r_slots = [cut(80, [3, 1024], BF16), cut(88, [3, 1024], BF16), cut(144, [3, 1024], BF16),
                   cut(150, [3, 1024], BF16)]
        r_full = [cut(96, [1024], F32), cut(100, [1024], F32)]
        r_rest = [cut(104, [1024], F32), cut(108, [1024], F32)]
        r_swap = [cut(120, [1024], F32), cut(124, [1024], F32)]
        t_sums = cut(120, [2, 2 * SQ], F32)
        t_spread = cut(124, [2 * SQ], F32)
        expert_at = (80, 128, 144, 0, 16, 32, 48, 64)
        w1_sb = [cut(at, [KE, F], F32) for at in expert_at]
        w2_sb = [cut(at + 8, [F // P, E], F32) for at in expert_at]
        xn_last = cut(96, [NT, E], F32)
        xn_t_last = cut(104, [KE, NT * P], F32)
        xs_in = cut(112, [SLOTS, E], F32)
        y_all = xs_in
        xs_t = cut(96, [KE, SLOTS * P], F32)
        b2_bc = cut(160, [NE, E], F32)
        picked = cut(96, [NT, E], F32)

        x_sb = sb("x_sb", [P, NT, E], F32)
        wo_sb = sb("wo_sb", [P, 2, 4, E], F32)
        bias_sb = sb("bias_sb", [P, 8], F32)
        b1_sb = sb("b1_sb", [P, NE, F // P], F32)
        gate_sb = sb("gate_sb", [P, KE, NE], F32)
        rows_bc = sb("rows_bc", [P, 2 * E + 2 * NE], F32)
        cst = sb("cst", [P, 4 * P], F32)
        causal = sb("causal", [P, 2, 2, SQ], BF16)
        ident_b = sb("ident_b", [P, P], BF16)
        ones_b = sb("ones_b", [P, P], BF16)
        lower_b = sb("lower_b", [P, P], BF16)
        zeros = sb("zeros", [P, E], F32)
        ln_stat = sb("ln_stat", [P, NT, 6], F32)
        ln_mv = sb("ln_mv", [P, NT, 2], F32)
        ln_r = sb("ln_r", [P, NT], F32)
        eps_sb = sb("eps_sb", [P, 1], F32)
        tile_any = sb("tile_any", [P, TK], F32)
        tile_any_b = sb("tile_any_b", [P, 2 * TK], BF16)
        tile_mixed = sb("tile_mixed", [P, TK], F32)
        row_dead = sb("row_dead", [P, SQ], F32)
        q_scale = sb("q_scale", [P, SQ], F32)
        neg_big = sb("neg_big", [P, SQ], F32)
        neg_big_col = sb("neg_big_col", [P, 2], F32)
        listing = sb("listing", [TK, 192], F32)
        tiles_i = sb("tiles_i", [1, 48], I32)
        m_run = sb("m_run", [P, NU, 16], F32)
        m_tile = sb("m_tile", [P, 1], F32)
        inverse = sb("inverse", [P, 16], F32)
        m_half = sb("m_half", [P, 32], F32)
        m_quick = sb("m_quick", [P, 3, 2, HU], F32)
        q_parts = sb("q_parts", [P, 2, 2, 3, 4], BF16)
        quick_rows = sb("quick_rows", [24, 2, P], BF16)
        m_old = sb("m_old", [P, 16], F32)
        m_cur = sb("m_cur", [P, 16], F32)
        m_neg = sb("m_neg", [P, 2, 16], F32)
        m_parts = sb("m_parts", [P, 2, 3, HU], BF16)
        m_diff = sb("m_diff", [P, 16], F32)
        m_rows = sb("m_rows", [48, P], BF16)
        f_bc = sb("f_bc", [P, 2, 16, 32], F32)
        hidden = f_bc[:, :, :, :].rearrange("p a n r -> p (a n r)").rearrange("p (c n) -> p c n", c=F // P)
        route = sb("route", [P, 8, NT, NE], F32)
        route_b = sb("route_b", [P, NT, NE], BF16)
        slot_i = sb("slot_i", [P, NT], I32)
        runs_i = sb("runs_i", [1, 2 * NE], I32)

        ident_f = cst[:, 0:P]
        xs_dram = nc.dram_tensor("xs_dram", [SLOTS * P, E], F32).ap()
        ys_dram = nc.dram_tensor("ys_dram", [SLOTS * P, E], F32).ap()

        ps_s = ctx.enter_context(nc.psum_tensor("ps_s", [P, 2, 1024], F32))
        ps_a = ctx.enter_context(nc.psum_tensor("ps_a", [P, 2, 512], F32))
        ps_o = ctx.enter_context(nc.psum_tensor("ps_o", [P, 512], F32))
        ps_m = ctx.enter_context(nc.psum_tensor("ps_m", [P, 512], F32))
        ps_t = ps_s[:, :, :].rearrange("p a n -> p (a n)")

        in_x, in_w, in_c = sem("in_x"), sem("in_w"), sem("in_c")
        in_m = [sem(f"in_m{i}") for i in range(4)]
        dve_own, act_own, pool_own = sem("dve_own"), sem("act_own"), sem("pool_own")
        const_ready = sem("const_ready")
        diff_ready, max_steps = sem("diff_ready"), sem("max_steps")
        ln_var = sem("ln_var")
        ln_std = sem("ln_std")
        xn_ready = sem("xn_ready")
        xt_full, xt_taken = sem("xt_full"), sem("xt_taken")
        q_proj, q_taken = sem("q_proj"), sem("q_taken")
        nz_ready = sem("nz_ready")
        counts_ready = sem("counts_ready")
        any_ready = sem("any_ready")
        entries_ready, entries_turned = sem("entries_ready"), sem("entries_turned")
        neg_ready = sem("neg_ready")
        neg_col_ready = sem("neg_col_ready")
        q_slots_ready = sem("q_slots_ready")
        q_stacked = sem("q_stacked")
        tiles_ready = sem("tiles_ready")
        edges_set, v_ones, mask_set = sem("edges_set"), sem("v_ones"), sem("mask_set")
        line_in, row_ready = sem("line_in"), sem("row_ready")
        cross_own, end_own = sem("cross_own"), sem("end_own")
        kept, minus_ready, state_ready = sem("kept"), sem("minus_ready"), sem("state_ready")
        ctx_rest_in = sem("ctx_rest_in")
        ctx_in_of, rows_set = [sem("ctx_in0"), sem("ctx_in1")], [sem("rows_set0"), sem("rows_set1")]
        masks_in = sem("masks_in")
        masks_ready = sem("masks_ready")
        ctx_in = sem("ctx_in")
        misc_full, misc_taken = sem("misc_full"), sem("misc_taken")
        k_act, k_pool = sem("k_act"), sem("k_pool")
        k_low, k_high = sem("k_low"), sem("k_high")
        a_scores, a_max = sem("a_scores"), sem("a_max")
        scores, exps, pvs = sem("scores"), sem("exps"), sem("pvs")
        o_free = sem("o_free")
        max_own = sem("max_own")
        mrow_in = sem("mrow_in")
        f_ready = sem("f_ready")
        sums_out = sem("sums_out")
        normed, att_in, att_full, x1_ready = sem("normed"), sem("att_in"), sem("att_full"), sem("x1_ready")
        out_done = sem("out_done")
        in_late, zero_ready, xs_zeroed = sem("in_late"), sem("zero_ready"), sem("xs_zeroed")
        rot_full, swapped, cos_done = sem("rot_full"), sem("swapped"), sem("cos_done")
        sin_done, rotated, rest_done = sem("sin_done"), sem("rotated"), sem("rest_done")
        parts_act, parts_pool = sem("parts_act"), sem("parts_pool")
        stacked = [sem("stacked0"), sem("stacked1")]
        v_full, v_taken = sem("v_full"), sem("v_taken")
        self_scores, self_max = sem("self_scores"), sem("self_max")
        parts_ready, rows_full, rows_taken, rows_in_place = (
            sem("parts_ready"), sem("rows_full"), sem("rows_taken"), sem("rows_in_place"))
        t_scores, t_exps, t_pvs = sem("t_scores"), sem("t_exps"), sem("t_pvs")
        t_out, t_inverted, t_kept = sem("t_out"), sem("t_inverted"), sem("t_kept")
        self_normed, att2_full, x2_ready = sem("self_normed"), sem("att2_full"), sem("x2_ready")
        gate_full, hot_ready, ranks_full = sem("gate_full"), sem("hot_ready"), sem("ranks_full")
        runs_ready, slots_ready, scattered = sem("runs_ready"), sem("slots_ready"), sem("scattered")
        xs_loaded = [sem(f"xs_loaded{i}") for i in range(3)]
        xs_full, xs_taken = sem("xs_full"), sem("xs_taken")
        w_in = [sem(f"w_in{e}") for e in range(NE)]
        b2_in = sem("b2_in")
        h_full, h_ready, y_full, y_taken = sem("h_full"), sem("h_ready"), sem("y_full"), sem("y_taken")
        ys_stored, x3_ready = sem("ys_stored"), sem("x3_ready")
        gathered = [sem(f"gathered{t}") for t in range(NT)]

        PV0 = 2 * STEPS

        def cross_attention(eng, quick, stage, before=None, start=None, end=None):
            eng.wait_ge(tiles_ready, 1)
            n = eng.value_load(tiles_i[0:1, TK:TK + 1], min_val=0, max_val=TK // CH)
            with eng.If(n < 1):
                for s in range(NU + 2):
                    quick(s)
            with eng.If(n > 0):
                if before:
                    before()
                with eng.Fori(0, n) as c:
                    if start:
                        start(c)
                    for s in (0, 1):
                        stage(c, s, s)
                    with eng.Fori(1, NB) as b:
                        for k in (0, 1):
                            stage(c, b * 2 + k, k)
                    for s in (NU, NU + 1):
                        stage(c, s, s)
                if end:
                    end(n)

        def load_ctx_tile(eng, b, j, t, done):
            src = ctx_l[bass.ds(t, 1), :, KE * P * b:KE * P * b + KE * P]
            eng.dma_start(ctx_of[b % 2][:, j, :, :], src.rearrange("a p n -> p (a n)").rearrange(
                "p (k n) -> p k n", k=KE)).then_inc(done, 16)

        def quick_tickets(s):
            b_on, a_on, k_on, par, _ = parts(s, s)
            if s < 2:
                return 2, None, 4 * s, 6
            v = tickets_before(s)
            k = v + 3 if a_on else v + 1
            return v, k - 1, k, k + (2 if k_on else 0)

        def expert_runs(eng):
            eng.wait_ge(runs_ready, 2)
            return [(eng.value_load(runs_i[0:1, NE + e:NE + e + 1], min_val=0, max_val=SLOTS - 1),
                     eng.value_load(runs_i[0:1, e:e + 1], min_val=1, max_val=SLOTS)) for e in range(NE)]

        def expert_tiles(eng, step, runs=None):
            for e, (first, end) in enumerate(runs or expert_runs(eng)):
                with eng.Fori(first, end) as j:
                    step(e, j)

        def parts(s, k):
            if isinstance(s, int):
                return s >= 2, 1 <= s <= 8, s <= 7, s % 2, s // 2
            return True, True, True, k, None

        def rows_of(part, of):
            return [D * r for r, p in enumerate(of) if p == part]

        def first(i):
            return 4 * (i // 2) + i % 2 + 1

        def second(i):
            return first(i) + 2

        block = ctx.enter_context(nc.Block())

        @block.sync
        def _(sp):
            sp.dma_start(x_sb[:, :, :], x_l).then_inc(in_x, 16)
            sp.dma_start(cst[:, :], consts).then_inc(in_c, 16)
            for i in range(4):
                tiles = slice(CH * i, CH * i + CH)
                sp.dma_start(mask_all[:, tiles, :], mask_first[:, tiles, :]).then_inc(in_m[i], 16)
            sp.dma_start(bias_sb[:, :], biases).then_inc(in_w, 16)
            sp.dma_start(rows_bc[:, :], rows_in[0, :].partition_broadcast(P)).then_inc(in_w, 16)
            sp.dma_start(w_sb[:, :, :, :], w_l).then_inc(in_w, 16)
            sp.dma_start(wo_sb[:, :, :, :], wo_pad).then_inc(in_late, 16)
            sp.dma_start(w_qkv[:, :, :], w_qkv_l).then_inc(in_late, 16)
            sp.dma_start(rope[:, :, :], rope_in).then_inc(in_late, 16)
            sp.dma_start(causal[:, :, :, :], causal_in).then_inc(in_late, 16)
            sp.dma_start(gate_sb[:, :, :], gate_l).then_inc(in_late, 16)
            sp.dma_start(b1_sb[:, :, :], b1_l).then_inc(in_late, 16)
            q_edge = q_stack.rearrange("p h u q -> p (h u q)")[PAIR:ROWS]
            k_edge = k_stack.rearrange("p a h n -> p (a h n)")[PAIR:ROWS]
            sp.dma_start(q_edge, edges_in[1]).then_inc(edges_set, 16)
            sp.wait_ge(nz_ready, TK)
            sp.dma_start(k_edge, edges_in[0]).then_inc(edges_set, 16)

            def stack_q():
                for part in range(3):
                    sp.wait_ge(q_slots_ready, part + 1)
                    for r in rows_of(part, OF_Q):
                        sp.dma_start(q_stack[r:r + D].rearrange("p h u q -> p h (u q)"), q_slots[:, part, :]
                                     ).then_inc(q_stacked, 16)

            def clear(i):
                dst = (xs_dram, ys_dram)[i % 2][3 * (i // 2) * P:3 * (i // 2) * P + 3 * P]
                sp.wait_ge(zero_ready, 1)
                sp.dma_start(dst.rearrange("(s p) n -> p s n", p=P),
                             zeros[:, :].unsqueeze(1).to_broadcast([P, 3, E])).then_inc(xs_zeroed, 16)

            def load_ctx(b, tiles):
                for j, t in enumerate(tiles):
                    load_ctx_tile(sp, b, j, t, ctx_in_of[b % 2])

            first_tiles = []

            def quick(s):
                b_on, a_on, k_on, par, _ = parts(s, s)
                v_at, last_at, k_at, first_at = quick_tickets(s)
                if s == 0:
                    for j in range(CH // 2):
                        first_tiles.append(sp.value_load(tiles_i[0:1, j:j + 1], min_val=0, max_val=TK))
                        load_ctx_tile(sp, 0, j, first_tiles[j], ctx_in_of[0])
                    for j in range(CH // 2, CH):
                        first_tiles.append(sp.value_load(tiles_i[0:1, j:j + 1], min_val=0, max_val=TK))
                    sp.wait_ge(q_proj, 4)
                    for j, t in enumerate(first_tiles):
                        sp.dma_start(mask_line[:, P * j:P * j + P], mask_l[bass.ds(t, 1), 0:1, SQ:SQ + P].rearrange(
                            "a p n -> p (a n)")).then_inc(line_in, 16)
                    stack_q()
                    sp.wait_ge(row_ready, 1)
                    sp.wait_ge(edges_set, 32)
                    sp.dma_start(k_stack.rearrange("p a h n -> p (a h) n")[PAIR:PAIR + 1],
                                 mask_row.unsqueeze(1).to_broadcast([1, 2 * HU, CH * P])).then_inc(mask_set, 16)
                elif s % 2 == 0 and s + 2 < NU:
                    sp.wait_ge(misc_full, v_at + 2)
                    load_ctx(s // 2 + 1, first_tiles)
                if b_on:
                    sp.wait_ge(misc_taken, last_at + 2)
                    rows_of_maxima(s - 2, 1)
                if s == 0:
                    for part in range(3):
                        sp.wait_ge(*((k_act, 1), (k_act, 2), (k_pool, 2))[part])
                        stack_k(par, 0, k_low, (part,))
                        stack_k(par, 1, k_high, (part,))
                    load_ctx(1, first_tiles)
                if k_on and s:
                    sp.wait_ge(k_act, 2 * s + 2)
                    sp.wait_ge(k_pool, 2 * s + 2)
                    sp.wait_ge(pvs, s * STEPS + CH)
                    stack_k(par, 0, k_low)
                if a_on:
                    sp.wait_ge(misc_taken, first_at + 2)
                    rows_of_maxima(s - 1, 0)
                if k_on and s:
                    sp.wait_ge(pvs, s * STEPS + STEPS)
                    stack_k(par, 1, k_high)
                if 2 <= s < 7:
                    clear(2 * s - 4)
                    clear(2 * s - 3)

            def rows_of_maxima(u, g):
                at = u % 2 * NB + u // 2
                for qt in range(2):
                    sp.dma_start(q_stack[PAIR + 1:ROWS, 4 * g:4 * g + 4, at, P * qt:P * qt + P],
                                 quick_rows[12 * qt:12 * qt + 12, g, :]).then_inc(rows_set[g], 16)

            def stack_k(par, g, done, some=(0, 1, 2)):
                for part in some:
                    for r in rows_of(part, OF_K):
                        sp.dma_start(k_stack[r:r + D, par, 4 * g:4 * g + 4, :],
                                     k_slots[64 * g:64 * g + 64, part, :]).then_inc(done, 16)

            def start(c):
                tiles = [sp.value_load(tiles_i[0:1, bass.ds(c * CH + j, 1)], min_val=0, max_val=TK)
                         for j in range(CH)]
                sp.wait_ge(masks_ready, c * 3 + 1)
                for j, t in enumerate(tiles):
                    sp.dma_start(mask_in[:, j, :], mask_l[bass.ds(t, 1), :, :].rearrange("a p q -> p (a q)")
                                 ).then_inc(masks_in, 16)

            def stage(c, s, k):
                b_on, a_on, k_on, par, _ = parts(s, k)
                cs = c * NU + s
                tk = c * (TICKETS * NU) + tickets_before(s)
                if k_on and par == 0:
                    tiles = [sp.value_load(tiles_i[0:1, bass.ds(c * CH + j, 1)], min_val=0, max_val=TK)
                             for j in range(CH)]
                    sp.wait_ge(misc_full, tk + (3 if a_on else 1))
                    for j, t in enumerate(tiles):
                        src = ctx_l[bass.ds(t, 1), :, bass.ds(s * (KE * P // 2), KE * P)]
                        sp.dma_start(ctx_sb[:, j, :, :], src.rearrange("a p n -> p (a n)").rearrange(
                            "p (k n) -> p k n", k=KE)).then_inc(ctx_in, 16)
                if k_on:
                    sp.wait_ge(k_act, cs * 2 + 3)
                    sp.wait_ge(k_pool, cs * 2 + 3)

                if k_on:
                    sp.wait_ge(pvs, cs * STEPS + CH)
                    stack_k(par, 0, k_low)
                if a_on:
                    n = tk + (2 if a_on else 0) + (2 if k_on else 0) + 1
                    sp.wait_ge(misc_taken, n + 1)
                    u_at = (s - 1) % 2 * 4 + (s - 1) // 2 if isinstance(s, int) else None
                    if u_at is None:
                        u_at = s // 2 + (NB - 1) if k == 0 else (s - 1) // 2
                    for qt in range(2):
                        sp.dma_start(q_stack[PAIR + 1:ROWS, :, bass.ds(u_at, 1), P * qt:P * qt + P].rearrange(
                            "p h u q -> p h (u q)"), m_rows[24 * qt:24 * qt + 24, :]).then_inc(mrow_in, 16)
                if k_on:
                    sp.wait_ge(pvs, cs * STEPS + STEPS)
                    stack_k(par, 1, k_high)

            def before():
                sp.wait_ge(q_proj, 4)
                stack_q()
                for i in range(2 * SLOTS // 3):
                    clear(i)

            cross_attention(sp, quick, stage, before, start)
            def stack_rotated(half, part):
                if half == 0 and part == 0:
                    sp.wait_ge(normed, NU)
                    sp.dma_start(k_edge, edges_in[0]).then_inc(stacked[0], 16)
                for t in range(2):
                    i = 2 * half + t
                    sp.wait_ge(*((parts_act, first(i)), (parts_act, second(i)), (parts_pool, i + 1))[part])
                    for r in rows_of(part, (OF_Q, OF_K)[t]):
                        if t == 0:
                            dst = q_stack[r:r + D, :, NB * half:NB * half + NB, :].rearrange("p h u q -> p h (u q)")
                        else:
                            dst = k_stack[r:r + D, half, :, :]
                        sp.dma_start(dst, r_slots[i][:, part, :]).then_inc(stacked[half], 16)

            for part in range(3):
                stack_rotated(0, part)

            def load_expert(e, piece):
                if piece == 0 and e == 1:
                    sp.wait_ge(rot_full, 4)
                    sp.wait_ge(v_full, NT)
                elif piece == 0 and e in (0, 2):
                    sp.wait_ge(stacked[1], 16 * 12)
                elif piece == 0 and e == 3:
                    sp.wait_ge(t_pvs, 4 * NB)
                if piece < 2:
                    sp.dma_start(w1_sb[e][:, piece, :], w1[e, P * piece:P * piece + P, :]).then_inc(w_in[e], 16)
                else:
                    rows = slice(4 * (piece - 2), 4 * (piece - 2) + 4)
                    sp.dma_start(w2_sb[e][:, rows, :], w2[e].rearrange("(c p) n -> p c n", p=P)[:, rows, :]
                                 ).then_inc(w_in[e], 16)

            for u in range(NU):
                sp.wait_ge(rows_taken, u + 1)
                for qt in range(2):
                    sp.dma_start(q_stack[PAIR + 1:ROWS, :, u, P * qt:P * qt + P], m_rows[24 * qt:24 * qt + 24, :]
                                 ).then_inc(rows_in_place, 16)
                if u < 3:
                    stack_rotated(1, u)
                for piece in (2 * u, 2 * u + 1):
                    load_expert((1, 0, 2, 3)[piece // 4], piece % 4)
            sp.wait_ge(t_pvs, 4 * NU)
            for e in range(4, NE):
                for piece in range(4):
                    load_expert(e, piece)
            sp.dma_start(b2_bc.rearrange("p e n -> p (e n)"), b2.rearrange("e n -> (e n)").partition_broadcast(P)
                         ).then_inc(b2_in, 16)
            sp.wait_ge(scattered, 16 * NT)
            for i in range(3):
                sp.dma_start(xs_in[:, 5 * i:5 * i + 5, :],
                             xs_dram[5 * P * i:5 * P * (i + 1)].rearrange("(s p) n -> p s n", p=P)).then_inc(xs_loaded[i], 16)

            def store(e, j):
                sp.wait_ge(y_taken, j + 2)
                sp.dma_start(ys_dram[bass.ds(j * P, P), :], y_all[:, bass.ds(j, 1), :].rearrange("p a n -> p (a n)")
                             ).then_inc(ys_stored, 16)

            expert_tiles(sp, store)
            for t in range(NT):
                sp.wait_ge(x3_ready, t + 1)
                sp.dma_start(out.rearrange("b (t p) d -> (b t) p d", p=P)[t], x_sb[:, t, :]).then_inc(out_done, 16)
            sp.wait_ge(out_done, 16 * NT)

        @block.vector
        def _(dve):
            own = Chain(dve, dve_own)
            own.add(dve.memset(eps_sb[:, :], EPS))
            own.add(dve.memset(ones_b[:, :], 1.0))
            own.wait()
            dve.wait_ge(in_c, 16)
            own.add(dve.tensor_copy(lower_b[:, :], cst[:, 2 * P:3 * P]))
            own.wait()
            dve.tensor_copy(ident_b[:, :], ident_f).then_inc(const_ready, 1)

            def row_stats(src, rows):
                for t in range(rows.start, rows.stop):
                    own.add(dve.bn_stats(ln_stat[:, t, :], src[:, t, :]))
                own.wait()
                for t in range(rows.start, rows.stop):
                    own.add(dve.bn_aggr(ln_mv[:, t, :], ln_stat[:, t, :]))

            def variances(half):
                own.wait()
                at = ln_r[:, 4 * half:4 * half + 4]
                dve.tensor_copy(at, ln_mv[:, 4 * half:4 * half + 4, 1]).then_inc(ln_var, 1)

            def normalise(n, half, dst):
                dve.wait_ge(ln_std, 2 * n - 1 + half)
                at = ln_r[:, 4 * half:4 * half + 4]
                own.add(dve.reciprocal(at, at))
                own.wait()
                for t in range(4 * half, 4 * half + 4):
                    dve.tensor_scalar(dst[:, t, :], x_sb[:, t, :], ln_mv[:, t, 0:1], ln_r[:, t:t + 1],
                                      ALU.subtract, ALU.mult).then_inc(xn_ready, 1)

            dve.wait_ge(in_x, 16)
            for half in range(2):
                row_stats(x_sb, slice(4 * half, 4 * half + 4))
                variances(half)
            normalise(1, 0, xn)
            normalise(1, 1, xn)
            for t in range(TK):
                if t % CH == 0:
                    dve.wait_ge(in_m[t // CH], 16)
                dve.tensor_scalar(mask_nz[:, t, :], mask_all[:, t, :], 0.0, 0.0, ALU.not_equal, ALU.add,
                                  accum_out=tile_any[:, t:t + 1]).then_inc(nz_ready, 1)
            dve.wait_ge(nz_ready, TK)
            own.add(dve.tensor_scalar(tile_mixed[:, :], tile_any[:, :], float(SQ), None, ALU.is_lt))
            own.wait()
            dve.scalar_tensor_tensor(tile_any_b[:, TK:2 * TK], tile_any[:, :], 0.0, tile_mixed[:, :],
                                     ALU.is_gt, ALU.mult).then_inc(any_ready, 1)
            dve.tensor_scalar(tile_any_b[:, 0:TK], tile_any[:, :], 0.0, None, ALU.is_gt).then_inc(any_ready, 1)
            dve.wait_ge(counts_ready, 1)
            own.add(dve.tensor_scalar(row_dead[:, :], ps_m[:, 0:SQ], 0.0, None, ALU.is_equal))
            own.add(dve.tensor_scalar(q_scale[:, :], ps_m[:, 0:SQ], 0.0, D ** -0.5, ALU.is_gt, ALU.mult))
            dve.tensor_scalar(neg_big[:, :], ps_m[:, 0:SQ], 0.0, -BIG, ALU.is_gt, ALU.mult).then_inc(neg_ready, 1)
            own.wait()
            part = lambda i, n=TK: listing[:, TK * i:TK * i + n]
            numbers, number = cst[0:TK, P:P + TK], cst[0:TK, P + 96:P + 97]
            counts, one, upto, place, found = (part(i) for i in range(5))
            count = upto[:, TK - 1:TK]
            dead, entry, beyond, chunks, mixed, single, quick_one = (listing[:, 160 + i:161 + i] for i in range(7))
            own.add(dve.tensor_reduce(dead, row_dead[0:TK, :], AX.X, ALU.max))
            own.add(dve.memset(one, 1.0))
            own.wait()
            own.add(dve.tensor_scalar(counts, ps_m[0:TK, SQ:SQ + TK], 0.0, dead, ALU.is_gt, ALU.max))
            own.wait()
            own.add(dve.tensor_tensor_scan(upto, one, counts, 0.0, ALU.mult, ALU.add))
            own.wait()
            own.add(dve.tensor_tensor(place, upto, counts, ALU.mult))
            own.wait()
            own.add(dve.tensor_scalar(place, place, -1.0, None, ALU.add))
            own.wait()
            own.add(dve.scalar_tensor_tensor(found, place, number, numbers, ALU.is_equal, ALU.mult))
            own.add(dve.tensor_scalar(beyond, number, count, float(TK), ALU.is_ge, ALU.mult))
            own.wait()
            own.add(dve.tensor_reduce(entry, found, AX.X, ALU.add))
            own.wait()
            dve.tensor_tensor(entry, entry, beyond, ALU.add).then_inc(entries_ready, 1)
            own.add(dve.tensor_scalar(counts[:, 0:TK // CH], numbers[:, ::CH], count, None, ALU.is_lt))
            own.add(dve.tensor_reduce(mixed, ps_m[0:TK, SQ + TK:SQ + 2 * TK], AX.X, ALU.max))
            own.wait()
            own.add(dve.tensor_reduce(chunks, counts[:, 0:TK // CH], AX.X, ALU.add))
            own.wait()
            own.add(dve.tensor_scalar(single, chunks, 1.0, None, ALU.is_equal))
            own.wait()
            own.add(dve.scalar_tensor_tensor(quick_one, mixed, 0.0, single, ALU.is_equal, ALU.mult))
            own.wait()
            own.add(dve.tensor_tensor(tiles_i[:, TK:TK + 1], chunks[0:1], quick_one[0:1], ALU.subtract))
            own.wait()
            dve.wait_ge(entries_turned, 1)
            dve.tensor_copy(tiles_i[:, 0:TK], ps_a[0:1, 0, 0:TK]).then_inc(tiles_ready, 1)

            def split_q(own):
                dve.wait_ge(q_taken, 4)
                own.add(dve.tensor_tensor(
                    q_full.rearrange("p (u q) -> p u q", u=NU), q_full.rearrange("p (u q) -> p u q", u=NU),
                    q_scale[:, :].unsqueeze(1).to_broadcast([P, NU, SQ]), ALU.mult))
                own.wait()
                dve.tensor_copy(q_slots[:, 0, :], q_full).then_inc(q_slots_ready, 1)
                dve.wait_ge(q_slots_ready, 1)
                own.add(dve.tensor_tensor(q_rest, q_full, q_slots[:, 0, :], ALU.subtract))
                own.wait()
                dve.tensor_copy(q_slots[:, 1, :], q_rest).then_inc(q_slots_ready, 1)
                dve.wait_ge(q_slots_ready, 2)
                dve.tensor_tensor(q_slots[:, 2, :], q_rest, q_slots[:, 1, :], ALU.subtract).then_inc(q_slots_ready, 1)

            step = Chain(dve, cross_own)

            def add_attention(b):
                rows = slice(2 * b, 2 * b + 2)
                dve.wait_ge(att2_full, b + 1)
                dve.wait_ge(pool_own, 2)
                dve.tensor_tensor(x_sb[:, rows, :], x_sb[:, rows, :], ps_m[:, :].rearrange("p (t n) -> p t n", t=2),
                                  ALU.add).then_inc(x2_ready, 1)
                dve.wait_ge(x2_ready, b + 1)
                row_stats(x_sb, rows)

            def invert(at, room, own, done):
                own.wait()
                own.add(dve.reciprocal(inverse[:, :], at[:, D::32]))
                own.wait()
                own.add(dve.tensor_copy(room.rearrange("p (b c) -> p b c", c=32),
                                        inverse[:, :].unsqueeze(2).to_broadcast([P, 16, 32])))
                own.wait()
                dve.transpose(at, room).then_inc(done, 1)

            def quick(s):
                b_on, a_on, k_on, par, _ = parts(s, s)
                v_at, last_at, k_at, first_at = quick_tickets(s)
                w = s - 1
                if s == 0:
                    split_q(step)
                    dve.wait_ge(line_in, 16 * CH)
                    dve.tensor_scalar(mask_row, mask_line, 0.0, -BIG, ALU.is_equal, ALU.mult).then_inc(row_ready, 1)
                    dve.wait_ge(k_act, 1)
                    dve.tensor_tensor(k_rest, k_full, k_slots[:, 0, :], ALU.subtract).then_inc(k_pool, 1)
                    dve.wait_ge(k_act, 2)
                    dve.wait_ge(k_pool, 1)
                    dve.tensor_tensor(k_slots[:, 2, :], k_rest, k_slots[:, 1, :], ALU.subtract).then_inc(k_pool, 1)

                def minus(g):
                    dve.wait_ge(a_max, 32 * w + 16 * g + 18)
                    step.wait()
                    top, neg, rest = (m_quick[:, i, g, :] for i in range(3))
                    step.add(dve.tensor_reduce(top, m_half[:, 16 * g:16 * g + 16].rearrange("p (n c) -> p n c", c=2),
                                               AX.X, ALU.max))
                    step.wait()
                    split = lambda a: a.rearrange("p (t h) -> p t h", t=2)
                    step.add(dve.tensor_scalar(neg, top, -1.0, None, ALU.mult))
                    step.add(dve.tensor_scalar(q_parts[:, g, :, 0, :], split(top), -1.0, None, ALU.mult))
                    step.wait()
                    step.add(dve.tensor_tensor(split(rest), split(neg), q_parts[:, g, :, 0, :], ALU.subtract))
                    step.wait()
                    step.add(dve.tensor_copy(q_parts[:, g, :, 1, :], split(rest)))
                    step.wait()
                    dve.tensor_tensor(q_parts[:, g, :, 2, :], split(rest), q_parts[:, g, :, 1, :], ALU.subtract
                                      ).then_inc(minus_ready, 1)

                def take_rows(u, g, ticket):
                    dve.wait_ge(misc_full, ticket + 1)
                    if u:
                        dve.wait_ge(rows_set[g], 32 * u)
                    dve.tensor_copy(quick_rows[:, g, :], ps_m[0:24, 0:P]).then_inc(misc_taken, 1)

                for i in range(STEPS):
                    if a_on:
                        hh, qt = i // 2, i % 2
                        for c2 in range(2):
                            xx = 2 * i + c2
                            dve.wait_ge(a_scores, 32 * w + xx + 1)
                            if xx == 0:
                                step.wait()
                            at = 16 * (hh // 4) + 8 * qt + 2 * (hh % 4) + c2
                            dve.tensor_reduce(m_half[:, at:at + 1], ps_a[:, c2, :], AX.X, ALU.max).then_inc(a_max, 1)
                    if b_on and i == 2:
                        take_rows(s - 2, 1, last_at)
                    if s >= 3 and i == 3:
                        invert(sums[:, (s - 3) % 2, :], spread, step, sums_out)
                    if a_on and i == 7:
                        minus(0)
                    if a_on and i == 10:
                        take_rows(w, 0, first_at)
                    if a_on and i == 15:
                        minus(1)
                if b_on:
                    dve.wait_ge(pvs, (s - 2) * STEPS + PV0 + STEPS)
                    if s >= 4:
                        dve.wait_ge(normed, s - 3)
                    dve.transpose(sums[:, s % 2, :], ps_o[:, :]).then_inc(kept, 1)
                    dve.tensor_copy(o_acc[:, s - 2, :], ps_o[:, :]).then_inc(o_free, 1)
                    dve.wait_ge(kept, s - 1)
                if s == NU + 1:
                    invert(sums[:, (NU - 1) % 2, :], spread, step, sums_out)
            def before():
                own = Chain(dve, cross_own)
                split_q(own)
                own.add(dve.memset(m_run[:, :, :], -2 * BIG))
                dve.wait_ge(q_stacked, 16 * 6)
                own.add(dve.memset(o_acc[:, :, :], 0.0))
                own.wait()
                dve.wait_ge(neg_col_ready, 1)
                dve.tensor_copy(neg_big_col[:, :], ps_m[:, 0:2]).then_inc(state_ready, 1)

            def start(c):
                dve.wait_ge(masks_in, c * (16 * CH) + 16 * CH)
                dve.wait_ge(pvs, c * (STEPS * NU) + PV0)
                dve.wait_ge(a_max, c * (32 * NU) + 2)
                dve.wait_ge(state_ready, 1)
                dve.scalar_tensor_tensor(bias_kq[:, :, :], mask_in[:, :, 0:SQ], 0.0,
                                         neg_big[:, :].unsqueeze(1).to_broadcast([P, CH, SQ]),
                                         ALU.is_equal, ALU.mult).then_inc(masks_ready, 1)
                for qt in range(2):
                    dve.tensor_scalar(bias_qk[:, qt, :].rearrange("p (j n) -> p j n", j=CH),
                                      mask_in[:, :, SQ + P * qt:SQ + P * qt + P], 0.0, neg_big_col[:, qt:qt + 1],
                                      ALU.is_equal, ALU.mult).then_inc(masks_ready, 1)

            def stage(c, s, k):
                b_on, a_on, k_on, par, _ = parts(s, k)
                cs = c * NU + s
                tk = c * (TICKETS * NU) + tickets_before(s)
                if a_on:
                    w = cs - 1
                    run = m_run[:, bass.ds(s - 1, 1), :].rearrange("p a n -> p (a n)")
                    mo = w * 7
                    if (isinstance(s, int) and s == 1):
                        dve.wait_ge(masks_ready, c * 3 + 4)
                    dve.wait_ge(f_ready, w + 1)
                    dve.wait_ge(a_max, w * 32 + 2)
                    dve.tensor_copy(m_old[:, :], run).then_inc(max_own, 1)
                    for xx in range(32):
                        hh, c2, qt = xx // 4, xx // 2 % 2, xx % 2
                        col = slice(HU * qt + hh, HU * qt + hh + 1)
                        dve.wait_ge(a_scores, w * 32 + xx + 1)
                        dve.wait_ge(a_max, w * 32 + xx + 1)
                        if xx == 0:
                            dve.wait_ge(max_own, mo + 1)
                        bias = bias_qk[:, qt, 512 * c2:512 * c2 + 512]
                        older = (m_cur if c2 else m_old)[:, col]
                        m3 = w * 64 + 2 * xx
                        dve.wait_ge(a_max, w * 32 + xx + 2)
                        dve.tensor_tensor(masked[:, :], ps_a[:, xx % 2, :], bias, ALU.add).then_inc(max_steps, 1)
                        dve.wait_ge(max_steps, m3 + 1)
                        dve.tensor_reduce(m_tile[:, :], masked[:, :], AX.X, ALU.max).then_inc(max_steps, 1)
                        dve.wait_ge(max_steps, m3 + 2)
                        dve.tensor_tensor(m_cur[:, col], m_tile[:, :], older, ALU.max).then_inc(a_max, 1)
                    dve.wait_ge(a_max, w * 32 + 34)
                    by_qt = lambda a: a.rearrange("p (t h) -> p t h", t=2)
                    dve.tensor_scalar(m_neg[:, 0, :], m_cur[:, :], -1.0, None, ALU.mult).then_inc(max_own, 1)
                    dve.tensor_scalar(m_parts[:, :, 0, :], by_qt(m_cur[:, :]), -1.0, None, ALU.mult
                                      ).then_inc(max_own, 1)
                    dve.tensor_copy(run, m_cur[:, :]).then_inc(max_own, 1)
                    dve.wait_ge(max_own, mo + 3)
                    dve.tensor_tensor(by_qt(m_neg[:, 1, :]), by_qt(m_neg[:, 0, :]), m_parts[:, :, 0, :],
                                      ALU.subtract).then_inc(max_own, 1)
                    dve.wait_ge(max_own, mo + 5)
                    dve.tensor_copy(m_parts[:, :, 1, :], by_qt(m_neg[:, 1, :])).then_inc(max_own, 1)
                    dve.wait_ge(max_own, mo + 6)
                    dve.tensor_tensor(m_parts[:, :, 2, :], by_qt(m_neg[:, 1, :]), m_parts[:, :, 1, :], ALU.subtract
                                      ).then_inc(max_own, 1)
                    dve.tensor_tensor(m_diff[:, :].rearrange("p (g t h) -> p g t h", g=2, t=2),
                                      m_old[:, :].rearrange("p (t g h) -> p g t h", g=2, t=2),
                                      m_cur[:, :].rearrange("p (t g h) -> p g t h", g=2, t=2),
                                      ALU.subtract).then_inc(diff_ready, 1)
                    n = tk + 2 + (2 if k_on else 0)
                    dve.wait_ge(misc_full, n + 2)
                    dve.wait_ge(mrow_in, w * 32 + 1)
                    dve.tensor_copy(m_rows[:, :], ps_m[0:48, 0:P]).then_inc(misc_taken, 1)
                if b_on:
                    w = cs - 2
                    acc = o_acc[:, bass.ds(s - 2, 1), :].rearrange("p a n -> p (a n)")
                    n = tk + (2 + 1 if a_on else 0) + (2 if k_on else 0)
                    dve.wait_ge(misc_full, n + 2)
                    dve.tensor_tensor(acc, acc, ps_m[:, :], ALU.mult).then_inc(misc_taken, 1)
                    dve.wait_ge(pvs, w * STEPS + PV0 + STEPS)
                    dve.wait_ge(misc_taken, n + 2)
                    dve.tensor_tensor(acc, acc, ps_o[:, :], ALU.add).then_inc(o_free, 1)

            def end(n):
                dve.wait_ge(o_free, n * NU + 1)
                own = Chain(dve, end_own)
                dve.memset(masked[:, 0:1], 0.0).then_inc(kept, 1)
                dve.wait_ge(kept, 1)
                for u in range(NU):
                    if u >= 2:
                        dve.wait_ge(normed, u - 1)
                    dve.transpose(sums[:, u % 2, :], o_acc[:, u, :]).then_inc(kept, 1)
                    dve.wait_ge(kept, u + 2)
                    invert(sums[:, u % 2, :], spread, own, sums_out)

            cross_attention(dve, quick, stage, before, start, end)
            for b in range(NB):
                dve.wait_ge(att_full, b + 1)
                dve.wait_ge(pool_own, 1)
                dve.tensor_tensor(x_sb[:, 2 * b:2 * b + 2, :], x_sb[:, 2 * b:2 * b + 2, :],
                                  ps_s[:, b % 2, 512:1024].rearrange("p (t n) -> p t n", t=2), ALU.add).then_inc(x1_ready, 1)
                dve.wait_ge(x1_ready, b + 1)
                row_stats(x_sb, slice(2 * b, 2 * b + 2))
                if b % 2:
                    variances(b // 2)
                    normalise(2, b // 2, xn)

            def turn(i):
                t, ps = i % 2, ps_s[:, i % 2, :]
                dve.wait_ge(rot_full, i + 1)
                if i >= 2:
                    dve.wait_ge(parts_act, first(i - 2))
                    dve.wait_ge(rotated, i - 1)
                    dve.wait_ge(rest_done, i - 1)
                elif i == 0:
                    dve.wait_ge(in_late, 96)
                    dve.wait_ge(att_full, NB)
                dve.stream_shuffle(r_swap[t], ps, [c ^ HU for c in range(32)]).then_inc(swapped, 1)
                dve.tensor_tensor(r_full[t].rearrange("p (b q) -> p b q", b=NB), ps.rearrange("p (b q) -> p b q", b=NB),
                                  rope[:, 2 * t, :].unsqueeze(1).to_broadcast([P, NB, SQ]), ALU.mult
                                  ).then_inc(cos_done, 1)

            def rotate(i):
                t = i % 2
                dve.wait_ge(cos_done, i + 1)
                dve.wait_ge(sin_done, i + 1)
                dve.tensor_tensor(r_full[t], r_full[t], r_swap[t], ALU.add).then_inc(rotated, 1)

            def leave_first(i):
                t = i % 2
                dve.wait_ge(parts_act, first(i))
                dve.wait_ge(rotated, i + 1)
                if i >= 2:
                    dve.wait_ge(parts_pool, i - 1)
                dve.tensor_tensor(r_rest[t], r_full[t], r_slots[i][:, 0, :], ALU.subtract).then_inc(rest_done, 1)

            for half in range(2):
                for work_on in (turn, rotate, leave_first):
                    work_on(2 * half)
                    work_on(2 * half + 1)

            by_qt = lambda a: a.rearrange("p (t h) -> p t h", t=2)
            for u in range(NU + 1):
                if u < NU:
                    for y in range(6):
                        dve.wait_ge(self_scores, 6 * u + y + 1)
                        if y == 0 and u:
                            own.wait()
                        at, heads = (4 * y, 4) if y < 2 else (HU + 2 * (y - 2), 2)
                        dve.tensor_reduce(m_cur[:, at:at + heads], ps_a[:, y % 2, :].rearrange("p (h k) -> p h k", h=heads),
                                          AX.X, ALU.max).then_inc(self_max, 1)
                        if y == 3 and u >= 2:
                            invert(t_sums[:, u % 2, :], t_spread, own, t_inverted)
                    dve.wait_ge(self_max, 6 * u + 6)
                    own.add(dve.tensor_scalar(m_neg[:, 0, :], m_cur[:, :], -1.0, None, ALU.mult))
                    if u:
                        dve.wait_ge(rows_full, u)
                    own.add(dve.tensor_scalar(m_parts[:, :, 0, :], by_qt(m_cur[:, :]), -1.0, None, ALU.mult))
                    own.wait()
                    own.add(dve.tensor_tensor(by_qt(m_neg[:, 1, :]), by_qt(m_neg[:, 0, :]), m_parts[:, :, 0, :],
                                              ALU.subtract))
                    own.wait()
                    own.add(dve.tensor_copy(m_parts[:, :, 1, :], by_qt(m_neg[:, 1, :])))
                    own.wait()
                    dve.tensor_tensor(m_parts[:, :, 2, :], by_qt(m_neg[:, 1, :]), m_parts[:, :, 1, :], ALU.subtract
                                      ).then_inc(parts_ready, 1)
                    dve.wait_ge(rows_full, u + 1)
                    if u:
                        dve.wait_ge(rows_in_place, 32 * u)
                    dve.tensor_copy(m_rows[:, :], ps_m[0:48, 0:P]).then_inc(rows_taken, 1)
                if u:
                    w = u - 1
                    if u == NU:
                        invert(t_sums[:, (w - 1) % 2, :], t_spread, own, t_inverted)
                    dve.wait_ge(t_pvs, 4 * w + 4)
                    dve.wait_ge(parts_pool, 4)
                    if w >= 2:
                        dve.wait_ge(self_normed, w - 1)
                    dve.transpose(t_sums[:, w % 2, :], ps_o[:, :]).then_inc(t_out, 1)
                    dve.wait_ge(t_out, w + 1)
                    if u == NU:
                        invert(t_sums[:, w % 2, :], t_spread, own, t_inverted)
                if u == NU:
                    normalise(3, 0, xn_last)
                if u >= NB + 2:
                    add_attention(u - NB - 2)
                if u == NB + 3:
                    variances(0)
            add_attention(NB - 1)
            variances(1)
            normalise(3, 1, xn_last)

            te = lambda k: route[:, k, :, :]
            over_t = lambda a: a.unsqueeze(1).to_broadcast([P, NT, NE])
            over_e = lambda a: a.unsqueeze(2).to_broadcast([P, NT, NE])

            def then(ins):
                own.add(ins)
                own.wait()

            dve.wait_ge(gate_full, 1)
            then(dve.tensor_tensor(te(0), ps_m[:, 0:NT * NE].rearrange("p (t e) -> p t e", t=NT),
                                   over_t(rows_bc[:, 2 * E:2 * E + NE]), ALU.add))
            then(dve.tensor_tensor(te(0), te(0), over_t(rows_bc[:, 2 * E + NE:2 * E + 2 * NE]), ALU.add))
            then(dve.tensor_reduce(route[:, 1, 0, :], te(0), AX.X, ALU.max))
            then(dve.tensor_tensor(te(2), te(0), over_e(route[:, 1, 0, :]), ALU.is_ge))
            rev = cst[:, P + 64:P + 64 + NE]
            then(dve.tensor_tensor(te(2), te(2), over_t(rev), ALU.mult))
            then(dve.tensor_reduce(route[:, 1, 1, :], te(2), AX.X, ALU.max))
            then(dve.tensor_tensor(te(3), over_t(rev), over_e(route[:, 1, 1, :]), ALU.is_equal))
            dve.tensor_copy(route_b[:, :, :], te(3)).then_inc(hot_ready, 1)
            dve.wait_ge(ranks_full, 1)
            total, tiles, upto, base, base_row = (route[:, 6, k, :] for k in range(5))
            then(dve.tensor_reduce(total, ps_m[:, 64:128].rearrange("p (t e) -> p e t", t=NT), AX.X, ALU.add))
            more = route[:, 7, :, 0:NT - 1]
            then(dve.tensor_tensor(more, total.unsqueeze(2).to_broadcast([P, NE, NT - 1]),
                                   cst[:, P + 80:P + 80 + NT - 1].unsqueeze(1).to_broadcast([P, NE, NT - 1]), ALU.is_gt))
            then(dve.tensor_reduce(tiles, more, AX.X, ALU.add))
            own.add(dve.memset(route[:, 6, 5, :], 1.0))
            then(dve.tensor_scalar(tiles, tiles, 1.0, None, ALU.add))
            then(dve.tensor_tensor_scan(upto, route[:, 6, 5, :], tiles, 0.0, ALU.mult, ALU.add))
            then(dve.tensor_tensor(base, upto, tiles, ALU.subtract))
            dve.tensor_copy(runs_i[:, 0:NE], upto[0:1]).then_inc(runs_ready, 1)
            dve.tensor_copy(runs_i[:, NE:2 * NE], base[0:1]).then_inc(runs_ready, 1)
            then(dve.tensor_scalar(base_row, base, float(P), None, ALU.mult))
            dve.wait_ge(ranks_full, 2)
            then(dve.tensor_tensor(te(2), ps_a[:, 0, 0:64].rearrange("p (t e) -> p t e", t=NT), over_t(base_row), ALU.add))
            then(dve.tensor_tensor(te(2), te(2), te(3), ALU.mult))
            then(dve.tensor_reduce(route[:, 1, 2, :], te(2), AX.X, ALU.add))
            dve.tensor_copy(slot_i[:, :], route[:, 1, 2, :]).then_inc(slots_ready, 1)

            dve.wait_ge(b2_in, 16)
            dve.wait_ge(xs_taken, 8)

            def y_out(e, j):
                dve.wait_ge(y_full, j + 2)
                dve.tensor_tensor(y_all[:, bass.ds(j, 1), :].rearrange("p a n -> p (a n)"), ps_o[:, 0:E],
                                  b2_bc[:, e, :], ALU.add).then_inc(y_taken, 1)

            expert_tiles(dve, y_out)
            for t in range(NT):
                dve.wait_ge(gathered[t], 16)
                dve.tensor_tensor(x_sb[:, t, :], x_sb[:, t, :], picked[:, t, :], ALU.add).then_inc(x3_ready, 1)

        @block.scalar
        def _(act):
            act.sem_inc(exps, 2)
            act.sem_inc(misc_taken, 1)
            act.sem_inc(a_max, 2)
            act.sem_inc(pvs, PV0)
            act.sem_inc(o_free, 1)
            act.sem_inc(h_ready, F // P)
            act.sem_inc(y_taken, 1)
            act.sem_inc(y_full, 1)

            def deviations(n, half):
                act.wait_ge(ln_var, 2 * n - 1 + half)
                act.wait_ge(const_ready, 1)
                at = ln_r[:, 4 * half:4 * half + 4]
                act.activation(at, at, ACT.Sqrt, bias=eps_sb[:, 0:1]).then_inc(ln_std, 1)

            def take_rows(n, half):
                for k in range(KE):
                    act.wait_ge(xt_full, 4 * (n - 1) + 2 * half + k + 1)
                    at = 1024 * k + 512 * half
                    act.copy((xn_t if n < 3 else xn_t_last)[:, k, 512 * half:512 * half + 512], ps_t[:, at:at + 512]
                             ).then_inc(xt_taken, 1)

            deviations(1, 0)
            deviations(1, 1)
            take_rows(1, 0)
            take_rows(1, 1)
            for i in range(4):
                act.wait_ge(q_proj, i + 1)
                if i == 0:
                    act.wait_ge(in_w, 48)
                src = [ps_a[:, 1, :], ps_o[:, :], ps_t[:, 512:1024], ps_t[:, 0:512]][i]
                act.activation(q_full[:, 512 * i:512 * i + 512], src, ACT.Identity,
                               bias=bias_sb[:, i // 2:i // 2 + 1]).then_inc(q_taken, 1)

            def stage(c, s, k):
                b_on, a_on, k_on, par, _ = parts(s, k)
                cs = c * NU + s
                tk = c * (TICKETS * NU) + tickets_before(s)

                def v_out(i):
                    act.wait_ge(misc_full, tk + i + 2)
                    if i == 0:
                        act.wait_ge(pvs, cs * STEPS)
                    act.copy(v_sb[:, 1 - par, 4 * i:4 * i + 4, :, 0:D],
                             ps_m[:, :].rearrange("p (j h d) -> p j h d", j=4, h=HU)).then_inc(misc_taken, 1)

                def k_out(i):
                    act.wait_ge(misc_full, tk + (2 if a_on else 0) + i + 2)
                    act.wait_ge(k_pool, cs * 2 + 1)
                    act.activation(k_full[:, 512 * i:512 * i + 512], ps_m[:, :], ACT.Identity,
                                   bias=bias_sb[:, 2 + par:3 + par]).then_inc(misc_taken, 1)

                def k_first():
                    act.wait_ge(misc_taken, tk + (2 if a_on else 0) + 3)
                    act.wait_ge(k_low, cs * 96 + 1)
                    act.wait_ge(k_high, cs * 96 + 1)
                    act.copy(k_slots[:, 0, :], k_full).then_inc(k_act, 1)

                def k_second():
                    act.wait_ge(k_pool, cs * 2 + 2)
                    act.copy(k_slots[:, 1, :], k_rest).then_inc(k_act, 1)

                def factor():
                    act.wait_ge(diff_ready, cs)
                    act.activation(f_bc[:, 1 - par, :, :], m_diff[:, :].unsqueeze(2).to_broadcast([P, 16, 32]),
                                   ACT.Exp).then_inc(f_ready, 1)

                for i in range(STEPS):
                    if b_on:
                        w = cs - 2
                        act.wait_ge(scores, w * STEPS + i + 1)
                        act.wait_ge(pvs, w * STEPS + PV0 + i - 1)
                        act.activation(probs[:, i % 2, :], ps_s[:, i % 2, :], ACT.Exp).then_inc(exps, 1)
                    if a_on and i < 2:
                        v_out(i)
                    if k_on and i in (6, 7):
                        k_out(i - 6)
                    if k_on and i == 8:
                        k_first()
                    if k_on and i == 11:
                        k_second()
                    if a_on and i == 14:
                        factor()

            def add_bv(u):
                act.wait_ge(normed, u + 1)
                for g in range(2):
                    at = o_acc[:, u, SQ * g:SQ * g + SQ]
                    act.activation(at, at, ACT.Identity, bias=bias_sb[:, 4 + u % 2 * 2 + g:5 + u % 2 * 2 + g]
                                   ).then_inc(att_in, 1)

            def take_v(u, i, ticket):
                act.wait_ge(misc_full, ticket + i + 1)
                if i == 0:
                    act.wait_ge(pvs, (u + 1) * STEPS)
                act.copy(v_sb[:, u % 2, 4 * i:4 * i + 4, :, 0:D],
                         ps_m[:, :].rearrange("p (j h d) -> p j h d", j=4, h=HU)).then_inc(misc_taken, 1)

            def quick(s):
                b_on, a_on, k_on, par, _ = parts(s, s)
                v_at, last_at, k_at, first_at = quick_tickets(s)
                if s == 0:
                    for j in range(CH // 2, CH):
                        load_ctx_tile(act, 0, j, act.value_load(tiles_i[0:1, j:j + 1], min_val=0, max_val=TK),
                                      ctx_rest_in)
                for i in range(STEPS):
                    if b_on:
                        act.wait_ge(scores, (s - 2) * STEPS + i + 1)
                        act.wait_ge(pvs, (s - 2) * STEPS + PV0 + i - 1)
                        act.activation(probs[:, i % 2, :], ps_s[:, i % 2, :], ACT.Exp).then_inc(exps, 1)
                    if a_on and s > 1 and i < 2:
                        take_v(s - 1, i, v_at)
                    if k_on and i in (3, 4):
                        act.wait_ge(misc_full, k_at + i - 2)
                        if s:
                            act.wait_ge(k_pool, 2 * s)
                        act.activation(k_full[:, 512 * (i - 3):512 * (i - 3) + 512], ps_m[:, :], ACT.Identity,
                                       bias=bias_sb[:, 2 + par:3 + par]).then_inc(misc_taken, 1)
                    if k_on and i == 5:
                        act.wait_ge(misc_taken, k_at + 3)
                        if s:
                            act.wait_ge(k_low, 96 * s)
                            act.wait_ge(k_high, 96 * s)
                        act.copy(k_slots[:, 0, :], k_full).then_inc(k_act, 1)
                    if k_on and i == 7:
                        act.wait_ge(k_pool, 2 * s + 1)
                        act.copy(k_slots[:, 1, :], k_rest).then_inc(k_act, 1)
                    if s == 0 and i in (8, 9):
                        take_v(0, i - 8, v_at)
                    if s >= 4 and i == 2:
                        add_bv(s - 4)
                if s == NU + 1:
                    add_bv(NU - 2)
                    add_bv(NU - 1)

            def before():
                act.wait_ge(state_ready, 1)
                for done in (masks_ready, misc_full, k_low, k_high, k_act, k_pool, mrow_in, f_ready):
                    act.sem_inc(done, 1)

            def end(n):
                for u in range(NU):
                    add_bv(u)

            cross_attention(act, quick, stage, before, None, end)

            def keep(u):
                act.wait_ge(t_out, u + 1)
                act.copy(o_acc[:, u, :], ps_o[:, :]).then_inc(t_kept, 1)

            deviations(2, 0)
            take_rows(2, 0)
            deviations(2, 1)
            take_rows(2, 1)
            def v_out(t):
                act.wait_ge(v_full, t + 1)
                act.copy(v_sb.rearrange("p a t h c -> p a t (h c)")[:, :, t, :].rearrange(
                    "p a (h c) -> p a h c", c=SLOT)[:, :, :, 0:D],
                         ps_a[:, t % 2, 0:E].rearrange("p (a h c) -> p a h c", a=2, h=HU)).then_inc(v_taken, 1)

            def first_part(i):
                act.wait_ge(rotated, i + 1)
                act.copy(r_slots[i][:, 0, :], r_full[i % 2]).then_inc(parts_act, 1)

            def second_part(i):
                act.wait_ge(rest_done, i + 1)
                act.copy(r_slots[i][:, 1, :], r_rest[i % 2]).then_inc(parts_act, 1)

            for half in range(2):
                for t in range(4 * half, 4 * half + 4):
                    v_out(t)
                for work_on in (first_part, second_part):
                    work_on(2 * half)
                    work_on(2 * half + 1)
            for u in range(NU):
                if u:
                    keep(u - 1)
                for i in range(4):
                    act.wait_ge(t_scores, 4 * u + i + 1)
                    if 4 * u + i >= 2:
                        act.wait_ge(t_pvs, 4 * u + i - 1)
                    n = 4 * SQ if i % 2 == 0 else 4 * P
                    act.activation(probs[:, i % 2, 0:n], ps_s[:, i % 2, 0:n], ACT.Exp).then_inc(t_exps, 1)
            deviations(3, 0)
            keep(NU - 1)
            take_rows(3, 0)
            deviations(3, 1)
            take_rows(3, 1)
            runs = expert_runs(act)
            for r in range(8):
                n = P * min(2, SLOTS - 2 * r)
                act.wait_ge(xs_full, r + 1)
                act.copy(xs_t[:, :, SQ * r:SQ * r + n],
                         ps_t[:, 512 * (r % 4):512 * (r % 4) + 512].rearrange("p (k n) -> p k n", k=KE)[:, :, 0:n]
                         ).then_inc(xs_taken, 1)

            def relu(e, j):
                for c in range(F // P):
                    if c % 2 == 0:
                        act.wait_ge(h_full, j * (F // P) + c + 2)
                    if c == 0:
                        act.wait_ge(y_full, j + 1)
                    act.activation(hidden[:, c, :], ps_t[:, 256 * c:256 * c + P], ACT.Relu, bias=b1_sb[:, e, c:c + 1]
                                   ).then_inc(h_ready, 1)

            expert_tiles(act, relu, runs)

        @block.gpsimd
        def _(pool):
            pool.memset(zeros[:, :], 0.0).then_inc(zero_ready, 1)
            pool.memset(v_sb[:, :, :, :, D:SLOT], 1.0).then_inc(v_ones, 1)
            pool.wait_ge(xn_ready, NT)
            pool.wait_ge(in_w, 48)
            def add_row(k):
                pool.tensor_tensor(x_sb[:, :, :], x_sb[:, :, :],
                                   rows_bc[:, E * k:E * k + E].unsqueeze(1).to_broadcast([P, NT, E]),
                                   ALU.add).then_inc(pool_own, 1)

            add_row(0)

            def stage(c, s, k):
                b_on, a_on, k_on, par, _ = parts(s, k)
                cs = c * NU + s
                if k_on:
                    credit = 0 if isinstance(c, int) else 1
                    pool.wait_ge(k_act, cs * 2 + 1 + credit)
                    pool.wait_ge(k_pool, cs * 2 + credit)
                    pool.tensor_tensor(k_rest, k_full, k_slots[:, 0, :], ALU.subtract).then_inc(k_pool, 1)
                    pool.wait_ge(k_act, cs * 2 + 2 + credit)
                    pool.wait_ge(k_pool, cs * 2 + 1 + credit)
                    pool.tensor_tensor(k_slots[:, 2, :], k_rest, k_slots[:, 1, :], ALU.subtract).then_inc(k_pool, 1)

            def divide(u):
                pool.wait_ge(sums_out, u + 1)
                pool.wait_ge(o_free, u + 2)
                pool.tensor_tensor(o_acc[:, u, :], o_acc[:, u, :], sums[:, u % 2, :], ALU.mult).then_inc(normed, 1)

            def quick(s):
                if s:
                    stage(0, s, s)
                if s >= 3:
                    divide(s - 3)
                if s == NU + 1:
                    divide(NU - 1)

            def end(n):
                for u in range(NU):
                    divide(u)

            cross_attention(pool, quick, stage, None, None, end)
            pool.wait_ge(xn_ready, 2 * NT)
            add_row(1)
            def sines(i):
                t = i % 2
                pool.wait_ge(swapped, i + 1)
                pool.tensor_tensor(r_swap[t].rearrange("p (b q) -> p b q", b=NB),
                                   r_swap[t].rearrange("p (b q) -> p b q", b=NB),
                                   rope[:, 2 * t + 1, :].unsqueeze(1).to_broadcast([P, NB, SQ]), ALU.mult
                                   ).then_inc(sin_done, 1)

            def third_part(i):
                pool.wait_ge(parts_act, second(i))
                pool.wait_ge(rest_done, i + 1)
                pool.tensor_tensor(r_slots[i][:, 2, :], r_rest[i % 2], r_slots[i][:, 1, :], ALU.subtract
                                   ).then_inc(parts_pool, 1)

            for half in range(2):
                for work_on in (sines, third_part):
                    work_on(2 * half)
                    work_on(2 * half + 1)
            for u in range(NU):
                pool.wait_ge(t_inverted, u + 1)
                pool.wait_ge(t_kept, u + 1)
                pool.tensor_tensor(o_acc[:, u, :], o_acc[:, u, :], t_sums[:, u % 2, :], ALU.mult
                                   ).then_inc(self_normed, 1)
            pool.wait_ge(slots_ready, 1)
            pool.wait_ge(xs_zeroed, 32 * SLOTS // 3)
            pool.wait_ge(xn_ready, 3 * NT)
            for t in range(NT):
                pool.indirect_dma_start(xs_dram, bass.IndirectOffsetOnAxis(ap=slot_i[:, t:t + 1], axis=0),
                                        xn_last[:, t, :], None).then_inc(scattered, 16)
            pool.wait_ge(runs_ready, 2)
            n = pool.value_load(runs_i[0:1, NE - 1:NE], min_val=NE, max_val=SLOTS)
            pool.wait_ge(ys_stored, n * 16)
            pool.tensor_tensor(m_neg[:, 0, :], m_neg[:, 1, :], m_neg[:, 1, :], ALU.add).then_inc(pool_own, 1)
            pool.wait_ge(pool_own, 3)
            for t in range(NT):
                pool.indirect_dma_start(picked[:, t, :], None, ys_dram,
                                        bass.IndirectOffsetOnAxis(ap=slot_i[:, t:t + 1], axis=0)).then_inc(gathered[t], 16)

        @block.tensor
        def _(pe):
            pe.wait_ge(const_ready, 1)

            def turn_rows(n, half):
                pe.wait_ge(xn_ready, NT * (n - 1) + 4 * half + 4)
                for k in range(KE):
                    for t in range(4 * half, 4 * half + 4):
                        mm = pe.transpose(ps_t[:, 1024 * k + P * t:1024 * k + P * t + P],
                                          (xn if n < 3 else xn_last)[:, t, P * k:P * k + P], ident_f)
                    mm.then_inc(xt_full, 1)

            turn_rows(1, 0)
            turn_rows(1, 1)
            for t in range(TK):
                pe.wait_ge(nz_ready, t + 1)
                pe.matmul(ps_m[:, 0:SQ], ones_b[:, :], mask_nz[:, t, :], start=(t == 0), stop=(t == TK - 1))
            pe.wait_ge(any_ready, 2)
            pe.matmul(ps_m[:, SQ:SQ + 2 * TK], ones_b[:, :], tile_any_b[:, :], start=True, stop=True).then_inc(counts_ready, 1)
            pe.wait_ge(in_w, 48)
            pe.wait_ge(xt_taken, 4)
            for i in range(4):
                half, bb = i // 2, i % 2
                dst = [ps_a[:, 1, :], ps_o[:, :], ps_t[:, 512:1024], ps_t[:, 0:512]][i]
                for k in range(KE):
                    mm = pe.matmul(dst, w_sb[:, 0, k, P * half:P * half + P], xn_t[:, k, 512 * bb:512 * bb + 512],
                                   start=(k == 0), stop=(k == KE - 1))
                mm.then_inc(q_proj, 1)
                if i == 1:
                    pe.wait_ge(entries_ready, 1)
                    pe.matmul(ps_a[0:1, 0, 0:TK], listing[:, 161:162], ident_f[0:TK, 0:TK], start=True, stop=True
                              ).then_inc(entries_turned, 1)
            pe.wait_ge(neg_ready, 1)

            def quick(s):
                b_on, a_on, k_on, par, _ = parts(s, s)
                v_at, last_at, k_at, first_at = quick_tickets(s)
                wa, wb = s - 1, s - 2
                at_a, at_b = wa % 2 * NB + wa // 2, wb % 2 * NB + wb // 2

                def take(ticket):
                    pe.wait_ge(misc_taken, ticket + 1)

                def turn_maxima(u, g, ticket):
                    pe.wait_ge(minus_ready, 2 * u + g + 1)
                    take(ticket)
                    pe.matmul(ps_m[0:24, 0:P], q_parts[:, g, :, :, :].rearrange("p t a h -> p (t a h)"), ident_b[:, :],
                              start=True, stop=True).then_inc(misc_full, 1)

                def make_k(i):
                    if i == 0 and par == 0:
                        pe.wait_ge(ctx_in_of[s // 2 % 2], (64, 128, 192, 256)[s // 2])
                    if i == 1 and s == 0:
                        pe.wait_ge(ctx_rest_in, 64)
                    take(k_at + i)
                    for kk in range(KE):
                        mm = pe.matmul(ps_m[:, :], w_sb[:, 1, kk, P * par:P * par + P],
                                       ctx_of[s // 2 % 2][:, 4 * i:4 * i + 4, kk, :],
                                       start=(kk == 0), stop=(kk == KE - 1))
                    mm.then_inc(misc_full, 1)

                def make_v(u, i, ticket):
                    take(ticket + i)
                    for j in range(4 * i, 4 * i + 4):
                        for kk in range(KE):
                            mm = pe.matmul(ps_m[:, P * (j % 4):P * (j % 4) + P], ctx_of[u // 2 % 2][:, j, kk, :],
                                           w_sb[:, 2, kk, P * (u % 2):P * (u % 2) + P],
                                           start=(kk == 0), stop=(kk == KE - 1))
                    mm.then_inc(misc_full, 1)

                def sums_of(i):
                    g, j = i // CH, i % CH
                    if i == 0:
                        pe.wait_ge(o_free, wb + 1)
                        if wb:
                            pe.wait_ge(kept, wb)
                        else:
                            pe.wait_ge(v_ones, 1)
                    pe.wait_ge(exps, wb * STEPS + i + 3)
                    for h4 in range(4):
                        mm = pe.matmul(ps_o[32 * h4:32 * h4 + 32, SQ * g:SQ * g + SQ],
                                       v_sb[:, par, j, 4 * g + h4, :], probs[:, i % 2, SQ * h4:SQ * h4 + SQ],
                                       start=(j == 0), stop=(j == CH - 1), tile_position=(0, 32 * h4),
                                       skip_group_check=True)
                    mm.then_inc(pvs, 1)

                if s == 1:
                    make_k(0)
                    make_k(1)
                for i in range(STEPS):
                    if b_on:
                        g, j = i // CH, i % CH
                        if j == 0:
                            pe.wait_ge(rows_set[g], 32 * wb + 32)
                        pe.wait_ge(exps, wb * STEPS + i + 1)
                        for h4 in range(4):
                            mm = pe.matmul(ps_s[:, i % 2, SQ * h4:SQ * h4 + SQ],
                                           k_stack[0:ROWS, par, 4 * g + h4, P * j:P * j + P],
                                           q_stack[0:ROWS, 4 * g + h4, at_b, :], start=True, stop=True)
                        mm.then_inc(scores, 1)
                    if a_on:
                        hh, qt = i // 2, i % 2
                        if i == 0:
                            pe.wait_ge(k_low, 96 * wa + 96)
                            if s == 1:
                                pe.wait_ge(q_stacked, 16 * 6)
                                pe.wait_ge(mask_set, 16)
                        if i == CH:
                            pe.wait_ge(k_high, 96 * wa + 96)
                        for c2 in range(2):
                            pe.wait_ge(a_max, 32 * wa + 2 * i + c2 + 1)
                            pe.matmul(ps_a[:, c2, :], q_stack[0:PAIR + 1, hh, at_a, P * qt:P * qt + P],
                                      k_stack[0:PAIR + 1, 1 - par, hh, 512 * c2:512 * c2 + 512],
                                      start=True, stop=True).then_inc(a_scores, 1)
                    if b_on and i:
                        sums_of(i - 1)
                    if a_on and s > 1 and i < 2:
                        make_v(wa, i, v_at)
                    if s == 0 and i in (5, 6):
                        make_v(0, i - 5, v_at)
                    if b_on and i == 2:
                        turn_maxima(wb, 1, last_at)
                    if k_on and s != 1 and i in (3, 4):
                        make_k(i - 3)
                    if a_on and i == 10:
                        turn_maxima(wa, 0, first_at)
                if b_on:
                    sums_of(STEPS - 1)

            def stage(c, s, k):
                b_on, a_on, k_on, par, _ = parts(s, k)
                cs = c * NU + s
                tk = c * (TICKETS * NU) + tickets_before(s)
                if isinstance(s, int):
                    at_a = (s - 1) % 2 * NB + (s - 1) // 2
                    at_b = (s - 2) % 2 * NB + (s - 2) // 2
                elif k == 0:
                    at_a, at_b = s // 2 + (NB - 1), s // 2 - 1
                else:
                    at_a, at_b = (s - 1) // 2, (s - 1) // 2 + (NB - 1)
                n = tk

                def fill(n, mm_of):
                    pe.wait_ge(misc_taken, n + 1)
                    mm_of().then_inc(misc_full, 1)

                def v_mm(i):
                    def go():
                        for j in range(4 * i, 4 * i + 4):
                            for kk in range(KE):
                                mm = pe.matmul(ps_m[:, P * (j % 4):P * (j % 4) + P], ctx_sb[:, j, kk, :],
                                               w_sb[:, 2, kk, P * (1 - par):P * (1 - par) + P],
                                               start=(kk == 0), stop=(kk == KE - 1))
                        return mm
                    return go

                def k_mm(i):
                    def go():
                        for kk in range(KE):
                            mm = pe.matmul(ps_m[:, :], w_sb[:, 1, kk, P * par:P * par + P],
                                           ctx_sb[:, 4 * i:4 * i + 4, kk, :], start=(kk == 0), stop=(kk == KE - 1))
                        return mm
                    return go

                def a_mm(xx):
                    hh, c2, qt = xx // 4, xx // 2 % 2, xx % 2
                    w = cs - 1
                    if xx == 0:
                        pe.wait_ge(k_low, w * 96 + 97)
                    if xx == 16:
                        pe.wait_ge(k_high, w * 96 + 97)
                    pe.wait_ge(a_max, w * 32 + xx + 1)
                    pe.matmul(ps_a[:, xx % 2, :],
                              q_stack[0:PAIR, hh, bass.ds(at_a, 1), P * qt:P * qt + P].rearrange("p a q -> p (a q)"),
                              k_stack[0:PAIR, 1 - par, hh, 512 * c2:512 * c2 + 512],
                              start=True, stop=True).then_inc(a_scores, 1)

                def s_mm(i):
                    g, j = i // CH, i % CH
                    w = cs - 2
                    if i == 0:
                        pe.wait_ge(mrow_in, w * 32 + 33)
                        pe.wait_ge(masks_ready, c * 3 + 2)
                    pe.wait_ge(exps, w * STEPS + i + 1)
                    for h4 in range(4):
                        if h4 % 2 == 0:
                            pe.matmul(ps_s[:, i % 2, SQ * h4:SQ * (h4 + 2)], ident_b[:, :],
                                      bias_kq[:, j:j + 1, :].to_broadcast([P, 2, SQ]),
                                      start=True, stop=False, skip_group_check=True)
                        mm = pe.matmul(ps_s[:, i % 2, SQ * h4:SQ * h4 + SQ],
                                       k_stack[0:ROWS, par, 4 * g + h4, P * j:P * j + P],
                                       q_stack[0:ROWS, 4 * g + h4, bass.ds(at_b, 1), :].rearrange("p a q -> p (a q)"),
                                       start=False, stop=h4 % 2 == 1, skip_group_check=True)
                    mm.then_inc(scores, 1)

                def pv_mm(i):
                    g, j = i // CH, i % CH
                    w = cs - 2
                    if i == 0:
                        pe.wait_ge(o_free, w + 1)
                    pe.wait_ge(exps, w * STEPS + i + 3)
                    for h4 in range(4):
                        mm = pe.matmul(ps_o[32 * h4:32 * h4 + 32, SQ * g:SQ * g + SQ],
                                       v_sb[:, par, j, 4 * g + h4, :], probs[:, i % 2, SQ * h4:SQ * h4 + SQ],
                                       start=(j == 0), stop=(j == CH - 1), tile_position=(0, 32 * h4),
                                       skip_group_check=True)
                    mm.then_inc(pvs, 1)

                def m_mm():
                    pe.wait_ge(max_own, (cs - 1) * 7 + 7)
                    return pe.matmul(ps_m[0:48, 0:P], m_parts[:, :, :, :].rearrange("p t a h -> p (t a h)"), ident_b[:, :],
                                     start=True, stop=True)

                def f_mm():
                    pe.wait_ge(f_ready, cs)
                    for gt in range(4):
                        mm = pe.matmul(ps_m[:, P * gt:P * gt + P],
                                       f_bc[:, par, 4 * gt:4 * gt + 4, :].rearrange("p h r -> p (h r)"), ident_f,
                                       start=True, stop=True)
                    return mm

                for i in range(STEPS):
                    if b_on:
                        s_mm(i)
                    if a_on:
                        for xx in range(3 * i, min(3 * i + 3, 32)):
                            a_mm(xx)
                    if b_on and i:
                        pv_mm(i - 1)
                    if a_on and i < 2:
                        fill(n, v_mm(i))
                        n = n + 1
                    if k_on and i in (6, 7):
                        if i == 6 and par == 0:
                            bt = c * NB + s // 2
                            pe.wait_ge(ctx_in, bt * 128 + 128)
                        fill(n, k_mm(i - 6))
                        n = n + 1
                    if a_on and i == 13:
                        fill(n, m_mm)
                        n = n + 1
                    if b_on and i == 14:
                        fill(n, f_mm)
                        n = n + 1
                if b_on:
                    pv_mm(STEPS - 1)

            def before():
                for qt in range(2):
                    mm = pe.matmul(ps_m[:, qt:qt + 1], neg_big[0:1, P * qt:P * qt + P], cst[0:1, 2 * P - 1:2 * P],
                                   start=True, stop=True)
                mm.then_inc(neg_col_ready, 1)
                pe.wait_ge(state_ready, 1)
                pe.wait_ge(q_stacked, 16 * 6)
                pe.wait_ge(edges_set, 32)
                pe.wait_ge(v_ones, 1)

            cross_attention(pe, quick, stage, before)
            for b in range(NB):
                pe.wait_ge(att_in, 4 * b + 4)
                if b >= 2:
                    pe.wait_ge(x1_ready, b - 1)
                for qt in range(2):
                    for hg in range(4):
                        mm = pe.matmul(ps_s[:, b % 2, 512 + E * qt:512 + E * qt + E],
                                       o_acc[:, 2 * b + hg // 2, SQ * (hg % 2) + P * qt:SQ * (hg % 2) + P * qt + P],
                                       wo_sb[:, 0, hg, :], start=(hg == 0), stop=(hg == 3))
                mm.then_inc(att_full, 1)

            def rotated_mm(i, bb):
                half, t = i // 2, i % 2
                for k in range(KE):
                    mm = pe.matmul(ps_s[:, i % 2, 512 * bb:512 * bb + 512],
                                   w_qkv[:, k, E * t + P * half:E * t + P * half + P],
                                   xn_t[:, k, 512 * bb:512 * bb + 512], start=(k == 0), stop=(k == KE - 1))
                return mm

            turn_rows(2, 0)
            pe.wait_ge(xt_taken, 6)
            pe.wait_ge(in_late, 96)
            rotated_mm(0, 0)
            rotated_mm(1, 0)
            pe.wait_ge(x1_ready, NB)
            turn_rows(2, 1)
            pe.wait_ge(xt_taken, 8)
            for i in range(4):
                if i >= 2:
                    pe.wait_ge(swapped, i - 1)
                    pe.wait_ge(cos_done, i - 1)
                    rotated_mm(i, 0)
                mm = rotated_mm(i, 1)
                mm.then_inc(rot_full, 1)
                if i % 2 == 1:
                    for tt in range(4 * (i // 2), 4 * (i // 2) + 4):
                        if tt >= 2:
                            pe.wait_ge(v_taken, tt - 1)
                        for k in range(KE):
                            mm = pe.matmul(ps_a[:, tt % 2, 0:E], xn_t[:, k, P * tt:P * tt + P],
                                           w_qkv[:, k, 2 * E:3 * E], start=(k == 0), stop=(k == KE - 1))
                        mm.then_inc(v_full, 1)
            pe.wait_ge(v_taken, NT)
            pe.wait_ge(cos_done, 4)
            pe.wait_ge(swapped, 4)

            mask_qk, mask_kq = causal[:, 0, 0:1, 0:P], causal[:, 1, 0:1, 0:P]

            def self_max_scores(u, y):
                half, b = u // NB, u % NB
                if b == 0 and y == 0:
                    pe.wait_ge(stacked[half], 16 * 12 + (16 if half == 0 else 0))
                if 6 * u + y >= 2:
                    pe.wait_ge(self_max, 6 * u + y - 1)
                qt = 0 if y < 2 else 1
                heads = range(4 * y, 4 * y + 4) if qt == 0 else range(2 * (y - 2), 2 * (y - 2) + 2)
                keys = P * (qt + 1)
                last = ps_a[:, y % 2, :].rearrange("p (h k) -> p h k", k=keys)[:, :, P * qt:keys]
                pe.matmul(last, ident_b[:, :], mask_qk.to_broadcast([P, len(heads), P]),
                          start=True, stop=False, skip_group_check=True)
                for i, hh in enumerate(heads):
                    mm = pe.matmul(ps_a[:, y % 2, keys * i:keys * i + keys],
                                   q_stack[0:PAIR, hh, u, P * qt:P * qt + P],
                                   k_stack[0:PAIR, half, hh, SQ * b:SQ * b + keys],
                                   start=False, stop=hh == heads[-1], skip_group_check=True)
                mm.then_inc(self_scores, 1)

            def self_sums(u, i):
                half, b, g, j = u // NB, u % NB, i // 2, i % 2
                if i == 0:
                    pe.wait_ge(rows_in_place, 32 * u + 32)
                if 4 * u + i >= 2:
                    pe.wait_ge(t_exps, 4 * u + i - 1)
                n = SQ - P * j
                for h4 in range(4):
                    if h4 % (2 if j == 0 else 4) == 0:
                        at = ps_s[:, i % 2, 512 * (h4 // 2):512 * (h4 // 2) + 512].rearrange("p (h q) -> p h q", q=n)
                        pe.matmul(at[:, :, 0:P], ident_b[:, :], mask_kq.to_broadcast([P, 512 // n, P]),
                                  start=True, stop=False, skip_group_check=True)
                    mm = pe.matmul(ps_s[:, i % 2, n * h4:n * h4 + n],
                                   k_stack[0:ROWS, half, 4 * g + h4, SQ * b + P * j:SQ * b + P * j + P],
                                   q_stack[0:ROWS, 4 * g + h4, u, P * j:SQ],
                                   start=False, stop=h4 == 3 or j == 0 and h4 == 1, skip_group_check=True)
                mm.then_inc(t_scores, 1)

            def self_pv(u, i):
                half, b, g, j = u // NB, u % NB, i // 2, i % 2
                if i == 0 and u:
                    pe.wait_ge(t_out, u)
                    pe.wait_ge(t_kept, u)
                pe.wait_ge(t_exps, 4 * u + i + 1)
                n = SQ - P * j
                for h4 in range(4):
                    mm = pe.matmul(ps_o[32 * h4:32 * h4 + 32, SQ * g + P * j:SQ * g + SQ],
                                   v_sb[:, half, 2 * b + j, 4 * g + h4, :], probs[:, i % 2, n * h4:n * h4 + n],
                                   start=(j == 0), stop=(j == 1), tile_position=(0, 32 * h4), skip_group_check=True)
                mm.then_inc(t_pvs, 1)

            def self_output(b):
                pe.wait_ge(self_normed, NB + b + 1)
                pe.wait_ge(rows_taken, min(NU, NB + b + 3))
                if b:
                    pe.wait_ge(x2_ready, b)
                for qt in range(2):
                    for hg in range(4):
                        mm = pe.matmul(ps_m[:, E * qt:E * qt + E],
                                       o_acc[:, hg // 2 * NB + b, SQ * (hg % 2) + P * qt:SQ * (hg % 2) + P * qt + P],
                                       wo_sb[:, 1, hg, :], start=(hg == 0), stop=(hg == 3))
                mm.then_inc(att2_full, 1)

            for u in range(NU + 1):
                steps = ((0,1,2,3),(4,5),(),())
                for i in range(4):
                    if u < NU:
                        for y in steps[i]:
                            self_max_scores(u, y)
                    if u:
                        self_sums(u - 1, i)
                    if i == 3 and u < NU:
                        pe.wait_ge(parts_ready, u + 1)
                        if u:
                            pe.wait_ge(rows_taken, u)
                        if u > NB + 2:
                            pe.wait_ge(x2_ready, u - NB - 2)
                        pe.matmul(ps_m[0:48, 0:P], m_parts[:, :, :, :].rearrange("p t a h -> p (t a h)"), ident_b[:, :],
                                  start=True, stop=True).then_inc(rows_full, 1)
                    if u and i:
                        self_pv(u - 1, i - 1)
                if u:
                    self_pv(u - 1, 3)
                if u >= NB + 2:
                    self_output(u - NB - 2)
            self_output(NB - 1)

            for half in range(2):
                turn_rows(3, half)
                pe.wait_ge(xt_taken, 10 + 2 * half)
                pe.wait_ge(x2_ready, NB)
                for t in range(4 * half, 4 * half + 4):
                    for k in range(KE):
                        mm = pe.matmul(ps_m[:, NE * t:NE * t + NE], xn_t_last[:, k, P * t:P * t + P], gate_sb[:, k, :],
                                       start=(k == 0), stop=(k == KE - 1))
            mm.then_inc(gate_full, 1)
            pe.wait_ge(hot_ready, 1)
            hot = route_b[:, :, :].rearrange("p t e -> p (t e)")
            pe.matmul(ps_m[:, 64:128], ones_b[:, :], hot, start=True, stop=True).then_inc(ranks_full, 1)
            pe.matmul(ps_a[:, 0, 0:64], lower_b[:, :], hot, start=True, stop=False, skip_group_check=True)
            for t in range(NT - 1):
                mm = pe.matmul(ps_a[:, 0, NE * (t + 1):NE * NT], ones_b[:, :],
                               route_b[:, t:t + 1, :].to_broadcast([P, NT - 1 - t, NE]),
                               start=False, stop=t == NT - 2, skip_group_check=True)
            mm.then_inc(ranks_full, 1)
            runs = expert_runs(pe)
            for r in range(8):
                for t in range(2 * r, min(2 * r + 2, SLOTS)):
                    if t % 5 == 0:
                        pe.wait_ge(xs_loaded[t // 5], 16)
                    if t == 2 * r and r >= 4:
                        pe.wait_ge(xs_taken, r - 3)
                    for k in range(KE):
                        mm = pe.transpose(ps_s[:, r % 4 // 2, 512 * (r % 2) + SQ * k + P * (t % 2):
                                               512 * (r % 2) + SQ * k + P * (t % 2) + P],
                                          xs_in[:, t, P * k:P * k + P], ident_f)
                mm.then_inc(xs_full, 1)
            pe.wait_ge(xs_taken, 8)

            def expert(e, j):
                for c in range(F // P):
                    if c == 0:
                        pe.wait_ge(w_in[e], 64)
                    if c % 2 == 0:
                        pe.wait_ge(h_ready, j * (F // P) + c + 2)
                    for k in range(KE):
                        mm = pe.matmul(ps_t[:, 256 * c:256 * c + P], w1_sb[e][:, k, P * c:P * c + P],
                                       xs_t[:, k, bass.ds(j * P, P)], start=(k == 0), stop=(k == KE - 1))
                    mm.then_inc(h_full, 1)
                for c in range(F // P):
                    if c == 0:
                        pe.wait_ge(y_taken, j + 1)
                    pe.wait_ge(h_ready, j * (F // P) + (F // P) + c + 1)
                    mm = pe.matmul(ps_o[:, 0:E], hidden[:, c, :], w2_sb[e][:, c, :],
                                   start=(c == 0), stop=(c == F // P - 1))
                mm.then_inc(y_full, 1)

            expert_tiles(pe, expert, runs)


def lay_out(i):
    c = np.zeros((TK + 1, P, NB, KE, P), np.float32)
    c[:TK] = i["ctx_1024"].reshape(NB, TK, P, KE, P).transpose(1, 4, 0, 3, 2)
    m = i["mask_1x1xSxS2_ik0"].reshape(SQ, TK, P)
    mk = np.zeros((TK + 1, P, 2 * SQ), m.dtype)
    mk[:TK, :, :SQ] = m.transpose(1, 2, 0)
    mk[:TK, :, SQ:] = m.reshape(2, P, TK, P).transpose(2, 1, 0, 3).reshape(TK, P, 2 * P)
    t = lambda w: w.T.reshape(KE, P, E).transpose(1, 0, 2)
    at = np.arange(P)
    by_value = (at % HU) * D + at // HU
    by_fours = (at // 64 * 4 + at % 4) * D + at % 64 // 4
    halves = lambda order: np.concatenate([order, order + P])
    w = np.stack([t(i["L0_xattn_Wq"])[:, :, halves(by_value)], t(i["L0_xattn_Wk"])[:, :, halves(by_fours)],
                  t(i["L0_xattn_Wv"])], 1)
    w_qkv = i["L0_attn_Wqkv"].reshape(E, 3, E).copy()
    w_qkv[:, :2] = w_qkv[:, :2][:, :, halves(by_value)]

    def pad(wt):
        r = np.zeros((4, 32, 4, E), np.float32)
        r[:, :D] = wt.reshape(4, 4, D, E).transpose(1, 2, 0, 3)
        return r.reshape(P, 4, E)

    b = np.zeros((P, 8), np.float32)
    b[:, 0:2] = i["L0_xattn_bq"].reshape(2, P).T[by_value]
    b[:, 2:4] = i["L0_xattn_bk"].reshape(2, P).T[by_fours]
    bv = np.zeros((4, 32, 4), np.float32)
    bv[:, :D] = i["L0_xattn_bv"].reshape(4, 4, D).transpose(1, 2, 0)
    b[:, 4:8] = bv.reshape(P, 4)
    cst = np.zeros((P, 4 * P), np.float32)
    cst[:, :P] = np.eye(P)
    cst[:, P:P + TK] = np.arange(TK)
    cst[:, P + 96] = np.arange(P)
    cst[:, P + 64:P + 64 + NE] = NE - np.arange(NE)
    cst[:, P + 80:P + 80 + NT - 1] = P * np.arange(1, NT)
    cst[:, 2 * P - 1] = 1
    cst[:, 2 * P:3 * P] = np.triu(np.ones((P, P)), 1)
    inv = (1.0 / np.float32(10000.0) ** (np.arange(0, D, 2, dtype=np.float32) / np.float32(D))).astype(np.float32)
    freq = np.repeat(np.outer(np.arange(SQ, dtype=np.float32), inv), 2, axis=1)
    sign = np.tile(np.array([-1, 1], np.float32), D // 2)
    cos, sin = np.cos(freq).T, (np.sin(freq) * sign).T
    rope = np.stack([cos * np.float32(D ** -0.5), sin * np.float32(D ** -0.5), cos, sin]).astype(np.float32)
    rope = np.tile(rope, (1, HU, 1)).transpose(1, 0, 2)[by_value]
    at = np.arange(SQ)
    hidden = np.where(at[None, :] > at[:, None], -BIG, 0).astype(np.float32)
    causal = np.stack([hidden.reshape(2, P, SQ), hidden.T.reshape(2, P, SQ)]).transpose(2, 0, 1, 3)
    edges = np.ones((2, 4, 2 * HU * CH * P), np.float32)
    edges[0, 0] = 0
    return {
        "x_l": i["x"].reshape(NT, P, E).transpose(1, 0, 2), "ctx_l": c.reshape(TK + 1, P, NB * KE * P), "mask_l": mk,
        "mask_first": mk[:TK, :, :SQ].transpose(1, 0, 2), "w_l": w,
        "w_qkv_l": w_qkv.reshape(KE, P, 3 * E).transpose(1, 0, 2),
        "wo_pad": np.stack([pad(i["L0_xattn_Wo"].T), pad(i["L0_attn_Wout"])], 1), "biases": b,
        "rows_in": np.concatenate([i["L0_xattn_bo"], i["L0_attn_bout"], i["L0_ffn_gate_b"],
                                   i["L0_ffn_expert_bias"]])[None],
        "consts": cst, "causal_in": causal.astype(mybir.dt.np(BF16)), "rope_in": rope,
        "gate_l": i["L0_ffn_gate_w"].T.reshape(KE, P, NE).transpose(1, 0, 2),
        "edges_in": edges.astype(mybir.dt.np(BF16)),
        "w1": i["L0_ffn_w1"], "b1_l": i["L0_ffn_b1"].reshape(NE, F // P, P).transpose(2, 0, 1),
        "w2": i["L0_ffn_w2"], "b2": i["L0_ffn_b2"],
    }


def kernel(**inputs):
    import concourse.bacc as bacc
    from concourse.bass_utils import run_bass_kernel_spmd

    nc = bacc.Bacc("TRN2", target_bir_lowering=False, num_devices=1)
    arrays = {k: np.ascontiguousarray(v) for k, v in lay_out({k: np.asarray(v) for k, v in inputs.items()}).items()}
    args = [nc.dram_tensor(k, v.shape, mybir.dt.from_np(v.dtype), kind="ExternalInput").ap()
            for k, v in arrays.items()]
    out = nc.dram_tensor("out", [NB, SQ, E], F32, kind="ExternalOutput").ap()
    build(nc, *args, out)
    return run_bass_kernel_spmd(nc, [arrays], core_ids=[0]).results[0]["out"]
```
